# Optimizing a Trainium2 kernel written in Bass

```python
import numpy as np
import jax
import jax.numpy as jnp

def _softmax(x, axis=-1):
    return jax.nn.softmax(x, axis=axis)

def _gelu(x):
    return jax.nn.gelu(x, approximate=True)

def _silu(x):
    return jax.nn.silu(x)

def _sigmoid(x):
    return jax.nn.sigmoid(x)

def _layernorm(x, axis=-1, eps=1e-05):
    m = jnp.mean(x, axis=axis, keepdims=True)
    v = jnp.var(x, axis=axis, keepdims=True)
    return (x - m) / jnp.sqrt(v + eps)

def _scatter_add(tgt, idx, src, axis=0):
    return tgt.at[idx].add(src)

def _segment_sum(src, seg, n):
    return jax.ops.segment_sum(src, seg, n)
kernel_name = 'mk_recurrent_d2_jaxref_r8_4ec2f4'

def setup_inputs(seed: int=0):
    np.random.seed(seed)
    _w = jnp.asarray

    def _L0_attn_setup():
        import jax, jax.numpy as jnp
        import numpy as np
        B, T, E, H = (2, 256, 128, 16)
        D = E // H
        key = jax.random.key(seed)
        k = jax.random.split(key, 6)
        return {'x': jax.random.normal(k[0], (B, T, E), dtype=jnp.float32), 'w_att_val': jax.random.normal(k[1], (H, D, D), dtype=jnp.float32) * (6.0 / D) ** 0.5, 'wv_w': jax.random.normal(k[2], (E, E), dtype=jnp.float32) * E ** (-0.5), 'wv_b': jnp.zeros((E,), dtype=jnp.float32), 'out_w': jax.random.normal(k[3], (E, E), dtype=jnp.float32) * E ** (-0.5), 'out_b': jnp.zeros((E,), dtype=jnp.float32)}
    _L0_attn_in = _L0_attn_setup()

    def _L0_ffn_setup():
        import jax, jax.numpy as jnp
        import numpy as np
        D = 128
        H = 512
        E = 8
        B, N = (2, 256)
        key = jax.random.key(seed)
        ks = jax.random.split(key, 5)
        x = jax.random.normal(ks[0], (B, N, D), dtype=jnp.float32)
        W1 = jax.random.normal(ks[1], (E, D, H), dtype=jnp.float32) / np.sqrt(D)
        W2 = jax.random.normal(ks[2], (E, H, D), dtype=jnp.float32) / np.sqrt(H)
        Wg = jax.random.normal(ks[3], (D, E), dtype=jnp.float32) / np.sqrt(D)
        bg = jax.random.normal(ks[4], (E,), dtype=jnp.float32) * 0.01
        return {'x': x, 'W1': W1, 'W2': W2, 'Wg': Wg, 'bg': bg}
    _L0_ffn_in = _L0_ffn_setup()

    def _L1_attn_setup():
        import jax, jax.numpy as jnp
        import numpy as np
        D_MODEL = 128
        N_HEADS = 16
        LATENT_HEADS = 8
        LATENT_DIM = 64
        N_LATENTS = 64
        WINDOW = 32
        HEAD_DIM = D_MODEL // N_HEADS
        LAT_HD = LATENT_DIM // LATENT_HEADS
        B, S = (2, 512)

        def _pool_to_latents(x):
            Bx, Sx, C = x.shape
            chunk = max(1, Sx // N_LATENTS)
            return x.reshape(Bx, N_LATENTS, chunk, C).mean(axis=2)

        def _local_window_attn(Q, K, V):
            Bx, H, Sx, D = Q.shape
            W = WINDOW
            nb = Sx // W
            Qb = Q.reshape(Bx, H, nb, W, D)
            Kp = jnp.pad(K, ((0, 0), (0, 0), (W, 0), (0, 0))).reshape(Bx, H, nb + 1, W, D)
            Vp = jnp.pad(V, ((0, 0), (0, 0), (W, 0), (0, 0))).reshape(Bx, H, nb + 1, W, D)
            Kw = jnp.concatenate([Kp[:, :, :-1], Kp[:, :, 1:]], axis=3)
            Vw = jnp.concatenate([Vp[:, :, :-1], Vp[:, :, 1:]], axis=3)
            i = jnp.arange(W)[:, None]
            j = jnp.arange(2 * W)[None, :]
            base = (j > i) & (j <= i + W)
            blk0 = (jnp.arange(nb) > 0)[:, None, None] | (j >= W)[None, :, :]
            mask = base[None, :, :] & blk0
            sc = jnp.einsum('bhnid,bhnjd->bhnij', Qb, Kw) / np.sqrt(D).astype(np.float32)
            sc = jnp.where(mask[None, None], sc, -jnp.inf)
            p = jax.nn.softmax(sc, axis=-1)
            out = jnp.einsum('bhnij,bhnjd->bhnid', p, Vw)
            return out.reshape(Bx, H, Sx, D)
        key = jax.random.key(seed)
        ks = jax.random.split(key, 11)
        std = 0.02
        w = lambda k, shp: jax.random.normal(k, shp, jnp.float32) * std
        return {'x': jax.random.normal(ks[0], (B, S, D_MODEL), jnp.float32), 'wq': w(ks[1], (D_MODEL, D_MODEL)), 'wk': w(ks[2], (D_MODEL, D_MODEL)), 'wv': w(ks[3], (D_MODEL, D_MODEL)), 'wgq': w(ks[4], (D_MODEL, LATENT_DIM)), 'wgk': w(ks[5], (D_MODEL, LATENT_DIM)), 'wgv': w(ks[6], (D_MODEL, LATENT_DIM)), 'r_out_w': w(ks[7], (LATENT_DIM, D_MODEL)), 'gate_local_w': w(ks[8], (N_HEADS, HEAD_DIM)), 'gate_remote_w': w(ks[9], (N_HEADS, HEAD_DIM)), 'w_out': w(ks[10], (D_MODEL, D_MODEL))}
    _L1_attn_in = _L1_attn_setup()

    def _L1_ffn_setup():
        import jax, jax.numpy as jnp
        import numpy as np
        DIM = 128
        DEPTH = 2
        HEADS = 8
        DIM_HEAD = 64
        WINDOW = 64
        INNER = HEADS * DIM_HEAD
        HID = int(DIM * 4 * 2 / 3)
        B, N = (2, 1024)
        QK_SCALE = 8.0

        def shift_token(t):
            t1, t2 = jnp.split(t, 2, axis=-1)
            t2 = jnp.pad(t2, ((0, 0), (1, 0), (0, 0)))[:, :-1]
            return jnp.concatenate([t1, t2], axis=-1)

        def l2norm(t):
            return t / jnp.clip(jnp.linalg.norm(t, axis=-1, keepdims=True), 1e-12)

        def rotate_half(x):
            x1, x2 = jnp.split(x, 2, axis=-1)
            return jnp.concatenate([-x2, x1], axis=-1)

        def rotary_xpos(q, k):
            n = q.shape[-2]
            half_idx = jnp.arange(0, DIM_HEAD, 2, dtype=jnp.float32)
            inv_freq = 1.0 / 10000.0 ** (half_idx / DIM_HEAD)
            t = jnp.arange(n, dtype=jnp.float32)
            freqs = t[:, None] * inv_freq[None, :]
            freqs = jnp.concatenate([freqs, freqs], axis=-1)
            base = (half_idx + 0.4 * DIM_HEAD) / (1.4 * DIM_HEAD)
            power = (t - n // 2) / float(WINDOW // 2)
            scale = base[None, :] ** power[:, None]
            scale = jnp.concatenate([scale, scale], axis=-1)
            cos, sin = (jnp.cos(freqs), jnp.sin(freqs))
            q = q * cos * scale + rotate_half(q) * sin * scale
            k = k * cos / scale + rotate_half(k) * sin / scale
            return (q, k)

        def local_attention(q, k, v):
            b, h, n, d = q.shape
            w = n // WINDOW
            bq = q.reshape(b, h, w, WINDOW, d) * QK_SCALE
            bk = k.reshape(b, h, w, WINDOW, d)
            bv = v.reshape(b, h, w, WINDOW, d)

            def look_around(t):
                p = jnp.pad(t, ((0, 0), (0, 0), (1, 0), (0, 0), (0, 0)))
                return jnp.concatenate([p[:, :, :w], p[:, :, 1:]], axis=3)
            bk, bv = (look_around(bk), look_around(bv))
            bt = jnp.arange(n).reshape(w, WINDOW)
            btp = jnp.pad(bt, ((1, 0), (0, 0)), constant_values=-1)
            btk = jnp.concatenate([btp[:w], btp[1:]], axis=1)
            sim = jnp.einsum('bhwid,bhwjd->bhwij', bq, bk)
            i = bt[:, :, None]
            j = btk[:, None, :]
            mask = (i < j) | (i > j + WINDOW) | (j == -1)
            sim = jnp.where(mask, -jnp.finfo(sim.dtype).max, sim)
            attn = jax.nn.softmax(sim, axis=-1)
            out = jnp.einsum('bhwij,bhwjd->bhwid', attn, bv)
            return out.reshape(b, h, n, d)

        def _layer(x, wqkv, qs, ksc, wo, lg, lb, w1, b1, w2, b2):
            b, n, _ = x.shape
            h = shift_token(x)
            qkv = h @ wqkv
            q, k, v = jnp.split(qkv, 3, axis=-1)
            to_heads = lambda t: t.reshape(b, n, HEADS, DIM_HEAD).transpose(0, 2, 1, 3)
            q, k, v = (to_heads(q), to_heads(k), to_heads(v))
            q = l2norm(q) * qs
            k = l2norm(k) * ksc
            q, k = rotary_xpos(q, k)
            o = local_attention(q, k, v)
            o = o.transpose(0, 2, 1, 3).reshape(b, n, INNER)
            x = x + o @ wo
            h = shift_token(x)
            mu = h.mean(-1, keepdims=True)
            var = h.var(-1, keepdims=True)
            h = (h - mu) / jnp.sqrt(var + 1e-05) * lg + lb
            h = h @ w1 + b1
            a, g = jnp.split(h, 2, axis=-1)
            h = a * jax.nn.gelu(g, approximate=False)
            x = x + h @ w2 + b2
            return x
        key = jax.random.key(seed)
        ks = jax.random.split(key, 6)
        return {'x': jax.random.normal(ks[0], (B, N, DIM), jnp.float32), 'wqkv': jax.random.normal(ks[1], (DEPTH, DIM, 3 * INNER), jnp.float32) * 0.02, 'q_scale': jnp.ones((DEPTH, DIM_HEAD), jnp.float32), 'k_scale': jnp.ones((DEPTH, DIM_HEAD), jnp.float32), 'wo': jax.random.normal(ks[2], (DEPTH, INNER, DIM), jnp.float32) * 0.02, 'ln_g': jnp.ones((DEPTH, DIM), jnp.float32), 'ln_b': jnp.zeros((DEPTH, DIM), jnp.float32), 'w1': jax.random.normal(ks[3], (DEPTH, DIM, 2 * HID), jnp.float32) * 0.02, 'b1': jnp.zeros((DEPTH, 2 * HID), jnp.float32), 'w2': jax.random.normal(ks[4], (DEPTH, HID, DIM), jnp.float32) * 0.02, 'b2': jnp.zeros((DEPTH, DIM), jnp.float32)}
    _L1_ffn_in = _L1_ffn_setup()
    _d = {'L0_attn_x': _L0_attn_in['x'], 'L0_attn_w_att_val': _L0_attn_in['w_att_val'], 'L0_attn_wv_w': _L0_attn_in['wv_w'], 'L0_attn_wv_b': _L0_attn_in['wv_b'], 'L0_attn_out_w': _L0_attn_in['out_w'], 'L0_attn_out_b': _L0_attn_in['out_b'], 'L0_ffn_W1': _L0_ffn_in['W1'], 'L0_ffn_W2': _L0_ffn_in['W2'], 'L0_ffn_Wg': _L0_ffn_in['Wg'], 'L0_ffn_bg': _L0_ffn_in['bg'], 'L1_attn_wq': _L1_attn_in['wq'], 'L1_attn_wk': _L1_attn_in['wk'], 'L1_attn_wv': _L1_attn_in['wv'], 'L1_attn_wgq': _L1_attn_in['wgq'], 'L1_attn_wgk': _L1_attn_in['wgk'], 'L1_attn_wgv': _L1_attn_in['wgv'], 'L1_attn_r_out_w': _L1_attn_in['r_out_w'], 'L1_attn_gate_local_w': _L1_attn_in['gate_local_w'], 'L1_attn_gate_remote_w': _L1_attn_in['gate_remote_w'], 'L1_attn_w_out': _L1_attn_in['w_out'], 'L1_ffn_wqkv': _L1_ffn_in['wqkv'], 'L1_ffn_q_scale': _L1_ffn_in['q_scale'], 'L1_ffn_k_scale': _L1_ffn_in['k_scale'], 'L1_ffn_wo': _L1_ffn_in['wo'], 'L1_ffn_ln_g': _L1_ffn_in['ln_g'], 'L1_ffn_ln_b': _L1_ffn_in['ln_b'], 'L1_ffn_w1': _L1_ffn_in['w1'], 'L1_ffn_b1': _L1_ffn_in['b1'], 'L1_ffn_w2': _L1_ffn_in['w2'], 'L1_ffn_b2': _L1_ffn_in['b2']}
    _x0 = _d['L0_attn_x']
    _d['L0_attn_x'] = jax.random.normal(jax.random.fold_in(jax.random.key(seed), 1), (16, 512, 128), dtype=_x0.dtype)
    del _x0
    return _d

def reference(L0_attn_x, L0_attn_w_att_val, L0_attn_wv_w, L0_attn_wv_b, L0_attn_out_w, L0_attn_out_b, L0_ffn_W1, L0_ffn_W2, L0_ffn_Wg, L0_ffn_bg, L1_attn_wq, L1_attn_wk, L1_attn_wv, L1_attn_wgq, L1_attn_wgk, L1_attn_wgv, L1_attn_r_out_w, L1_attn_gate_local_w, L1_attn_gate_remote_w, L1_attn_w_out, L1_ffn_wqkv, L1_ffn_q_scale, L1_ffn_k_scale, L1_ffn_wo, L1_ffn_ln_g, L1_ffn_ln_b, L1_ffn_w1, L1_ffn_b1, L1_ffn_w2, L1_ffn_b2):

    def _L0_attn_ref(x, w_att_val, wv_w, wv_b, out_w, out_b):
        import jax, jax.numpy as jnp
        import numpy as np
        B, T, E, H = (2, 256, 128, 16)
        D = E // H
        b, t, e = x.shape
        h, d, _ = w_att_val.shape
        x_h = x.reshape(b, t, h, d).transpose(0, 2, 1, 3)
        xw = jnp.einsum('bhtd,hde->bhte', x_h, w_att_val)
        att = jnp.einsum('bhte,bhse->bhts', xw, x_h) / jnp.sqrt(jnp.asarray(d, x.dtype))
        att = jax.nn.softmax(att, axis=-1)
        vx = x @ wv_w.T + wv_b
        vx = vx.reshape(b, t, h, d).transpose(0, 2, 1, 3)
        o = jnp.einsum('bhts,bhsd->bhtd', att, vx)
        o = o.transpose(0, 2, 1, 3).reshape(b, t, e)
        return o @ out_w.T + out_b

    def _L0_ffn_ref(x, W1, W2, Wg, bg):
        import jax, jax.numpy as jnp
        import numpy as np
        D = 128
        H = 512
        E = 8
        B, N = (2, 256)
        b, n, d = x.shape
        e = Wg.shape[1]
        xf = x.reshape(b * n, d)
        logits = xf @ Wg + bg
        one_hot = jax.nn.one_hot(jnp.argmax(logits, axis=-1), e, dtype=x.dtype)
        h = jax.nn.gelu(jnp.einsum('td,edh->eth', xf, W1), approximate=True)
        y = jnp.einsum('eth,ehd->etd', h, W2)
        out = jnp.einsum('etd,te->td', y, one_hot)
        return out.reshape(b, n, d)

    def _L1_attn_ref(x, wq, wk, wv, wgq, wgk, wgv, r_out_w, gate_local_w, gate_remote_w, w_out):
        import jax, jax.numpy as jnp
        import numpy as np
        D_MODEL = 128
        N_HEADS = 16
        LATENT_HEADS = 8
        LATENT_DIM = 64
        N_LATENTS = 64
        WINDOW = 32
        HEAD_DIM = D_MODEL // N_HEADS
        LAT_HD = LATENT_DIM // LATENT_HEADS
        B, S = (2, 512)

        def _pool_to_latents(x):
            Bx, Sx, C = x.shape
            chunk = max(1, Sx // N_LATENTS)
            return x.reshape(Bx, N_LATENTS, chunk, C).mean(axis=2)

        def _local_window_attn(Q, K, V):
            Bx, H, Sx, D = Q.shape
            W = WINDOW
            nb = Sx // W
            Qb = Q.reshape(Bx, H, nb, W, D)
            Kp = jnp.pad(K, ((0, 0), (0, 0), (W, 0), (0, 0))).reshape(Bx, H, nb + 1, W, D)
            Vp = jnp.pad(V, ((0, 0), (0, 0), (W, 0), (0, 0))).reshape(Bx, H, nb + 1, W, D)
            Kw = jnp.concatenate([Kp[:, :, :-1], Kp[:, :, 1:]], axis=3)
            Vw = jnp.concatenate([Vp[:, :, :-1], Vp[:, :, 1:]], axis=3)
            i = jnp.arange(W)[:, None]
            j = jnp.arange(2 * W)[None, :]
            base = (j > i) & (j <= i + W)
            blk0 = (jnp.arange(nb) > 0)[:, None, None] | (j >= W)[None, :, :]
            mask = base[None, :, :] & blk0
            sc = jnp.einsum('bhnid,bhnjd->bhnij', Qb, Kw) / np.sqrt(D).astype(np.float32)
            sc = jnp.where(mask[None, None], sc, -jnp.inf)
            p = jax.nn.softmax(sc, axis=-1)
            out = jnp.einsum('bhnij,bhnjd->bhnid', p, Vw)
            return out.reshape(Bx, H, Sx, D)
        Bx, Sx, _ = x.shape
        chunk = max(1, Sx // N_LATENTS)
        Q = (x @ wq).reshape(Bx, Sx, N_HEADS, HEAD_DIM).transpose(0, 2, 1, 3)
        K = (x @ wk).reshape(Bx, Sx, N_HEADS, HEAD_DIM).transpose(0, 2, 1, 3)
        V = (x @ wv).reshape(Bx, Sx, N_HEADS, HEAD_DIM).transpose(0, 2, 1, 3)
        local = _local_window_attn(Q, K, V)
        GQ = (x @ wgq).reshape(Bx, Sx, LATENT_HEADS, LAT_HD).transpose(0, 2, 1, 3)
        GK = _pool_to_latents(x @ wgk).reshape(Bx, N_LATENTS, LATENT_HEADS, LAT_HD).transpose(0, 2, 1, 3)
        GV = _pool_to_latents(x @ wgv).reshape(Bx, N_LATENTS, LATENT_HEADS, LAT_HD).transpose(0, 2, 1, 3)
        lsc = jnp.einsum('bhsd,bhnd->bhsn', GQ, GK) / np.sqrt(LAT_HD).astype(np.float32)
        lmask = jnp.arange(N_LATENTS)[None, :] <= (jnp.arange(Sx) // chunk)[:, None]
        lsc = jnp.where(lmask[None, None], lsc, -jnp.inf)
        lp = jax.nn.softmax(lsc, axis=-1)
        rem = jnp.einsum('bhsn,bhnd->bhsd', lp, GV)
        rem = rem.transpose(0, 2, 1, 3).reshape(Bx, Sx, LATENT_DIM) @ r_out_w
        rem = rem.reshape(Bx, Sx, N_HEADS, HEAD_DIM).transpose(0, 2, 1, 3)
        gl = jax.nn.sigmoid(jnp.einsum('bhsd,hd->bhs', Q, gate_local_w))[..., None]
        gr = jax.nn.sigmoid(jnp.einsum('bhsd,hd->bhs', Q, gate_remote_w))[..., None]
        out = gl * local + gr * rem
        out = out.transpose(0, 2, 1, 3).reshape(Bx, Sx, D_MODEL)
        return out @ w_out

    def _L1_ffn_ref(x, wqkv, q_scale, k_scale, wo, ln_g, ln_b, w1, b1, w2, b2):
        import jax, jax.numpy as jnp
        import numpy as np
        DIM = 128
        DEPTH = 2
        HEADS = 8
        DIM_HEAD = 64
        WINDOW = 64
        INNER = HEADS * DIM_HEAD
        HID = int(DIM * 4 * 2 / 3)
        B, N = (2, 1024)
        QK_SCALE = 8.0

        def shift_token(t):
            t1, t2 = jnp.split(t, 2, axis=-1)
            t2 = jnp.pad(t2, ((0, 0), (1, 0), (0, 0)))[:, :-1]
            return jnp.concatenate([t1, t2], axis=-1)

        def l2norm(t):
            return t / jnp.clip(jnp.linalg.norm(t, axis=-1, keepdims=True), 1e-12)

        def rotate_half(x):
            x1, x2 = jnp.split(x, 2, axis=-1)
            return jnp.concatenate([-x2, x1], axis=-1)

        def rotary_xpos(q, k):
            n = q.shape[-2]
            half_idx = jnp.arange(0, DIM_HEAD, 2, dtype=jnp.float32)
            inv_freq = 1.0 / 10000.0 ** (half_idx / DIM_HEAD)
            t = jnp.arange(n, dtype=jnp.float32)
            freqs = t[:, None] * inv_freq[None, :]
            freqs = jnp.concatenate([freqs, freqs], axis=-1)
            base = (half_idx + 0.4 * DIM_HEAD) / (1.4 * DIM_HEAD)
            power = (t - n // 2) / float(WINDOW // 2)
            scale = base[None, :] ** power[:, None]
            scale = jnp.concatenate([scale, scale], axis=-1)
            cos, sin = (jnp.cos(freqs), jnp.sin(freqs))
            q = q * cos * scale + rotate_half(q) * sin * scale
            k = k * cos / scale + rotate_half(k) * sin / scale
            return (q, k)

        def local_attention(q, k, v):
            b, h, n, d = q.shape
            w = n // WINDOW
            bq = q.reshape(b, h, w, WINDOW, d) * QK_SCALE
            bk = k.reshape(b, h, w, WINDOW, d)
            bv = v.reshape(b, h, w, WINDOW, d)

            def look_around(t):
                p = jnp.pad(t, ((0, 0), (0, 0), (1, 0), (0, 0), (0, 0)))
                return jnp.concatenate([p[:, :, :w], p[:, :, 1:]], axis=3)
            bk, bv = (look_around(bk), look_around(bv))
            bt = jnp.arange(n).reshape(w, WINDOW)
            btp = jnp.pad(bt, ((1, 0), (0, 0)), constant_values=-1)
            btk = jnp.concatenate([btp[:w], btp[1:]], axis=1)
            sim = jnp.einsum('bhwid,bhwjd->bhwij', bq, bk)
            i = bt[:, :, None]
            j = btk[:, None, :]
            mask = (i < j) | (i > j + WINDOW) | (j == -1)
            sim = jnp.where(mask, -jnp.finfo(sim.dtype).max, sim)
            attn = jax.nn.softmax(sim, axis=-1)
            out = jnp.einsum('bhwij,bhwjd->bhwid', attn, bv)
            return out.reshape(b, h, n, d)

        def _layer(x, wqkv, qs, ksc, wo, lg, lb, w1, b1, w2, b2):
            b, n, _ = x.shape
            h = shift_token(x)
            qkv = h @ wqkv
            q, k, v = jnp.split(qkv, 3, axis=-1)
            to_heads = lambda t: t.reshape(b, n, HEADS, DIM_HEAD).transpose(0, 2, 1, 3)
            q, k, v = (to_heads(q), to_heads(k), to_heads(v))
            q = l2norm(q) * qs
            k = l2norm(k) * ksc
            q, k = rotary_xpos(q, k)
            o = local_attention(q, k, v)
            o = o.transpose(0, 2, 1, 3).reshape(b, n, INNER)
            x = x + o @ wo
            h = shift_token(x)
            mu = h.mean(-1, keepdims=True)
            var = h.var(-1, keepdims=True)
            h = (h - mu) / jnp.sqrt(var + 1e-05) * lg + lb
            h = h @ w1 + b1
            a, g = jnp.split(h, 2, axis=-1)
            h = a * jax.nn.gelu(g, approximate=False)
            x = x + h @ w2 + b2
            return x
        for l in range(DEPTH):
            x = _layer(x, wqkv[l], q_scale[l], k_scale[l], wo[l], ln_g[l], ln_b[l], w1[l], b1[l], w2[l], b2[l])
        return x
    x = L0_attn_x
    xn = _layernorm(x, axis=-1)
    s = _L0_attn_ref(xn, L0_attn_w_att_val, L0_attn_wv_w, L0_attn_wv_b, L0_attn_out_w, L0_attn_out_b)
    g = _silu(_L0_ffn_ref(xn, L0_ffn_W1, L0_ffn_W2, L0_ffn_Wg, L0_ffn_bg))
    x = x + s * g
    xn = _layernorm(x, axis=-1)
    s = _L1_attn_ref(xn, L1_attn_wq, L1_attn_wk, L1_attn_wv, L1_attn_wgq, L1_attn_wgk, L1_attn_wgv, L1_attn_r_out_w, L1_attn_gate_local_w, L1_attn_gate_remote_w, L1_attn_w_out)
    g = _silu(_L1_ffn_ref(xn, L1_ffn_wqkv, L1_ffn_q_scale, L1_ffn_k_scale, L1_ffn_wo, L1_ffn_ln_g, L1_ffn_ln_b, L1_ffn_w1, L1_ffn_b1, L1_ffn_w2, L1_ffn_b2))
    x = x + s * g
    return x

_drawn_inputs = setup_inputs


def setup_inputs(seed=0):
    import zlib

    import numpy as np

    out = dict(_drawn_inputs(seed))
    spreads = {'L0_attn_wv_b': (0.0, 0.1),
     'L0_attn_out_b': (0.0, 0.1),
     'L1_ffn_q_scale': (1.0, 0.6),
     'L1_ffn_k_scale': (1.0, 0.6),
     'L1_ffn_ln_g': (1.0, 0.6),
     'L1_ffn_ln_b': (0.0, 0.8),
     'L1_ffn_b1': (0.0, 0.8),
     'L1_ffn_b2': (0.0, 0.8)}
    factors = {'L0_ffn_bg': 3.387,
     'L1_attn_wq': 8.0,
     'L1_attn_wk': 8.0,
     'L1_attn_wv': 8.0,
     'L1_attn_wgq': 8.0,
     'L1_attn_wgk': 8.0,
     'L1_attn_wgv': 8.0,
     'L1_attn_r_out_w': 8.0,
     'L1_attn_gate_local_w': 8.0,
     'L1_attn_gate_remote_w': 8.0,
     'L1_attn_w_out': 8.0,
     'L1_ffn_wqkv': 8.0,
     'L1_ffn_wo': 8.0,
     'L1_ffn_w1': 8.0,
     'L1_ffn_w2': 8.0}
    for name, (base, spread) in spreads.items():
        noise = np.random.default_rng([zlib.crc32(name.encode()), seed]).standard_normal(out[name].shape)
        drawn = base * np.exp(spread * noise) if base else spread * noise
        out[name] = jnp.asarray(drawn.astype(out[name].dtype))
    for name, factor in factors.items():
        out[name] = (out[name] * factor).astype(out[name].dtype)
    return out
```

```python
from contextlib import ExitStack

import numpy as np

import concourse.bass as bass
from concourse import mybir

ALU = mybir.AluOpType
ACT = mybir.ActivationFunctionType
AX = mybir.AxisListType
F32 = mybir.dt.float32
BF16 = mybir.dt.bfloat16
I32 = mybir.dt.int32

P = 128
B, T, E = 16, 512, 128
NT = T // P
H0, D0 = 16, 8
NX, HX = 8, 512
XC = HX // P
WIN = 32
LH, NL = 8, 64
POOL = T // NL
FH, FD, FW = 8, 64, 64
INNER = FH * FD
HID = int(E * 4 * 2 / 3)
HC = [(c, min(P, HID - c)) for c in range(0, HID, P)]
DEPTH = 2
SPLIT = 3
STACK = SPLIT * SPLIT * D0
ROWS = STACK + 2
G = H0 // 4
LKEYS = P + WIN
FKEYS = P + FW
EPS = 1e-5
MASKED = -1e30
HEAD_SCALE = float(D0) ** -0.5
QK_SCALE = 8.0
RSQRT_MAGIC = float(0x5F3759DF)


def shape_constants():
    bf = mybir.dt.np(BF16)
    c = {"ident": np.eye(P, dtype=np.float32), "ident_bf": np.eye(P, dtype=np.float32).astype(bf)}
    c["ones_bf"] = np.ones((2, 8 * T), np.float32).astype(bf)
    q, k = np.arange(P)[:, None], np.arange(LKEYS)[None, :] - WIN
    c["win_q"] = np.where((k > q - WIN) & (k <= q), 0.0, MASKED)
    k, q = np.arange(P)[:, None], np.arange(LKEYS)[None, :]
    c["win_k"] = np.where((k > q - WIN) & (k <= q), 0.0, MASKED)
    q, k = np.arange(P)[:, None], np.arange(FKEYS)[None, :] - FW
    c["band_q"] = np.where((k >= q - FW) & (k <= q), 0.0, MASKED)
    k, q = np.arange(P)[:, None], np.arange(FKEYS)[None, :]
    c["band_k"] = np.where((k >= q - FW) & (k <= q), 0.0, MASKED)
    t = np.arange(T).reshape(NT, P).T[:, :, None]
    lat = np.arange(NL)
    c["lat_q"] = np.where(lat[None, None, :] <= t // POOL, 0.0, MASKED).reshape(P, NT * NL)
    c["lat_k"] = np.where((np.arange(P) % NL)[:, None] <= np.arange(T)[None, :] // POOL, 0.0, MASKED)
    for n in ("win_q", "win_k", "band_q", "band_k"):
        c[n] = np.concatenate([c[n], c[n]], axis=1)
    for n in ("win_q", "win_k", "band_q", "band_k", "lat_q", "lat_k"):
        c[n] = c[n].astype(np.float32).astype(bf)
    c["blocks"] = np.kron(np.eye(H0), np.ones((D0, 1))).astype(np.float32)
    sel = np.zeros((P, FH, P), np.float32)
    for h in range(FH):
        sel[[h, FH + h], h, :] = 1.0
    c["pick"] = sel.reshape(P, FH * P).astype(bf)
    half = np.arange(0, FD, 2, dtype=np.float32)
    freq = np.arange(T, dtype=np.float32)[:, None] * (1.0 / 10000.0 ** (half / FD)).astype(np.float32)
    freq = np.concatenate([freq, freq], axis=1)
    base = (half + 0.4 * FD) / (1.4 * FD)
    scale = base[None, :] ** ((np.arange(T) - T // 2) / float(FW // 2))[:, None]
    scale = np.concatenate([scale, scale], axis=1)
    sign = np.where(np.arange(FD) < FD // 2, -1.0, 1.0)
    rot = np.stack([np.cos(freq) * scale, np.sin(freq) * scale * sign,
                    np.cos(freq) / scale, np.sin(freq) / scale * sign])
    c["rotary"] = rot.reshape(4, NT, P, FD).transpose(2, 0, 1, 3).reshape(P, 4 * T // P * FD).astype(np.float32)
    return {n: np.ascontiguousarray(a) for n, a in c.items()}


class Banks:

    def __init__(self, tiles, filled, emptied, plan):
        self.tiles, self.filled, self.emptied = tiles, filled, emptied
        self.number, self.outs = {}, {}
        count = dict.fromkeys(emptied, 0)
        self.plan = [product for product, _ in plan]
        for n, (product, engines) in enumerate(plan):
            assert product not in self.number, product
            self.number[product] = n
            for e in engines:
                count[e] += 1
            self.outs[product] = {e: (emptied[e], count[e]) for e in engines}

    def bank(self, product):
        return self.tiles[self.number[product] % len(self.tiles)]

    def made(self, product):
        return self.filled, self.number[product] + 1

    def brought(self, product, engine):
        return self.outs[product][engine]

    def take(self, pe, product):
        n = self.number[product] - len(self.tiles)
        for semaphore, value in self.outs[self.plan[n]].values() if n >= 0 else ():
            pe.wait_ge(semaphore, value)
        return self.bank(product)

    def full(self, eng, product):
        eng.wait_ge(*self.made(product))
        return self.bank(product)


def merge(*streams):
    heads = [next(s, None) for s in streams]
    while any(h is not None for h in heads):
        n = min((h, i) for i, h in enumerate(heads) if h is not None)[1]
        heads[n] = next(streams[n], None)


def mixer_kernel(nc, x_in, att_w, wv0T, wv0_b, wo0T, wo0_b, W1, W2, Wg, bg, wq, wk, wv, wgqk, wgv,
                 r_out, gate_l, gate_r, w_out, wqkv, q_sc, k_sc, wo, ln_g, ln_b, w1, b1, w2, b2,
                 consts, out):
    ctx = ExitStack()
    with ctx:
        def sb(name, shape, dt=F32):
            return ctx.enter_context(nc.sbuf_tensor(name, shape, dt))

        sems = []

        def sem(name):
            sems.append(ctx.enter_context(nc.semaphore(name)))
            return sems[-1]

        banks = [ctx.enter_context(nc.psum_tensor(f"bank{i}", [P, T], F32)) for i in range(8)]

        ident, ident_bf = sb("ident", [P, P]), sb("ident_bf", [P, P], BF16)
        win_q, win_k = sb("win_q", [P, 2 * LKEYS], BF16), sb("win_k", [P, 2 * LKEYS], BF16)
        band_q, band_k = sb("band_q", [P, 2 * FKEYS], BF16), sb("band_k", [P, 2 * FKEYS], BF16)
        lat_q, lat_k = sb("lat_q", [P, NT, NL], BF16), sb("lat_k", [P, T], BF16)
        blocks, pick = sb("blocks", [P, H0]), sb("pick", [P, FH, P], BF16)
        att_c, attW = sb("att_c", [P, D0]), sb("attW", [P, E])
        wv0_s, wo0_s = sb("wv0_s", [P, E]), sb("wo0_s", [P, E])
        bv0, bo0 = sb("bv0", [P, E]), sb("bo0", [P, E])
        Wg_s, bg_s = sb("Wg_s", [P, NX]), sb("bg_s", [P, NX])
        wq_s, wk_s, wv_s, w_out_s = (sb(n, [P, E]) for n in ("wq_s", "wk_s", "wv_s", "w_out_s"))
        wgqk_s, wgv_s, r_out_s = sb("wgqk_s", [P, E]), sb("wgv_s", [P, NL]), sb("r_out_s", [NL, E])
        gcol, gateW = sb("gcol", [P, 2]), sb("gateW", [P, 2, H0])
        wqkv_s, wo_s = sb("wqkv_s", [P, DEPTH, 3 * INNER]), sb("wo_s", [P, DEPTH, INNER // P, E])
        w1_s, w2_s = sb("w1_s", [P, DEPTH, 2 * HID]), sb("w2_s", [P, DEPTH, len(HC), E])
        b1_s, b2_s = sb("b1_s", [P, DEPTH, 2, len(HC)]), sb("b2_s", [P, DEPTH, E])
        lng_s, lnb_s = sb("lng_s", [P, DEPTH]), sb("lnb_s", [P, DEPTH])
        qks = sb("qks", [P, DEPTH, 2, FD])
        rotf = sb("rotf", [P, DEPTH, 4, NT, FD])

        x_a, x1_a, xn_a = sb("x_a", [P, NT, E]), sb("x1_a", [P, NT, E]), sb("xn_a", [P, NT, E])
        stats_a, mv_a, rs_a = sb("stats_a", [P, NT, 6]), sb("mv_a", [P, NT, 2]), sb("rs_a", [P, 4, NT])
        kq_a = sb("kq_a", [P, 2, T])
        RING = 2
        Kst_a, Qst_a = sb("Kst_a", [ROWS, RING, 4, T], BF16), sb("Qst_a", [ROWS, RING, 4, T], BF16)
        V_a = sb("V_a", [P, NT, H0, D0 + 1])
        nmax_a, mparts_a = sb("nmax_a", [P, G, NT, 4]), sb("mparts_a", [P, G, NT, 2, 4])
        mhi_a, mT_a = sb("mhi_a", [P, G, NT, 4], BF16), sb("mT_a", [8, 2, T], BF16)
        PR_A = 8
        prob_a = sb("prob_a", [P, PR_A, T])
        res_a = prob_a[:, 0:2, :]
        parts_a = prob_a[:, 2:5, :].rearrange("p a t -> p (a t)").bitcast(BF16).rearrange("p (w c t) -> p w c t", w=2, t=T)
        og_a, rden_a = sb("og_a", [P, T]), sb("rden_a", [P, NT, 4])
        otok_a, oT_a, s_a = xn_a, sb("oT_a", [P, T]), sb("s_a", [P, T])
        lg_a, hot_a, sc_a = sb("lg_a", [P, NT, NX]), sb("hot_a", [P, NT, NX]), sb("sc_a", [P, NT, NX])
        before_a, mx_a = sb("before_a", [P, NT, NX]), sb("mx_a", [P, NT])
        hid_a = prob_a[:, 0:XC, :]
        y_a, th_a = og_a, oT_a
        W1_s, W2_s = sb("W1_s", [P, 2, HX]), sb("W2_s", [P, 2, XC, E])

        x_b, xn_b, x_f = sb("x_b", [P, NT, E]), sb("xn_b", [P, NT, E]), sb("x_f", [P, NT, E])
        stats_b, mv_b, rs_b = sb("stats_b", [P, NT, 6]), sb("mv_b", [P, NT, 2]), sb("rs_b", [P, 4, NT])
        xnT_b, hT = sb("xnT_b", [P, T]), sb("hT", [P, T])
        pool_b, psum_l = sb("pool_b", [P, 2, NL]), sb("psum_l", [P, 2, NL])
        V_b, V_l = sb("V_b", [P, NT, H0, D0 + 1]), sb("V_l", [P, 4, 32])
        nmax_b, mparts_b = sb("nmax_b", [P, G, NT, 4]), sb("mparts_b", [P, G, NT, 2, 4])
        mhi_b, mT_b = sb("mhi_b", [P, G, NT, 4], BF16), sb("mT_b", [8, 2, T], BF16)
        nmax_l, mhi_l = sb("nmax_l", [P, NT, LH]), sb("mhi_l", [P, NT, LH], BF16)
        mparts_l, mT_l = sb("mparts_l", [P, NT, 2, LH]), sb("mT_l", [2 * LH, T], BF16)
        PR_B = 4
        prob_b = sb("prob_b", [P, PR_B, T])
        res_b = prob_b[:, 0:3, :]
        og_b, rden_b = sb("og_b", [P, T]), sb("rden_b", [P, 32])
        loc_b, rem_b = sb("loc_b", [P, NT, E]), sb("rem_b", [P, NT, NL])
        gate_b = sb("gate_b", [P, NT, 2, H0])
        mix_b, s_b = sb("mix_b", [P, T]), sb("s_b", [P, T])
        kT = sb("kT", [P, FH // 2, 2, T])
        V_f = sb("V_f", [P, NT, FH, FD + 1])
        ss, rn = sb("ss", [P, 2, FH]), sb("rn", [P, 3, 2 * FH])
        nmax_f, mhi_f = sb("nmax_f", [P, NT, FH]), sb("mhi_f", [P, NT, FH], BF16)
        mparts_f, mT_f = sb("mparts_f", [P, NT, 2, FH]), sb("mT_f", [P, T], BF16)
        rden_f = sb("rden_f", [P, 2])
        AREA = RING * 4 * T + LH * (T + NL) // 2 + 3 * T
        area, used = sb("area", [P, AREA]), [0]

        def take_area(words, rows=P):
            used[0] += words
            assert used[0] <= AREA, used
            return area[0:rows, used[0] - words:used[0]]

        Kst_b, Qst_b = (take_area(RING * 4 * T // 2, ROWS).bitcast(BF16).rearrange("p (r h t) -> p r h t", r=RING, t=T)
                        for _ in range(2))
        Qst_l = take_area(LH * T // 2, ROWS).bitcast(BF16).rearrange("p (h t) -> p h t", t=T)
        Kst_l = take_area(LH * NL // 2, ROWS).bitcast(BF16).rearrange("p (h t) -> p h t", t=NL)
        assert 3 * SPLIT * T // 2 <= used[0]
        parts_b = area[:, 0:3 * SPLIT * T // 2].bitcast(BF16).rearrange("p (w c t) -> p w c t", w=3, t=T)
        qkg_b = take_area(3 * T).rearrange("p (w t) -> p w t", t=T)
        used[0] = 0
        qk_raw, sq, cosp, qk_rot = (take_area(2 * INNER).rearrange("p (a n) -> p a n", a=2) for _ in range(4))
        qT = take_area(FH // 2 * T).rearrange("p (c t) -> p c t", t=T)
        used[0] = 0
        oT_f = take_area(INNER // P * T).rearrange("p (c t) -> p c t", t=T)
        gelu_f, u_f = take_area(T), take_area(len(HC) * T).rearrange("p (c t) -> p c t", t=T)
        otok_f = sb("otok_f", [P, 2, NT, P])

        def scratch(name, shape):
            return nc.dram_tensor(name, shape, BF16, kind="Internal").ap()

        dq_a, dk_a, dm_a = scratch("dq_a", [SPLIT, P, SPLIT, T]), scratch("dk_a", [P, SPLIT, T]), scratch("dm_a", [G, 8, T])
        dq_b, dk_b, dm_b = scratch("dq_b", [SPLIT, P, SPLIT, T]), scratch("dk_b", [P, SPLIT, T]), scratch("dm_b", [G, 8, T])
        dq_l, dk_l, dm_l = scratch("dq_l", [SPLIT, 64, SPLIT, T]), scratch("dk_l", [64, SPLIT, NL]), scratch("dm_l", [16, T])

        acc_a, acc_b = banks[4], banks[7]

        s_weights, s_setup, s_zeroed = sem("weights"), sem("setup"), sem("zeroed")
        rotary = prob_a[:, 0:2, :].rearrange("p a t -> p (a t)").rearrange("p (a t d) -> p a t d", a=4, d=FD)
        with nc.Block() as block:
            @block.sync
            def _(sp):
                loads = [(ident[:], consts["ident"]), (ident_bf[:], consts["ident_bf"]),
                         (win_q[:], consts["win_q"]), (win_k[:], consts["win_k"]),
                         (band_q[:], consts["band_q"]), (band_k[:], consts["band_k"]),
                         (lat_q[:], consts["lat_q"].rearrange("p (t l) -> p t l", l=NL)), (lat_k[:], consts["lat_k"]),
                         (blocks[:], consts["blocks"]), (pick[:], consts["pick"].rearrange("p (h k) -> p h k", k=P)),
                         (rotary, consts["rotary"].rearrange("p (a t d) -> p a t d", a=4, d=FD)),
                         (att_c[:], att_w.rearrange("h d e -> (h d) e")), (wv0_s[:], wv0T), (wo0_s[:], wo0T),
                         (bv0[:], wv0_b.partition_broadcast(P)), (bo0[:], wo0_b.partition_broadcast(P)),
                         (Wg_s[:], Wg), (bg_s[:], bg.partition_broadcast(P)),
                         (wq_s[:], wq), (wk_s[:], wk), (wv_s[:], wv), (w_out_s[:], w_out),
                         (wgqk_s[:], wgqk), (wgv_s[:], wgv), (r_out_s[:], r_out),
                         (gcol[:, 0:1], gate_l.rearrange("h (d o) -> (h d) o", o=1)),
                         (gcol[:, 1:2], gate_r.rearrange("h (d o) -> (h d) o", o=1)),
                         (wqkv_s[:], wqkv.rearrange("l d n -> d l n")),
                         (wo_s[:], wo.rearrange("l (c p) d -> p l c d", p=P)),
                         (w1_s[:], w1.rearrange("l d n -> d l n")),
                         (Kst_a[STACK:ROWS, :, :, :].rearrange("p r h t -> p (r h t)"), consts["ones_bf"])]
                for l in range(DEPTH):
                    loads += [(dst[:, l:l + 1], src[l, :].rearrange("(d o) -> d o", o=1)) for dst, src in ((lng_s, ln_g), (lnb_s, ln_b))]
                    loads += [(b2_s[:, l, :], b2[l, :].partition_broadcast(P)),
                              (qks[:, l, 0, :], q_sc[l, :].partition_broadcast(P)),
                              (qks[:, l, 1, :], k_sc[l, :].partition_broadcast(P))]
                    for c, (c0, n) in enumerate(HC):
                        loads += [(w2_s[0:n, l, c, :], w2[l, c0:c0 + n, :])]
                        loads += [(b1_s[0:n, l, half, c:c + 1],
                                   b1[l, half * HID + c0:half * HID + c0 + n].rearrange("(p o) -> p o", o=1))
                                  for half in range(2)]
                for dst, src in loads:
                    sp.dma_start(dst, src).then_inc(s_weights, 16)
                sp.wait_ge(s_weights, 16 * len(loads))
                sp.sem_inc(s_setup, 1)

            @block.vector
            def _(dve):
                nc.vector.memset(acc_a[:], 0.0)
                nc.vector.memset(acc_b[:], 0.0)
                for tile in (V_l[:], kT[:], mT_f[:], hT[64:P, 0:1], x1_a[:]):
                    last = nc.vector.memset(tile, 0.0)
                for tile in (V_a[:, :, :, D0:D0 + 1], V_b[:, :, :, D0:D0 + 1], V_f[:, :, :, FD:FD + 1]):
                    last = nc.vector.memset(tile, 1.0)
                last.then_inc(s_zeroed, 1)
                dve.wait_ge(s_zeroed, 1)
                nc.vector.memset(V_l[0:64, :, D0:D0 + 1], 1.0)
                nc.vector.memset(V_l[64:P, :, 16 + D0:16 + D0 + 1], 1.0)
                dve.wait_ge(s_setup, 1)
                blk = blocks[:].unsqueeze(2).to_broadcast([P, H0, D0])
                nc.vector.tensor_tensor(attW[:].rearrange("p (h e) -> p h e", e=D0), blk,
                                        att_c[:].unsqueeze(1).to_broadcast([P, H0, D0]), ALU.mult)
                for g in range(2):
                    nc.vector.tensor_scalar(gateW[:, g, :], blocks[:], gcol[:, g:g + 1], None, ALU.mult)
                for l in range(DEPTH):
                    for a in range(2):
                        s = qks[:, l, a, :].unsqueeze(1)
                        nc.vector.tensor_tensor(rotf[:, l, 2 * a], rotary[:, 2 * a],
                                                s.to_broadcast([P, NT, FD]), ALU.mult)
                        for lo in (0, FD // 2):
                            hi = FD // 2 - lo
                            nc.vector.tensor_tensor(
                                rotf[:, l, 2 * a + 1, :, lo:lo + 32], rotary[:, 2 * a + 1, :, lo:lo + 32],
                                s[:, :, hi:hi + 32].to_broadcast([P, NT, 32]), ALU.mult)

        def engine_sems(p):
            return {e: sem(f"{p}_emptied_by_{e}") for e in ("act", "dve")}

        a_x_in, a_xn, a_split, a_spill = (sem(n) for n in ("a_x_in", "a_xn", "a_split", "a_spill"))
        a_stack = [sem(f"a_stack{g}") for g in range(G)]
        a_mparts, a_mspill, a_mrow = sem("a_mparts"), [sem(f"a_mspill{g}") for g in range(G)], [sem(f"a_mrow{g}") for g in range(G)]
        a_av, a_og, a_tanh, a_x1 = (sem(n) for n in ("a_av", "a_og", "a_tanh", "a_x1"))
        a_w = [sem("a_expert0"), sem("a_expert1")]
        a_filled, a_emptied = sem("a_filled"), engine_sems("a")
        a_dve_step = sem("a_dve_step")
        b_x, b_xn, b_pool, b_split, b_spill = (sem(n) for n in ("b_x", "b_xn", "b_pool", "b_split", "b_spill"))
        b_ones, b_lstack = sem("b_ones"), sem("b_lstack")
        b_stack = [sem(f"b_stack{g}") for g in range(G)]
        b_mparts, b_mspill, b_mrow = sem("b_mparts"), [sem(f"b_mspill{g}") for g in range(G)], [sem(f"b_mrow{g}") for g in range(G)]
        b_lmparts, b_lmspill, b_lmrow = sem("b_lmparts"), sem("b_lmspill"), sem("b_lmrow")
        b_av, b_og, b_gate, b_mix = (sem(n) for n in ("b_av", "b_og", "b_gate", "b_mix"))
        b_filled, b_emptied = sem("b_filled"), engine_sems("b")
        b_dve_step, b_pool_step = sem("b_dve_step"), sem("b_pool_step")
        f_sq, f_sin, f_rot, f_mparts, f_prob_used = (sem(n) for n in ("f_sq", "f_sin", "f_rot", "f_mparts", "f_prob_used"))
        f_x, f_norm, f_gelu = (sem(n) for n in ("f_x", "f_norm", "f_gelu"))
        b_tanh, b_out, b_stored = sem("b_tanh"), sem("b_out"), sem("b_stored")

        first = [[("first", g, j, t) for j in range(4) for t in range(NT)] for g in range(G)]
        second = [[("second", g, k, j) for k in range(NT) for j in range(4)] for g in range(G)]
        plan_a = [("xnT", ["act"]), ("xw", ["act"]), ("v", ["dve"]), ("logits", ["dve"])]
        plan_a += [(f, ["dve"]) for f in first[0]] + [(("mT", 0), ["act"])]
        for g in range(G):
            for n in range(16):
                if g + 1 < G:
                    plan_a.append((first[g + 1][n], ["dve"]))
                plan_a.append((second[g][n], ["act"]))
            if g + 1 < G:
                plan_a.append((("mT", g + 1), ["act"]))
            plan_a.append((("oT", g), ["dve"]))
        plan_a += [("otokT", ["act"]), ("proj", ["dve"])]
        for e in range(NX):
            plan_a += [(("hid", e, c), ["act"]) for c in range(XC)] + [(("y", e), ["dve"])]
        bfirst = [[("first", g, t, h) for t in range(NT) for h in range(2)] for g in range(G)]
        bsecond = [[("second", g, k, h) for k in range(NT) for h in range(2)] for g in range(G)]
        plan_b = [("xnT", ["act"]), ("q", ["act"]), ("k", ["act"]), ("gqk", ["act", "dve"]),
                  ("v", ["act"]), ("gv", ["act"]), ("gates", ["act"])]
        plan_b += [(f, ["dve"]) for f in bfirst[0]] + [(("mT", 0), ["act"])]
        plan_b += [(("lfirst", t), ["dve"]) for t in range(NT)] + [("lmT", ["act"])]
        for g in range(G):
            for n in range(8):
                if g + 1 < G:
                    plan_b.append((bfirst[g + 1][n], ["dve"]))
                plan_b.append((bsecond[g][n], ["act"]))
            if g + 1 < G:
                plan_b.append((("mT", g + 1), ["act"]))
            plan_b.append((("oT", g), ["dve"]))
        plan_b += [(("lsecond", u), ["act"]) for u in range(4)] + [("loT", ["dve"]), ("remT", ["act"])]
        plan_b += [("rproj", ["dve"]), ("mixT", ["act"]), ("wout", ["act"])]
        for l in range(DEPTH):
            for t in range(NT):
                plan_b += [(("fq", l, t), ["act"]), (("fk", l, t), ["act"]), (("fv", l, t), ["act"])]
                plan_b += [(("qkT", l, t, a), ["act"]) for a in range(2)]
            plan_b += [(("ffirst", l, t, c), ["dve"]) for t in range(NT) for c in range(FH // 2)]
            plan_b += [(("fmT", l), ["act"])]
            for c in range(FH // 2):
                for k in range(NT):
                    plan_b += [(("fsecond", l, c, k), ["act"]), (("fav", l, c, k), ["dve"])]
                plan_b += [(("foT", l, c), ["act"])]
            plan_b += [(("fwo", l), ["dve"])]
            plan_b += [(("fx", l), ["act"]), (("fback", l), ["dve"]), (("fnT", l), ["dve"])]
            for c in range(len(HC)):
                plan_b += [(("fg", l, c), ["act"]), (("fa", l, c), ["dve"])]
            plan_b += [(("fw2", l), ["dve"])]
            if l + 1 < DEPTH:
                plan_b += [(("fnext", l), ["act"])]
        BA = Banks(banks[0:4], a_filled, a_emptied, plan_a)
        BB = Banks(banks[5:7], b_filled, b_emptied, plan_b)

        def transposes(dst, src, n=E, inc=None):
            for t in range(NT):
                last = nc.tensor.transpose(dst[0:n, t * P:(t + 1) * P], src[:, t, :], ident[:])
            last.then_inc(inc, 1)

        def chain(eng, s):
            count = [0]

            def link(ins):
                count[0] += 1
                ins.then_inc(s, 1)
                eng.wait_ge(s, count[0])
            return link

        def rsqrt(link, v, y, t):
            link(nc.vector.tensor_scalar(y.bitcast(I32), v.bitcast(I32), 1, None, ALU.logical_shift_right))
            link(nc.vector.tensor_scalar(y.bitcast(I32), y.bitcast(I32), -1.0, RSQRT_MAGIC, ALU.mult, ALU.add))
            for _ in range(3):
                link(nc.vector.scalar_tensor_tensor(out=t, in0=v, scalar=-0.5, in1=y, op0=ALU.mult, op1=ALU.mult))
                link(nc.vector.tensor_tensor(t, t, y, ALU.mult))
                link(nc.vector.scalar_tensor_tensor(out=y, in0=t, scalar=1.5, in1=y, op0=ALU.add, op1=ALU.mult))

        def layernorm(link, src, dst, stats, mv, rs, inc):
            for t in range(NT):
                last = nc.vector.bn_stats(stats[:, t, :], src[:, t, :])
            link(last)
            for t in range(NT):
                last = nc.vector.bn_aggr(mv[:, t, :], stats[:, t, :])
            link(last)
            link(nc.vector.tensor_scalar(rs[:, 0, :], mv[:, :, 1], EPS, None, ALU.add))
            rsqrt(link, rs[:, 0, :], rs[:, 1, :], rs[:, 2, :])
            for t in range(NT):
                last = nc.vector.tensor_scalar(dst[:, t, :], src[:, t, :], mv[:, t, 0:1], rs[:, 1, t:t + 1],
                                               ALU.subtract, ALU.mult)
            last.then_inc(inc, 1)

        def split(link, src, res, parts, inc):
            link(nc.vector.tensor_copy(parts[0], src))
            link(nc.vector.tensor_tensor(res, src, parts[0], ALU.subtract))
            link(nc.vector.tensor_copy(parts[1], res))
            link(nc.vector.tensor_tensor(res, res, parts[1], ALU.subtract))
            nc.vector.tensor_copy(parts[2], res).then_inc(inc, 1)

        def split_max(link, nmax, mhi, parts, inc):
            link(nc.vector.tensor_copy(mhi, nmax))
            nc.vector.tensor_copy(parts[0], mhi)
            nc.vector.tensor_tensor(parts[1], nmax, mhi, ALU.subtract).then_inc(inc, 1)

        def spill(sp, parts_q, parts_k, dq, dk, s):
            for i in range(SPLIT):
                sp.dma_start(dq[i, :, 0:SPLIT - i, :], parts_q[:, i:SPLIT, :]).then_inc(s, 16)
                if i:
                    sp.dma_start(dq[i, :, SPLIT - i:SPLIT, :], parts_q[:, 0:i, :]).then_inc(s, 16)
            sp.dma_start(dk, parts_k).then_inc(s, 16)

        SPILLED, STACKED = 6 * 16, 6 * 16

        def load_stack(sp, dq, dk, h, n, Qst, Kst, s):
            for i in range(SPLIT):
                r = slice(i * SPLIT * D0, (i + 1) * SPLIT * D0)
                rows = slice(h * D0, (h + n) * D0)
                sp.dma_start(Qst[r, :, :], dq[i, rows].rearrange("(h d) c t -> (d c) h t", d=D0)).then_inc(s, 16)
                sp.dma_start(Kst[r, :, :], dk[rows].rearrange("(h d) c t -> (d c) h t", d=D0)).then_inc(s, 16)

        def max_to_stack(sp, mT, dm, Qst, spilled, landed):
            sp.dma_start(dm, mT).then_inc(spilled, 16)
            sp.wait_ge(spilled, 16)
            sp.dma_start(Qst[STACK:ROWS, :, :], dm.rearrange("(a h) t -> a h t", a=2)).then_inc(landed, 16)

        def a_sync(sp, b):
            yield 0
            sp.dma_start(x_a[:], x_in[b, :, :].rearrange("o (n p) f -> p (o n) f", p=P)).then_inc(a_x_in, 16)
            yield 4
            sp.wait_ge(a_split, 1)
            spill(sp, parts_a[:, 1], parts_a[:, 0], dq_a, dk_a, a_spill)
            sp.wait_ge(a_spill, SPILLED)

            def stack(g):
                load_stack(sp, dq_a, dk_a, 4 * g, 4, Qst_a[:, g % RING], Kst_a[:, g % RING], a_stack[g])

            for g in range(RING):
                stack(g)
            for g in range(G):
                yield 20 + 20 * g
                sp.wait_ge(*BA.brought(("mT", g), "act"))
                max_to_stack(sp, mT_a[:, g % 2, :], dm_a[g], Qst_a[:, g % RING], a_mspill[g], a_mrow[g])
                if g + RING < G:
                    yield 38 + 20 * g
                    sp.wait_ge(*BA.made(second[g][-1]))
                    stack(g + RING)
            for e in range(NX):
                yield 104 + 5 * e
                if e >= 2:
                    sp.wait_ge(*BA.made(("y", e - 2)))
                sp.dma_start(W1_s[:, e % 2, :], W1[e]).then_inc(a_w[e % 2], 16)
                sp.dma_start(W2_s[:, e % 2], W2[e].rearrange("(c p) d -> p c d", p=P)).then_inc(a_w[e % 2], 16)

        def a_tensor(pe):
            yield 1
            pe.wait_ge(a_xn, 1)
            transposes(BA.take(pe, "xnT"), xn_a, inc=a_filled)
            yield 2
            pe.wait_ge(*BA.brought("xnT", "act"))
            nc.tensor.matmul(BA.take(pe, "xw")[:], attW[:], kq_a[:, 0, :], start=True, stop=True).then_inc(a_filled, 1)
            ps = BA.take(pe, "v")
            for t in range(NT):
                last = nc.tensor.matmul(ps[:, t * E:(t + 1) * E], kq_a[:, 0, t * P:(t + 1) * P], wv0_s[:], start=True, stop=True)
            last.then_inc(a_filled, 1)
            ps = BA.take(pe, "logits")
            for t in range(NT):
                last = nc.tensor.matmul(ps[:, t * NX:(t + 1) * NX], kq_a[:, 0, t * P:(t + 1) * P], Wg_s[:], start=True, stop=True)
            last.then_inc(a_filled, 1)

            def first_pass(g, n):
                _, _, j, t = f = first[g][n]
                if n == 0:
                    pe.wait_ge(a_stack[g], STACKED)
                nc.tensor.matmul(BA.take(pe, f)[:], Qst_a[0:STACK, g % RING, j, t * P:(t + 1) * P],
                                 Kst_a[0:STACK, g % RING, j, :], start=True, stop=True).then_inc(a_filled, 1)

            def max_rows(g):
                pe.wait_ge(a_mparts, g + 1)
                transposes(BA.take(pe, ("mT", g)), mparts_a[:, g].rearrange("p t a j -> p t (a j)"), 8, a_filled)

            def values(g, k):
                pe.wait_ge(*BA.brought(("second", g, k, 3), "act"))
                if k == 0:
                    if g == 0:
                        pe.wait_ge(*BA.brought("v", "dve"))
                    else:
                        pe.wait_ge(a_og, g)
                for j in range(4):
                    last = nc.tensor.matmul(acc_a[32 * j:32 * j + D0 + 1, :], V_a[:, k, 4 * g + j, :],
                                            prob_a[:, (4 * k + j) % PR_A, :], start=(k == 0), stop=(k == NT - 1))
                last.then_inc(a_av, 1)

            for n in range(16):
                yield 9 + n / 2
                first_pass(0, n)
            yield 18
            max_rows(0)
            for g in range(G):
                for n in range(16):
                    yield 22 + 20 * g + n
                    if g + 1 < G:
                        first_pass(g + 1, n)
                    if n == 0:
                        pe.wait_ge(a_mrow[g], 16)
                    _, _, k, j = s = second[g][n]
                    nc.tensor.matmul(BA.take(pe, s)[:], Kst_a[:, g % RING, j, k * P:(k + 1) * P], Qst_a[:, g % RING, j, :],
                                     start=True, stop=True).then_inc(a_filled, 1)
                    if n % 4 == 1 and n > 4:
                        values(g, n // 4 - 1)
                yield 38 + 20 * g
                values(g, 3)
                if g + 1 < G:
                    max_rows(g + 1)
                yield 39 + 20 * g
                pe.wait_ge(a_og, g + 1)
                transposes(BA.take(pe, ("oT", g)), og_a[:].rearrange("p (t q) -> p t q", q=P), inc=a_filled)
            yield 104
            pe.wait_ge(*BA.brought(("oT", G - 1), "dve"))
            transposes(BA.take(pe, "otokT"), otok_a, inc=a_filled)
            yield 105
            pe.wait_ge(*BA.brought("otokT", "act"))
            ps = BA.take(pe, "proj")
            for t in range(NT):
                last = nc.tensor.matmul(ps[:, t * E:(t + 1) * E], oT_a[:, t * P:(t + 1) * P], wo0_s[:], start=True, stop=True)
            last.then_inc(a_filled, 1)
            for e in range(NX):
                for c in range(XC):
                    yield 106 + 5 * e + c
                    if c == 0:
                        pe.wait_ge(a_w[e % 2], 32 * (e // 2 + 1))
                    nc.tensor.matmul(BA.take(pe, ("hid", e, c))[:], W1_s[:, e % 2, c * P:(c + 1) * P], kq_a[:, 0, :],
                                     start=True, stop=True).then_inc(a_filled, 1)
                yield 110 + 5 * e
                pe.wait_ge(*BA.brought(("hid", e, XC - 1), "act"))
                ps = BA.take(pe, ("y", e))
                for t in range(NT):
                    for c in range(XC):
                        last = nc.tensor.matmul(ps[:, t * E:(t + 1) * E], hid_a[:, c, t * P:(t + 1) * P],
                                                W2_s[:, e % 2, c, :], start=(c == 0), stop=(c == XC - 1))
                last.then_inc(a_filled, 1)

        def a_scalar(act):
            def bring(product, dst, func=ACT.Copy, rows=P, **kw):
                nc.scalar.activation(dst, BA.full(act, product)[0:rows, :], func, **kw).then_inc(a_emptied["act"], 1)

            yield 1
            bring("xnT", kq_a[:, 0, :])
            yield 2
            bring("xw", kq_a[:, 1, :])
            yield 19
            bring(("mT", 0), mT_a[:, 0, :], rows=8)
            for g in range(G):
                for n in range(16):
                    yield 22 + 20 * g + n
                    if n % 4 == 0 and 4 * g + n // 4 >= 2:
                        act.wait_ge(a_av, 4 * g + n // 4 - 1)
                    bring(second[g][n], prob_a[:, n % PR_A, :], ACT.Exp, scale=HEAD_SCALE)
                yield 38 + 20 * g
                if g + 1 < G:
                    if g >= 1:
                        act.wait_ge(a_mspill[g - 1], 16)
                    bring(("mT", g + 1), mT_a[:, (g + 1) % 2, :], rows=8)
                act.wait_ge(a_av, 4 * g + 4)
                if g:
                    act.wait_ge(*BA.made(("oT", g - 1)))
                nc.scalar.activation(og_a[:], acc_a[:], ACT.Copy).then_inc(a_og, 1)
            yield 104
            bring("otokT", oT_a[:])
            for e in range(NX):
                for c in range(XC):
                    yield 106 + 5 * e + c
                    if c == 0:
                        if e:
                            act.wait_ge(*BA.made(("y", e - 1)))
                        else:
                            act.wait_ge(a_av, 4 * G)
                    bring(("hid", e, c), hid_a[:, c, :], ACT.Gelu_apprx_tanh)
            yield 150
            act.wait_ge(*BA.made("proj"))
            act.wait_ge(*BA.brought(("y", NX - 1), "dve"))
            nc.scalar.activation(th_a[:], y_a[:], ACT.Tanh, scale=0.5).then_inc(a_tanh, 1)

        def a_vector(dve, beside_b):
            link = chain(dve, a_dve_step)
            emptied = a_emptied["dve"]
            yield 0
            dve.wait_ge(a_x_in, 16)
            layernorm(link, x_a, xn_a, stats_a, mv_a, rs_a, a_xn)
            yield 2
            ps = BA.full(dve, "v")
            nc.vector.tensor_tensor(V_a[:, :, :, 0:D0], ps[:].rearrange("p (t h d) -> p t h d", t=NT, d=D0),
                                    bv0[:].rearrange("p (h d) -> p h d", d=D0).unsqueeze(1)
                                    .to_broadcast([P, NT, H0, D0]), ALU.add).then_inc(emptied, 1)
            yield 3
            ps = BA.full(dve, "logits")
            nc.vector.tensor_tensor(lg_a[:], ps[:, 0:NT * NX].rearrange("p (t e) -> p t e", e=NX),
                                    bg_s[:].unsqueeze(1).to_broadcast([P, NT, NX]), ALU.add).then_inc(emptied, 1)
            dve.wait_ge(*BA.brought("logits", "dve"))
            link(nc.vector.tensor_reduce(out=mx_a[:], in_=lg_a[:], op=ALU.max, axis=AX.X))
            link(nc.vector.tensor_tensor(sc_a[:], lg_a[:], mx_a[:].unsqueeze(2).to_broadcast([P, NT, NX]), ALU.is_equal))
            link(nc.vector.memset(before_a[:, :, 0:1], 0.0))
            for e in range(1, NX):
                link(nc.vector.tensor_tensor(before_a[:, :, e:e + 1], before_a[:, :, e - 1:e], sc_a[:, :, e - 1:e], ALU.max))
            link(nc.vector.tensor_scalar(before_a[:], before_a[:], -1.0, 1.0, ALU.mult, ALU.add))
            link(nc.vector.tensor_tensor(hot_a[:], before_a[:], sc_a[:], ALU.mult))
            dve.wait_ge(*BA.brought("xw", "act"))
            split(link, kq_a[:], res_a, [parts_a[:, :, c, :] for c in range(SPLIT)], a_split)

            def first_pass(g, n):
                _, _, j, t = f = first[g][n]
                nc.vector.tensor_reduce(out=nmax_a[:, g, t, j:j + 1], in_=BA.full(dve, f)[:], op=ALU.max, axis=AX.X,
                                        negate=True).then_inc(emptied, 1)

            def max_parts(g):
                dve.wait_ge(*BA.brought(first[g][-1], "dve"))
                split_max(link, nmax_a[:, g], mhi_a[:, g], [mparts_a[:, g, :, p, :] for p in range(2)], a_mparts)

            for n in range(16):
                yield 9 + n / 2
                first_pass(0, n)
            yield 18
            max_parts(0)
            for g in range(G):
                for n in range(16):
                    yield 22 + 20 * g + n
                    if g + 1 < G:
                        first_pass(g + 1, n)
                yield 38 + 20 * g
                if g + 1 < G:
                    max_parts(g + 1)
                yield 39 + 20 * g
                ps = BA.full(dve, ("oT", g))[:].rearrange("p (t j c) -> p t j c", t=NT, c=32)
                link(nc.vector.reciprocal(rden_a[:], ps[:, :, :, D0]))
                nc.vector.tensor_tensor(otok_a[:, :, 32 * g:32 * g + 32].rearrange("p t (j d) -> p t j d", d=D0),
                                        ps[:, :, :, 0:D0], rden_a[:].unsqueeze(3).to_broadcast([P, NT, 4, D0]),
                                        ALU.mult).then_inc(emptied, 1)
            yield 106
            tiles = "p (t e) -> p t e"
            ps = BA.full(dve, "proj")
            nc.vector.tensor_tensor(s_a[:].rearrange(tiles, e=E), ps[:].rearrange(tiles, e=E),
                                    bo0[:].unsqueeze(1).to_broadcast([P, NT, E]), ALU.add).then_inc(emptied, 1)
            for e in range(NX):
                yield 111 + 5 * e
                ps = BA.full(dve, ("y", e))
                if e:
                    dve.wait_ge(*BA.brought(("y", e - 1), "dve"))
                for t in range(NT):
                    y, src, hot = y_a[:, t * E:(t + 1) * E], ps[:, t * E:(t + 1) * E], hot_a[:, t, e:e + 1]
                    if e == 0:
                        last = nc.vector.tensor_scalar(y, src, hot, None, ALU.mult)
                    else:
                        last = nc.vector.scalar_tensor_tensor(out=y, in0=src, scalar=hot, in1=y, op0=ALU.mult, op1=ALU.add)
                last.then_inc(emptied, 1)
            yield 151
            dve.wait_ge(a_tanh, 1)
            link(nc.vector.scalar_tensor_tensor(out=th_a[:], in0=th_a[:], scalar=1.0, in1=y_a[:], op0=ALU.add, op1=ALU.mult))
            link(nc.vector.tensor_tensor(th_a[:], th_a[:], s_a[:], ALU.mult))
            if beside_b:
                dve.wait_ge(b_x, 1)
            nc.vector.scalar_tensor_tensor(out=x1_a[:].rearrange("p t e -> p (t e)"), in0=th_a[:], scalar=0.5,
                                           in1=x_a[:].rearrange("p t e -> p (t e)"), op0=ALU.mult, op1=ALU.add).then_inc(a_x1, 1)

        def b_sync(sp, b):
            yield 4
            sp.wait_ge(b_split, 1)
            spill(sp, parts_b[:, 0], parts_b[:, 1], dq_b, dk_b, b_spill)
            spill(sp, parts_b[0:64, 2], parts_b[64:P, 2, :, 0:NL], dq_l, dk_l, b_spill)
            sp.wait_ge(b_spill, 2 * SPILLED)
            sp.dma_start(Kst_b[STACK:ROWS].rearrange("p r h t -> p (r h t)"), consts["ones_bf"]).then_inc(b_ones, 16)
            sp.dma_start(Kst_l[STACK:ROWS].rearrange("p h t -> p (h t)"), consts["ones_bf"][:, 0:LH * NL]).then_inc(b_ones, 16)

            def stack(g):
                load_stack(sp, dq_b, dk_b, 4 * g, 4, Qst_b[:, g % RING], Kst_b[:, g % RING], b_stack[g])

            stack(0)
            load_stack(sp, dq_l, dk_l, 0, LH, Qst_l, Kst_l, b_lstack)
            stack(1)
            yield 20
            sp.wait_ge(*BB.brought(("mT", 0), "act"))
            max_to_stack(sp, mT_b[:, 0, :], dm_b[0], Qst_b[:, 0], b_mspill[0], b_mrow[0])
            sp.wait_ge(*BB.brought("lmT", "act"))
            max_to_stack(sp, mT_l[:], dm_l, Qst_l, b_lmspill, b_lmrow)
            for g in range(G):
                if g + 1 < G:
                    yield 32 + 12 * g
                    sp.wait_ge(*BB.made(bsecond[g][-1]))
                    if g + RING < G:
                        stack(g + RING)
                    sp.wait_ge(*BB.brought(("mT", g + 1), "act"))
                    max_to_stack(sp, mT_b[:, (g + 1) % 2, :], dm_b[g + 1], Qst_b[:, (g + 1) % RING], b_mspill[g + 1], b_mrow[g + 1])
            yield 400
            sp.wait_ge(b_out, 1)
            sp.dma_start(out[b, :, :].rearrange("o (n p) f -> p (o n) f", p=P), x_f[:]).then_inc(b_stored, 16)
            sp.wait_ge(b_stored, 16)

        def b_gpsimd(pool):
            yield 0
            nc.gpsimd.tensor_copy(x_b[:], x1_a[:]).then_inc(b_x, 1)
            for l in range(DEPTH):
                for t in range(NT):
                    yield 90 + 150 * l + 5 * t
                    pool.wait_ge(*BB.brought(("fk", l, t), "act"))
                    n = NT * l + t
                    if n:
                        pool.wait_ge(f_rot, n)
                    else:
                        pass
                    raw = qk_raw.rearrange("p a (h d) -> p a h d", d=FD)
                    sin = sq.rearrange("p a (h d) -> p a h d", d=FD)
                    pool.wait_ge(f_sq, n + 1)
                    for a in range(2):
                        for lo in (0, FD // 2):
                            hi = FD // 2 - lo
                            last = nc.gpsimd.tensor_tensor(
                                sin[:, a, :, lo:lo + 32], raw[:, a, :, hi:hi + 32],
                                rotf[:, l, 2 * a + 1, t, lo:lo + 32].unsqueeze(1).to_broadcast([P, FH, 32]), ALU.mult)
                    last.then_inc(f_sin, 1)

        def b_tensor(pe):
            yield 1
            pe.wait_ge(b_xn, 1)
            transposes(BB.take(pe, "xnT"), xn_b, inc=b_filled)
            yield 2
            pe.wait_ge(*BB.brought("xnT", "act"))
            for product, w in (("q", wq_s), ("k", wk_s), ("gqk", wgqk_s)):
                nc.tensor.matmul(BB.take(pe, product)[:], w[:], xnT_b[:], start=True, stop=True).then_inc(b_filled, 1)
            yield 3
            ps = BB.take(pe, "v")
            for t in range(NT):
                last = nc.tensor.matmul(ps[:, t * E:(t + 1) * E], xnT_b[:, t * P:(t + 1) * P], wv_s[:], start=True, stop=True)
            last.then_inc(b_filled, 1)
            pe.wait_ge(b_pool, 1)
            nc.tensor.matmul(BB.take(pe, "gv")[:, 0:NL], pool_b[:].rearrange("p a l -> p (a l)"), wgv_s[:],
                             start=True, stop=True).then_inc(b_filled, 1)
            pe.wait_ge(*BB.brought("q", "act"))
            ps = BB.take(pe, "gates")
            for t in range(NT):
                last = nc.tensor.matmul(ps[:, t * 32:(t + 1) * 32], qkg_b[:, 0, t * P:(t + 1) * P],
                                        gateW[:].rearrange("p g h -> p (g h)"), start=True, stop=True)
            last.then_inc(b_filled, 1)

            def first_pass(g, n):
                _, _, t, hp = f = bfirst[g][n]
                if n == 0:
                    pe.wait_ge(b_stack[g], STACKED)
                skip = WIN if t == 0 else 0
                nk = LKEYS - skip
                k0 = t * P - WIN + skip
                ps = BB.take(pe, f)
                nc.tensor.matmul(ps[:, 0:2 * nk], ident_bf[:], win_q[:].rearrange("p (a k) -> p a k", a=2)[:, :, skip:],
                                 start=True, stop=False)
                for a in range(2):
                    last = nc.tensor.matmul(ps[:, a * nk:(a + 1) * nk], Qst_b[0:STACK, g % RING, 2 * hp + a, t * P:(t + 1) * P],
                                            Kst_b[0:STACK, g % RING, 2 * hp + a, k0:k0 + nk], start=False, stop=(a == 1))
                last.then_inc(b_filled, 1)

            def max_rows(g):
                pe.wait_ge(b_mparts, g + 1)
                transposes(BB.take(pe, ("mT", g)), mparts_b[:, g].rearrange("p t a j -> p t (a j)"), 8, b_filled)

            def values(g, k):
                pe.wait_ge(*BB.brought(("second", g, k, 1), "act"))
                if k == 0:
                    if g == 0:
                        pe.wait_ge(*BB.brought("v", "act"))
                    else:
                        pe.wait_ge(b_og, g)
                nq = min(LKEYS, T - k * P)
                for j in range(4):
                    last = nc.tensor.matmul(acc_b[32 * j:32 * j + D0 + 1, k * P:k * P + nq], V_b[:, k, 4 * g + j, :],
                                            prob_b[:, (2 * k + j // 2) % PR_B, (j % 2) * nq:(j % 2 + 1) * nq],
                                            start=(k == 0), stop=(k == NT - 1), skip_group_check=True)
                last.then_inc(b_av, 1)

            for n in range(8):
                yield 9 + n
                first_pass(0, n)
            yield 17
            max_rows(0)
            for t in range(NT):
                yield 18 + t / 4
                if t == 0:
                    pe.wait_ge(b_lstack, STACKED)
                ps = BB.take(pe, ("lfirst", t))
                nc.tensor.matmul(ps[:], ident_bf[:], lat_q[:, t, :].unsqueeze(1).to_broadcast([P, LH, NL]), start=True, stop=False)
                for h in range(LH):
                    last = nc.tensor.matmul(ps[:, h * NL:(h + 1) * NL], Qst_l[0:STACK, h, t * P:(t + 1) * P],
                                            Kst_l[0:STACK, h, :], start=False, stop=(h == LH - 1))
                last.then_inc(b_filled, 1)
            yield 19
            pe.wait_ge(b_lmparts, 1)
            transposes(BB.take(pe, "lmT"), mparts_l[:].rearrange("p t a h -> p t (a h)"), 2 * LH, b_filled)
            for g in range(G):
                for n in range(8):
                    yield 22 + 12 * g + n
                    if g + 1 < G:
                        first_pass(g + 1, n)
                    if n == 0:
                        pe.wait_ge(b_mrow[g], 16)
                        pe.wait_ge(b_ones, 32)
                    _, _, k, hp = s = bsecond[g][n]
                    nq = min(LKEYS, T - k * P)
                    ps = BB.take(pe, s)
                    nc.tensor.matmul(ps[:, 0:2 * nq], ident_bf[:], win_k[:].rearrange("p (a k) -> p a k", a=2)[:, :, 0:nq],
                                     start=True, stop=False)
                    for a in range(2):
                        last = nc.tensor.matmul(ps[:, a * nq:(a + 1) * nq], Kst_b[:, g % RING, 2 * hp + a, k * P:(k + 1) * P],
                                                Qst_b[:, g % RING, 2 * hp + a, k * P:k * P + nq], start=False, stop=(a == 1))
                    last.then_inc(b_filled, 1)
                    if n % 2 == 0 and n:
                        values(g, n // 2 - 1)
                yield 30 + 12 * g
                values(g, 3)
                if g + 1 < G:
                    max_rows(g + 1)
                yield 31 + 12 * g
                pe.wait_ge(b_og, g + 1)
                transposes(BB.take(pe, ("oT", g)), og_b[:].rearrange("p (t q) -> p t q", q=P), inc=b_filled)
            for u in range(4):
                yield 72 + u
                if u == 0:
                    pe.wait_ge(b_lmrow, 16)
                ps = BB.take(pe, ("lsecond", u))
                nc.tensor.matmul(ps[:], ident_bf[:], lat_k[:], start=True, stop=False, skip_group_check=True)
                for a in range(2):
                    last = nc.tensor.matmul(ps[64 * a:64 * a + 64, :], Kst_l[:, 2 * u + a, :], Qst_l[:, 2 * u + a, :],
                                            start=False, stop=(a == 1), skip_group_check=True)
                last.then_inc(b_filled, 1)
            yield 76
            pe.wait_ge(*BB.brought(("lsecond", 3), "act"))
            pe.wait_ge(*BB.brought("gv", "act"))
            pe.wait_ge(b_og, G)
            for u in range(4):
                last = nc.tensor.matmul(acc_b[32 * u:32 * u + 32, :], V_l[:, u, :], prob_b[:, u, :], start=True, stop=True)
            last.then_inc(b_av, 1)
            yield 77
            pe.wait_ge(b_og, G + 1)
            transposes(BB.take(pe, "loT"), og_b[:].rearrange("p (t q) -> p t q", q=P), inc=b_filled)
            yield 78
            pe.wait_ge(*BB.brought("loT", "dve"))
            transposes(BB.take(pe, "remT"), rem_b, NL, b_filled)
            yield 79
            pe.wait_ge(*BB.brought("remT", "act"))
            ps = BB.take(pe, "rproj")
            for t in range(NT):
                last = nc.tensor.matmul(ps[:, t * E:(t + 1) * E], og_b[0:NL, t * P:(t + 1) * P], r_out_s[:], start=True, stop=True)
            last.then_inc(b_filled, 1)
            yield 80
            pe.wait_ge(b_mix, 1)
            transposes(BB.take(pe, "mixT"), mix_b[:].rearrange("p (t e) -> p t e", e=E), inc=b_filled)
            yield 81
            pe.wait_ge(*BB.brought("mixT", "act"))
            ps = BB.take(pe, "wout")
            for t in range(NT):
                last = nc.tensor.matmul(ps[:, t * E:(t + 1) * E], og_b[:, t * P:(t + 1) * P], w_out_s[:], start=True, stop=True)
            last.then_inc(b_filled, 1)

            for l in range(DEPTH):
                s0 = 88 + 150 * l
                for t in range(NT):
                    yield s0 + 5 * t
                    if l and t == 0:
                        pe.wait_ge(*BB.brought(("fnext", l - 1), "act"))
                    for n, product in enumerate(("fq", "fk", "fv")):
                        nc.tensor.matmul(BB.take(pe, (product, l, t))[:], hT[:, t * P:(t + 1) * P],
                                         wqkv_s[:, l, n * INNER:(n + 1) * INNER], start=True, stop=True).then_inc(b_filled, 1)
                    yield s0 + 5 * t + 4
                    pe.wait_ge(f_rot, NT * l + t + 1)
                    for a in range(2):
                        ps = BB.take(pe, ("qkT", l, t, a))
                        for c in range(FH // 2):
                            last = nc.tensor.transpose(ps[:, c * P:(c + 1) * P], qk_rot[:, a, c * P:(c + 1) * P], ident[:])
                        last.then_inc(b_filled, 1)
                for t in range(NT):
                    for c in range(FH // 2):
                        yield s0 + 22 + 4 * t + c
                        if t == 0 and c == 0:
                            pe.wait_ge(*BB.brought(("qkT", l, NT - 1, 1), "act"))
                        skip = FW if t == 0 else 0
                        nk = FKEYS - skip
                        k0 = t * P - FW + skip
                        ps = BB.take(pe, ("ffirst", l, t, c))
                        nc.tensor.matmul(ps[:, 0:2 * nk], ident_bf[:], band_q[:].rearrange("p (a k) -> p a k", a=2)[:, :, skip:],
                                         start=True, stop=False)
                        for a in range(2):
                            last = nc.tensor.matmul(ps[:, a * nk:(a + 1) * nk], qT[:, c, t * P:(t + 1) * P],
                                                    kT[:, c, a, k0:k0 + nk], start=False, stop=(a == 1))
                        last.then_inc(b_filled, 1)
                yield s0 + 39
                pe.wait_ge(f_mparts, l + 1)
                transposes(BB.take(pe, ("fmT", l)), mparts_f[:].rearrange("p t a h -> p t (a h)"), 2 * FH, b_filled)

                def keys_first(c, k):
                    if c == 0 and k == 0:
                        pe.wait_ge(*BB.brought(("fmT", l), "act"))
                    nq = min(FKEYS, T - k * P)
                    q = slice(k * P, k * P + nq)
                    ps = BB.take(pe, ("fsecond", l, c, k))
                    nc.tensor.matmul(ps[:, 0:2 * nq], ident_bf[:], band_k[:].rearrange("p (a k) -> p a k", a=2)[:, :, 0:nq],
                                     start=True, stop=False)
                    for a in range(2):
                        nc.tensor.matmul(ps[:, a * nq:(a + 1) * nq], pick[:, 2 * c + a, :], mT_f[:, q], start=False, stop=False)
                        last = nc.tensor.matmul(ps[:, a * nq:(a + 1) * nq], kT[:, c, a, k * P:(k + 1) * P], qT[:, c, q],
                                                start=False, stop=(a == 1))
                    last.then_inc(b_filled, 1)

                def values_f(c, k):
                    pe.wait_ge(*BB.brought(("fsecond", l, c, k), "act"))
                    ps = BB.take(pe, ("fav", l, c, k))
                    nq = min(FKEYS, T - k * P)
                    for a in range(2):
                        o = ps[:, a * (FD + 1):(a + 1) * (FD + 1)]
                        last = nc.tensor.matmul(o, prob_b[:, k % PR_B, a * nq:a * nq + P], V_f[:, k, 2 * c + a, :],
                                                start=True, stop=True)
                        if k:
                            last = nc.tensor.matmul(o[0:FW, :], prob_b[:, (k - 1) % PR_B, a * FKEYS + P:(a + 1) * FKEYS],
                                                    V_f[:, k - 1, 2 * c + a, :], start=False, stop=True, skip_group_check=True)
                    last.then_inc(b_filled, 1)

                for c in range(FH // 2):
                    for k in range(NT):
                        yield s0 + 42 + 8 * c + 2 * k
                        keys_first(c, k)
                        yield s0 + 43 + 8 * c + 2 * k
                        values_f(c, k)
                    yield s0 + 50 + 8 * c
                    pe.wait_ge(*BB.brought(("fav", l, c, NT - 1), "dve"))
                    transposes(BB.take(pe, ("foT", l, c)), otok_f[:, c % 2], inc=b_filled)
                yield s0 + 76
                pe.wait_ge(*BB.brought(("foT", l, FH // 2 - 1), "act"))
                ps = BB.take(pe, ("fwo", l))
                for t in range(NT):
                    for c in range(INNER // P):
                        last = nc.tensor.matmul(ps[:, t * E:(t + 1) * E], oT_f[:, c, t * P:(t + 1) * P], wo_s[:, l, c, :],
                                                start=(c == 0), stop=(c == INNER // P - 1))
                last.then_inc(b_filled, 1)
                yield s0 + 78
                pe.wait_ge(*BB.brought(("fwo", l), "dve"))
                transposes(BB.take(pe, ("fx", l)), x_f, inc=b_filled)
                yield s0 + 80
                pe.wait_ge(*BB.brought(("fx", l), "act"))
                transposes(BB.take(pe, ("fback", l)), hT[:].rearrange("p (t q) -> p t q", q=P), inc=b_filled)
                yield s0 + 82
                pe.wait_ge(*BB.brought(("fback", l), "dve"))
                transposes(BB.take(pe, ("fnT", l)), xn_b, inc=b_filled)
                for c, (c0, n) in enumerate(HC):
                    yield s0 + 84 + 2 * c
                    if c == 0:
                        pe.wait_ge(*BB.brought(("fnT", l), "dve"))
                    for product, col in (("fg", HID + c0), ("fa", c0)):
                        nc.tensor.matmul(BB.take(pe, (product, l, c))[0:n, :], w1_s[:, l, col:col + n], xnT_b[:],
                                         start=True, stop=True).then_inc(b_filled, 1)
                yield s0 + 92
                pe.wait_ge(*BB.brought(("fa", l, len(HC) - 1), "dve"))
                ps = BB.take(pe, ("fw2", l))
                for t in range(NT):
                    for c, (c0, n) in enumerate(HC):
                        last = nc.tensor.matmul(ps[:, t * E:(t + 1) * E], u_f[0:n, c, t * P:(t + 1) * P], w2_s[0:n, l, c, :],
                                                start=(c == 0), stop=(c == len(HC) - 1))
                last.then_inc(b_filled, 1)
                if l + 1 < DEPTH:
                    yield s0 + 96
                    pe.wait_ge(f_x, 2 * l + 2)
                    transposes(BB.take(pe, ("fnext", l)), x_f, inc=b_filled)

        def b_scalar(act):
            def bring(product, dst, func=ACT.Copy, rows=slice(0, P), cols=slice(0, T), last=True, **kw):
                ins = nc.scalar.activation(dst, BB.full(act, product)[rows, cols], func, **kw)
                if last:
                    ins.then_inc(b_emptied["act"], 1)

            def shifted(product):
                bring(product, hT[0:64, :], rows=slice(0, 64), last=False)
                bring(product, hT[64:P, 1:T], rows=slice(64, P), cols=slice(0, T - 1))

            yield 1
            bring("xnT", xnT_b[:], last=False)
            shifted("xnT")
            yield 2
            bring("q", qkg_b[:, 0, :])
            bring("k", qkg_b[:, 1, :])
            bring("gqk", qkg_b[0:64, 2, :], rows=slice(0, 64))
            yield 3
            ps = BB.full(act, "v")
            nc.scalar.activation(V_b[:].rearrange("p t h c -> p (t h) c")[:, :, 0:D0],
                                 ps[:].rearrange("p (n d) -> p n d", d=D0), ACT.Copy).then_inc(b_emptied["act"], 1)
            ps = BB.full(act, "gv")
            for a in range(2):
                half = slice(64 * a, 64 * a + 64)
                last = nc.scalar.activation(V_l[half, :, 16 * a:16 * a + D0],
                                            ps[half, 0:NL].rearrange("p (u a d) -> p u a d", a=2, d=D0)[:, :, a, :], ACT.Copy)
            last.then_inc(b_emptied["act"], 1)
            ps = BB.full(act, "gates")
            nc.scalar.activation(gate_b[:].rearrange("p t g h -> p (t g h)"), ps[:, 0:P], ACT.Tanh,
                                 scale=0.5).then_inc(b_emptied["act"], 1)
            yield 18
            bring(("mT", 0), mT_b[:, 0, :], rows=slice(0, 8))
            yield 20
            bring("lmT", mT_l[:], rows=slice(0, 2 * LH))
            for g in range(G):
                for n in range(8):
                    yield 22 + 12 * g + n
                    if n % 2 == 0 and 4 * g + n // 2 >= 2:
                        act.wait_ge(b_av, 4 * g + n // 2 - 1)
                    nq = min(LKEYS, T - n // 2 * P)
                    if g == 0 and n == 0:
                        act.wait_ge(b_split, 1)
                    bring(bsecond[g][n], prob_b[:, n % PR_B, 0:2 * nq], ACT.Exp, cols=slice(0, 2 * nq), scale=HEAD_SCALE)
                yield 30 + 12 * g
                if g + 1 < G:
                    if g >= 1:
                        act.wait_ge(b_mspill[g - 1], 16)
                    bring(("mT", g + 1), mT_b[:, (g + 1) % 2, :], rows=slice(0, 8))
                act.wait_ge(b_av, 4 * g + 4)
                if g:
                    act.wait_ge(*BB.made(("oT", g - 1)))
                nc.scalar.activation(og_b[:], acc_b[:], ACT.Copy).then_inc(b_og, 1)
            for u in range(4):
                yield 72 + u
                bring(("lsecond", u), prob_b[:, u, :], ACT.Exp, scale=HEAD_SCALE)
            yield 76
            act.wait_ge(b_av, 4 * G + 1)
            act.wait_ge(*BB.made(("oT", G - 1)))
            nc.scalar.activation(og_b[:], acc_b[:], ACT.Copy).then_inc(b_og, 1)
            yield 78
            bring("remT", og_b[0:NL, :], rows=slice(0, NL))
            yield 80
            act.wait_ge(*BB.made("rproj"))
            bring("mixT", og_b[:])
            yield 81
            bring("wout", s_b[:])
            for l in range(DEPTH):
                s0 = 88 + 150 * l
                for t in range(NT):
                    yield s0 + 5 * t
                    n = NT * l + t
                    if n:
                        act.wait_ge(f_sin, n)
                        act.wait_ge(f_rot, n)
                    for a, product in enumerate(("fq", "fk")):
                        bring((product, l, t), sq[:, a, :], ACT.Square, last=False)
                        bring((product, l, t), qk_raw[:, a, :])
                    ps = BB.full(act, ("fv", l, t))
                    nc.scalar.activation(V_f[:, t, :, 0:FD], ps[:].rearrange("p (h d) -> p h d", d=FD), ACT.Copy)\
                        .then_inc(b_emptied["act"], 1)
                    yield s0 + 5 * t + 4
                    ps = BB.full(act, ("qkT", l, t, 0))
                    nc.scalar.activation(qT[:, :, t * P:(t + 1) * P], ps[:].rearrange("p (c q) -> p c q", q=P), ACT.Copy)\
                        .then_inc(b_emptied["act"], 1)
                    ps = BB.full(act, ("qkT", l, t, 1))
                    for a in range(2):
                        half = slice(64 * a, 64 * a + 64)
                        last = nc.scalar.activation(kT[half, :, a, t * P:(t + 1) * P],
                                                    ps[half, :].rearrange("p (c q) -> p c q", q=P), ACT.Copy)
                    last.then_inc(b_emptied["act"], 1)
                yield s0 + 40
                bring(("fmT", l), mT_f[0:2 * FH, :], rows=slice(0, 2 * FH))
                for c in range(FH // 2):
                    for k in range(NT):
                        yield s0 + 42 + 8 * c + 2 * k
                        nq = min(FKEYS, T - k * P)
                        if c:
                            act.wait_ge(*BB.made(("fav", l, c - 1, min(k + 1, NT - 1))))
                        bring(("fsecond", l, c, k), prob_b[:, k % PR_B, 0:2 * nq], ACT.Exp, cols=slice(0, 2 * nq), scale=QK_SCALE)
                    yield s0 + 51 + 8 * c
                    bring(("foT", l, c), oT_f[:, c, :])
                yield s0 + 79
                shifted(("fx", l))
                for c, (c0, n) in enumerate(HC):
                    yield s0 + 84 + 2 * c
                    if c:
                        act.wait_ge(*BB.brought(("fa", l, c - 1), "dve"))
                    nc.scalar.activation(gelu_f[0:n, :], BB.full(act, ("fg", l, c))[0:n, :], ACT.Gelu,
                                         bias=b1_s[0:n, l, 1, c:c + 1]).then_inc(b_emptied["act"], 1)
                if l + 1 < DEPTH:
                    yield s0 + 97
                    shifted(("fnext", l))
            yield 390
            act.wait_ge(f_x, 2 * DEPTH)
            nc.scalar.activation(mix_b[:], x_f[:].rearrange("p t e -> p (t e)"), ACT.Tanh, scale=0.5).then_inc(b_tanh, 1)

        def b_vector(dve):
            link = chain(dve, b_dve_step)
            emptied = b_emptied["dve"]
            yield 0
            dve.wait_ge(b_x, 1)
            layernorm(link, x_b, xn_b, stats_b, mv_b, rs_b, b_xn)
            yield 1
            dve.wait_ge(*BB.brought("xnT", "act"))
            link(nc.vector.tensor_reduce(out=psum_l[:, 0, :], in_=xnT_b[:].rearrange("p (l t) -> p l t", t=POOL), op=ALU.add,
                                         axis=AX.X))
            for a in range(2):
                last = nc.vector.tensor_scalar(pool_b[:, a, :], psum_l[:, 0, :], 1.0 / POOL, None, ALU.mult)
            last.then_inc(b_pool, 1)
            yield 2
            ps = BB.full(dve, "gqk")
            nc.vector.tensor_reduce(out=psum_l[64:P, 1, :], in_=ps[64:P, :].rearrange("p (l t) -> p l t", t=POOL), op=ALU.add,
                                    axis=AX.X).then_inc(emptied, 1)
            dve.wait_ge(*BB.brought("gqk", "dve"))
            nc.vector.memset(qkg_b[64:P, 2, NL:T], 0.0)
            link(nc.vector.tensor_scalar(qkg_b[64:P, 2, 0:NL], psum_l[64:P, 1, :], 1.0 / POOL, None, ALU.mult))
            yield 3
            dve.wait_ge(*BB.brought("gqk", "act"))
            split(link, qkg_b[:], res_b, [parts_b[:, :, c, :] for c in range(SPLIT)], b_split)
            dve.wait_ge(*BB.brought("gates", "act"))
            g2 = gate_b[:].rearrange("p t g h -> p (t g h)")
            nc.vector.tensor_scalar(g2, g2, 0.5, 0.5, ALU.mult, ALU.add).then_inc(b_gate, 1)

            def first_pass(g, n):
                _, _, t, hp = f = bfirst[g][n]
                nk = LKEYS - (WIN if t == 0 else 0)
                nc.vector.tensor_reduce(out=nmax_b[:, g, t, 2 * hp:2 * hp + 2],
                                        in_=BB.full(dve, f)[:, 0:2 * nk].rearrange("p (a k) -> p a k", a=2),
                                        op=ALU.max, axis=AX.X, negate=True).then_inc(emptied, 1)

            def max_parts(g):
                dve.wait_ge(*BB.brought(bfirst[g][-1], "dve"))
                split_max(link, nmax_b[:, g], mhi_b[:, g], [mparts_b[:, g, :, p, :] for p in range(2)], b_mparts)

            for n in range(8):
                yield 9 + n
                first_pass(0, n)
            yield 17
            max_parts(0)
            for t in range(NT):
                yield 18 + t / 4
                nc.vector.tensor_reduce(out=nmax_l[:, t, :], in_=BB.full(dve, ("lfirst", t))[:].rearrange("p (h l) -> p h l", l=NL),
                                        op=ALU.max, axis=AX.X, negate=True).then_inc(emptied, 1)
            yield 19
            dve.wait_ge(*BB.brought(("lfirst", NT - 1), "dve"))
            split_max(link, nmax_l[:], mhi_l[:], [mparts_l[:, :, p, :] for p in range(2)], b_lmparts)
            for g in range(G):
                for n in range(8):
                    yield 22 + 12 * g + n
                    if g + 1 < G:
                        first_pass(g + 1, n)
                yield 30 + 12 * g
                if g + 1 < G:
                    max_parts(g + 1)
                yield 31 + 12 * g
                ps = BB.full(dve, ("oT", g))[:].rearrange("p (t j c) -> p t j c", t=NT, c=32)
                rden = rden_b[:, 0:4 * NT].rearrange("p (t j) -> p t j", j=4)
                link(nc.vector.reciprocal(rden, ps[:, :, :, D0]))
                nc.vector.tensor_tensor(loc_b[:, :, 32 * g:32 * g + 32].rearrange("p t (j d) -> p t j d", d=D0),
                                        ps[:, :, :, 0:D0], rden.unsqueeze(3).to_broadcast([P, NT, 4, D0]),
                                        ALU.mult).then_inc(emptied, 1)
                dve.wait_ge(*BB.brought(("oT", g), "dve"))
            yield 77
            ps = BB.full(dve, "loT")[:].rearrange("p (n s) -> p n s", s=16)
            link(nc.vector.reciprocal(rden_b[:], ps[:, :, D0]))
            nc.vector.tensor_tensor(rem_b[:].rearrange("p t (h d) -> p (t h) d", d=D0), ps[:, :, 0:D0],
                                    rden_b[:].unsqueeze(2).to_broadcast([P, NT * LH, D0]), ALU.mult).then_inc(emptied, 1)
            yield 79
            dve.wait_ge(b_gate, 1)
            heads = "p t (h d) -> p t h d"

            def gate(g):
                return gate_b[:, :, g, :].unsqueeze(3).to_broadcast([P, NT, H0, D0])

            loc = loc_b[:].rearrange(heads, d=D0)
            link(nc.vector.tensor_tensor(loc, loc, gate(0), ALU.mult))
            nc.vector.tensor_tensor(mix_b[:].rearrange("p (t h d) -> p t h d", t=NT, d=D0),
                                    BB.full(dve, "rproj")[:].rearrange("p (t h d) -> p t h d", t=NT, d=D0),
                                    gate(1), ALU.mult).then_inc(emptied, 1)
            dve.wait_ge(*BB.brought("rproj", "dve"))
            nc.vector.tensor_tensor(mix_b[:], mix_b[:], loc_b[:].rearrange("p t e -> p (t e)"), ALU.add).then_inc(b_mix, 1)

            flat = "p t e -> p (t e)"
            for l in range(DEPTH):
                s0 = 88 + 150 * l
                for t in range(NT):
                    yield s0 + 5 * t
                    n = NT * l + t
                    if n:
                        dve.wait_ge(*BB.made(("qkT", (n - 1) // NT, (n - 1) % NT, 1)))
                    for a, product in enumerate(("fq", "fk")):
                        dve.wait_ge(*BB.brought((product, l, t), "act"))
                        nc.vector.tensor_tensor(cosp[:, a, :].rearrange("p (h d) -> p h d", d=FD),
                                                qk_raw[:, a, :].rearrange("p (h d) -> p h d", d=FD),
                                                rotf[:, l, 2 * a, t, :].unsqueeze(1).to_broadcast([P, FH, FD]), ALU.mult)
                    link_sq = nc.vector.tensor_reduce(out=ss[:], in_=sq.rearrange("p a (h d) -> p a h d", d=FD), op=ALU.add, axis=AX.X)
                    link_sq.then_inc(f_sq, 1)
                    dve.wait_ge(f_sq, n + 1)
                    yield s0 + 5 * t + 2
                    v = rn[:, 0, :]
                    link(nc.vector.tensor_scalar(v, ss[:].rearrange("p a h -> p (a h)"), 1e-24, None, ALU.max))
                    rsqrt(link, v, rn[:, 1, :], rn[:, 2, :])
                    dve.wait_ge(f_sin, n + 1)
                    link(nc.vector.tensor_tensor(cosp, cosp, sq, ALU.add))
                    nc.vector.tensor_tensor(qk_rot.rearrange("p a (h d) -> p (a h) d", d=FD), cosp.rearrange("p a (h d) -> p (a h) d", d=FD),
                                            rn[:, 1, :].unsqueeze(2).to_broadcast([P, 2 * FH, FD]), ALU.mult).then_inc(f_rot, 1)
                    dve.wait_ge(f_rot, n + 1)
                for t in range(NT):
                    for c in range(FH // 2):
                        yield s0 + 22 + 4 * t + c
                        nk = FKEYS - (FW if t == 0 else 0)
                        nc.vector.tensor_reduce(out=nmax_f[:, t, 2 * c:2 * c + 2],
                                                in_=BB.full(dve, ("ffirst", l, t, c))[:, 0:2 * nk].rearrange("p (a k) -> p a k", a=2),
                                                op=ALU.max, axis=AX.X, negate=True).then_inc(emptied, 1)
                yield s0 + 38
                dve.wait_ge(*BB.brought(("ffirst", l, NT - 1, FH // 2 - 1), "dve"))
                split_max(link, nmax_f[:], mhi_f[:], [mparts_f[:, :, p, :] for p in range(2)], f_mparts)
                for c in range(FH // 2):
                    for k in range(NT):
                        yield s0 + 43 + 8 * c + 2 * k
                        ps = BB.full(dve, ("fav", l, c, k))[:, 0:2 * (FD + 1)].rearrange("p (a d) -> p a d", a=2)
                        if c >= 2 and k == 0:
                            dve.wait_ge(*BB.made(("foT", l, c - 2)))
                        link(nc.vector.reciprocal(rden_f[:], ps[:, :, FD]))
                        nc.vector.tensor_tensor(otok_f[:, c % 2, k, :].rearrange("p (a d) -> p a d", a=2), ps[:, :, 0:FD],
                                                rden_f[:].unsqueeze(2).to_broadcast([P, 2, FD]), ALU.mult).then_inc(emptied, 1)
                        dve.wait_ge(*BB.brought(("fav", l, c, k), "dve"))
                yield s0 + 77
                x_in_l = xn_b if l == 0 else x_f
                nc.vector.tensor_tensor(x_f[:].rearrange(flat), BB.full(dve, ("fwo", l))[:], x_in_l[:].rearrange(flat),
                                        ALU.add).then_inc(emptied, 1)
                yield s0 + 81
                ps = BB.full(dve, ("fback", l))
                layernorm(link, ps[:].rearrange("p (t e) -> p t e", e=E), xn_b, stats_b, mv_b, rs_b, emptied)
                yield s0 + 83
                nc.vector.tensor_scalar(xnT_b[:], BB.full(dve, ("fnT", l))[:], lng_s[:, l:l + 1], lnb_s[:, l:l + 1],
                                        ALU.mult, ALU.add).then_inc(emptied, 1)
                for c, (c0, n) in enumerate(HC):
                    yield s0 + 85 + 2 * c
                    dve.wait_ge(*BB.brought(("fg", l, c), "act"))
                    nc.vector.scalar_tensor_tensor(out=u_f[0:n, c, :], in0=BB.full(dve, ("fa", l, c))[0:n, :],
                                                   scalar=b1_s[0:n, l, 0, c:c + 1], in1=gelu_f[0:n, :],
                                                   op0=ALU.add, op1=ALU.mult).then_inc(emptied, 1)
                yield s0 + 93
                nc.vector.tensor_tensor(x_f[:].rearrange(flat), BB.full(dve, ("fw2", l))[:], x_f[:].rearrange(flat),
                                        ALU.add).then_inc(emptied, 1)
                dve.wait_ge(*BB.brought(("fw2", l), "dve"))
                nc.vector.tensor_tensor(x_f[:], x_f[:], b2_s[:, l, :].unsqueeze(1).to_broadcast([P, NT, E]), ALU.add)\
                    .then_inc(f_x, 2)
            yield 391
            dve.wait_ge(b_tanh, 1)
            dve.wait_ge(f_x, 2 * DEPTH)
            link(nc.vector.scalar_tensor_tensor(out=mix_b[:], in0=mix_b[:], scalar=1.0, in1=x_f[:].rearrange(flat),
                                                op0=ALU.add, op1=ALU.mult))
            dve.wait_ge(*BB.brought("wout", "act"))
            link(nc.vector.tensor_tensor(mix_b[:], mix_b[:], s_b[:], ALU.mult))
            nc.vector.scalar_tensor_tensor(out=x_f[:].rearrange(flat), in0=mix_b[:], scalar=0.5, in1=x_b[:].rearrange(flat),
                                           op0=ALU.mult, op1=ALU.add).then_inc(b_out, 1)


        lo, hi = min(s.num for s in sems), max(s.num for s in sems)

        def clear_all():
            nc.multi_engine_barrier(list(nc.engines), sems_to_clear=range(lo, hi + 1))

        def iteration(row_a, row_b):
            with nc.Block() as block:
                @block.sync
                def _(sp):
                    merge(*([a_sync(sp, row_a)] if row_a is not None else []), *([b_sync(sp, row_b)] if row_b is not None else []))

                @block.gpsimd
                def _(pool):
                    merge(*([b_gpsimd(pool)] if row_b is not None else []))

                @block.tensor
                def _(pe):
                    merge(*([a_tensor(pe)] if row_a is not None else []), *([b_tensor(pe)] if row_b is not None else []))

                @block.scalar
                def _(act):
                    merge(*([a_scalar(act)] if row_a is not None else []), *([b_scalar(act)] if row_b is not None else []))

                @block.vector
                def _(dve):
                    merge(*([a_vector(dve, row_b is not None)] if row_a is not None else []), *([b_vector(dve)] if row_b is not None else []))
            clear_all()

        clear_all()
        iteration(bass.ds(0, 1), None)
        with nc.Fori(1, B) as b:
            iteration(bass.ds(b, 1), bass.ds(b - 1, 1))
        iteration(None, bass.ds(B - 1, 1))


_SAME = {"att_w": "L0_attn_w_att_val", "wv0_b": "L0_attn_wv_b", "wo0_b": "L0_attn_out_b", "W1": "L0_ffn_W1",
         "W2": "L0_ffn_W2", "Wg": "L0_ffn_Wg", "bg": "L0_ffn_bg", "wq": "L1_attn_wq", "wk": "L1_attn_wk",
         "wv": "L1_attn_wv", "wgv": "L1_attn_wgv", "r_out": "L1_attn_r_out_w", "gate_l": "L1_attn_gate_local_w",
         "gate_r": "L1_attn_gate_remote_w", "w_out": "L1_attn_w_out", "wqkv": "L1_ffn_wqkv",
         "q_sc": "L1_ffn_q_scale", "k_sc": "L1_ffn_k_scale", "wo": "L1_ffn_wo", "ln_g": "L1_ffn_ln_g",
         "ln_b": "L1_ffn_ln_b", "w1": "L1_ffn_w1", "b1": "L1_ffn_b1", "w2": "L1_ffn_w2", "b2": "L1_ffn_b2"}


def kernel(**inputs):
    import concourse.bacc as bacc
    from concourse.bass_utils import run_bass_kernel_spmd

    a = {n: np.asarray(v) for n, v in inputs.items()}
    laid = {"x_in": a["L0_attn_x"], "wv0T": a["L0_attn_wv_w"].T, "wo0T": a["L0_attn_out_w"].T,
            "wgqk": np.concatenate([a["L1_attn_wgq"], a["L1_attn_wgk"]], axis=1)}
    laid |= {n: a[full] for n, full in _SAME.items()}
    consts = shape_constants()

    nc = bacc.Bacc("TRN2", target_bir_lowering=False, num_devices=1)
    arrays = {}

    def dram(name, array):
        arrays[name] = np.ascontiguousarray(array)
        return nc.dram_tensor(name, array.shape, mybir.dt.from_np(array.dtype), kind="ExternalInput").ap()

    aps = {n: dram(f"in_{n}", v) for n, v in laid.items()}
    const_aps = {n: dram(f"const_{n}", v) for n, v in consts.items()}
    out = nc.dram_tensor("out_0", (B, T, E), F32, kind="ExternalOutput").ap()
    mixer_kernel(nc, **aps, consts=const_aps, out=out)
    r = run_bass_kernel_spmd(nc, [arrays], core_ids=[0])
    return r.results[0]["out_0"]
```

```python
from contextlib import ExitStack

import numpy as np

import concourse.bass as bass
from concourse import mybir

ALU = mybir.AluOpType
ACT = mybir.ActivationFunctionType
AX = mybir.AxisListType
F32 = mybir.dt.float32
BF16 = mybir.dt.bfloat16
I32 = mybir.dt.int32

P = 128
B, T, E = 16, 512, 128
NT = T // P
H0, D0 = 16, 8
NX, HX = 8, 512
XC = HX // P
WIN = 32
LH, NL = 8, 64
POOL = T // NL
FH, FD, FW = 8, 64, 64
INNER = FH * FD
HID = int(E * 4 * 2 / 3)
HC = [(c, min(P, HID - c)) for c in range(0, HID, P)]
DEPTH = 2
UNITS = FH // 2 * NT
SPLIT = 3
STACK = SPLIT * SPLIT * D0
ROWS = STACK + 2
G = H0 // 4
LKEYS = P + WIN
FKEYS = P + FW
EPS = 1e-5
MASKED = -1e30

A_FIRST, A_MAX, A_PROJ, A_END = 26, 39, 170, 232
A_GROUP = (42, 64, 122, 146)
A_EXPERT = (88, 95, 102, 109, 198, 205, 212, 219)
LAYER, LAYER_AT = 110, 88
UNIT = 1.8
HEAD_SCALE = float(D0) ** -0.5
QK_SCALE = 8.0
RSQRT_MAGIC = float(0x5F3759DF)


def shape_constants():
    bf = mybir.dt.np(BF16)
    c = {"ident": np.eye(P, dtype=np.float32), "ident_bf": np.eye(P, dtype=np.float32).astype(bf)}
    c["ones_bf"] = np.ones((2, 8 * T), np.float32).astype(bf)
    q, k = np.arange(P)[:, None], np.arange(LKEYS)[None, :] - WIN
    c["win_q"] = np.where((k > q - WIN) & (k <= q), 0.0, MASKED)
    k, q = np.arange(P)[:, None], np.arange(LKEYS)[None, :]
    c["win_k"] = np.where((k > q - WIN) & (k <= q), 0.0, MASKED)
    q, k = np.arange(P)[:, None], np.arange(FKEYS)[None, :] - FW
    c["band_q"] = np.where((k >= q - FW) & (k <= q), 0.0, MASKED)
    k, q = np.arange(P)[:, None], np.arange(FKEYS)[None, :]
    c["band_k"] = np.where((k >= q - FW) & (k <= q), 0.0, MASKED)
    t = np.arange(T).reshape(NT, P).T[:, :, None]
    lat = np.arange(NL)
    c["lat_q"] = np.where(lat[None, None, :] <= t // POOL, 0.0, MASKED).reshape(P, NT * NL)
    c["lat_k"] = np.where((np.arange(P) % NL)[:, None] <= np.arange(T)[None, :] // POOL, 0.0, MASKED)
    for n in ("win_q", "win_k", "band_q", "band_k", "lat_q", "lat_k"):
        c[n] = c[n].astype(np.float32).astype(bf)
    c["blocks"] = np.kron(np.eye(H0), np.ones((D0, 1))).astype(np.float32)
    sel = np.zeros((P, FH, P), np.float32)
    for h in range(FH):
        sel[[h, FH + h], h, :] = 1.0
    c["pick"] = sel.reshape(P, FH * P).astype(bf)
    half = np.arange(0, FD, 2, dtype=np.float32)
    freq = np.arange(T, dtype=np.float32)[:, None] * (1.0 / 10000.0 ** (half / FD)).astype(np.float32)
    freq = np.concatenate([freq, freq], axis=1)
    base = (half + 0.4 * FD) / (1.4 * FD)
    scale = base[None, :] ** ((np.arange(T) - T // 2) / float(FW // 2))[:, None]
    scale = np.concatenate([scale, scale], axis=1)
    sign = np.where(np.arange(FD) < FD // 2, -1.0, 1.0)
    rot = np.stack([np.cos(freq) * scale, np.sin(freq) * scale * sign,
                    np.cos(freq) / scale, np.sin(freq) / scale * sign])
    c["rotary"] = rot.reshape(4, NT, P, FD).transpose(2, 0, 1, 3).reshape(P, 4 * T // P * FD).astype(np.float32)
    return {n: np.ascontiguousarray(a) for n, a in c.items()}


class Banks:

    def __init__(self, tiles, filled, emptied, plan):
        self.tiles, self.filled, self.emptied = tiles, filled, emptied
        self.number, self.outs = {}, {}
        count = dict.fromkeys(emptied, 0)
        self.plan = [product for product, _ in plan]
        for n, (product, engines) in enumerate(plan):
            assert product not in self.number, product
            self.number[product] = n
            for e in engines:
                count[e] += 1
            self.outs[product] = {e: (emptied[e], count[e]) for e in engines}

    def bank(self, product):
        return self.tiles[self.number[product] % len(self.tiles)]

    def made(self, product):
        return self.filled, self.number[product] + 1

    def brought(self, product, engine):
        return self.outs[product][engine]

    def take(self, pe, product):
        n = self.number[product] - len(self.tiles)
        for semaphore, value in self.outs[self.plan[n]].values() if n >= 0 else ():
            pe.wait_ge(semaphore, value)
        return self.bank(product)

    def full(self, eng, product):
        eng.wait_ge(*self.made(product))
        return self.bank(product)


def merge(*streams):
    heads = [next(s, None) for s in streams]
    while any(h is not None for h in heads):
        n = min((h, i) for i, h in enumerate(heads) if h is not None)[1]
        heads[n] = next(streams[n], None)


def mixer_kernel(nc, x_in, att_w, wv0T, wv0_b, wo0T, wo0_b, W1, W2, Wg, bg, wq, wk, wv, wgqk, wgv,
                 r_out, gate_l, gate_r, w_out, wqkv, q_sc, k_sc, wo, ln_g, ln_b, w1, b1, w2, b2,
                 consts, out):
    ctx = ExitStack()
    with ctx:
        def sb(name, shape, dt=F32):
            return ctx.enter_context(nc.sbuf_tensor(name, shape, dt))

        sems = []

        def sem(name):
            sems.append(ctx.enter_context(nc.semaphore(name)))
            return sems[-1]

        banks = [ctx.enter_context(nc.psum_tensor(f"bank{i}", [P, T], F32)) for i in range(8)]

        ident, ident_bf = sb("ident", [P, P]), sb("ident_bf", [P, P], BF16)
        win_q, win_k = sb("win_q", [P, LKEYS], BF16), sb("win_k", [P, LKEYS], BF16)
        band_q, band_k = sb("band_q", [P, FKEYS], BF16), sb("band_k", [P, FKEYS], BF16)
        lat_q, lat_k = sb("lat_q", [P, NT, NL], BF16), sb("lat_k", [P, T], BF16)
        blocks, pick = sb("blocks", [P, H0]), sb("pick", [P, FH, P], BF16)
        att_c, attW = sb("att_c", [P, D0]), sb("attW", [P, E])
        wv0_s, wo0_s = sb("wv0_s", [P, E]), sb("wo0_s", [P, E])
        bv0, bo0 = sb("bv0", [P, E]), sb("bo0", [P, E])
        Wg_s, bg_s = sb("Wg_s", [P, NX]), sb("bg_s", [P, NX])
        wq_s, wk_s, wv_s, w_out_s = (sb(n, [P, E]) for n in ("wq_s", "wk_s", "wv_s", "w_out_s"))
        wgqk_s, wgv_s, r_out_s = sb("wgqk_s", [P, E]), sb("wgv_s", [P, NL]), sb("r_out_s", [NL, E])
        gcol, gateW = sb("gcol", [P, 2]), sb("gateW", [P, 2, H0])
        wqkv_s, wo_s = sb("wqkv_s", [P, DEPTH, 3 * INNER]), sb("wo_s", [P, DEPTH, INNER // P, E])
        w1_s, w2_s = sb("w1_s", [P, DEPTH, 2 * HID]), sb("w2_s", [P, DEPTH, len(HC), E])
        b1_s, b2_s = sb("b1_s", [P, DEPTH, 2, len(HC)]), sb("b2_s", [P, DEPTH, E])
        lng_s, lnb_s = sb("lng_s", [P, DEPTH]), sb("lnb_s", [P, DEPTH])
        qks = sb("qks", [P, DEPTH, 2, FD])
        rotf = sb("rotf", [P, DEPTH, 4, NT, FD])

        x_a, x1_a, xn_a = sb("x_a", [P, NT, E]), sb("x1_a", [P, NT, E]), sb("xn_a", [P, NT, E])
        stats_a, mv_a, rs_a = sb("stats_a", [P, NT, 6]), sb("mv_a", [P, NT, 2]), sb("rs_a", [P, 4, NT])
        kq_a = sb("kq_a", [P, 2, T])
        RING = 2
        Kst_a, Qst_a = sb("Kst_a", [ROWS, RING, 4, T], BF16), sb("Qst_a", [ROWS, RING, 4, T], BF16)
        V_a = sb("V_a", [P, NT, H0, D0 + 1])
        nmax_a, mparts_a = sb("nmax_a", [P, G, NT, 4]), sb("mparts_a", [P, G, NT, 2, 4])
        mhi_a, mT_a = sb("mhi_a", [P, G, NT, 4], BF16), sb("mT_a", [8, 2, T], BF16)
        PR_A = 8
        prob_a = sb("prob_a", [P, PR_A, T])
        res_a = prob_a[:, 0:2, :]
        parts_a = prob_a[:, 2:5, :].rearrange("p a t -> p (a t)").bitcast(BF16).rearrange("p (w c t) -> p w c t", w=2, t=T)
        og_a, rden_a = sb("og_a", [P, T]), sb("rden_a", [P, NT, 4])
        otok_a, oT_a, s_a = xn_a, sb("oT_a", [P, T]), sb("s_a", [P, T])
        lg_a, hot_a, sc_a = sb("lg_a", [P, NT, NX]), sb("hot_a", [P, NT, NX]), sb("sc_a", [P, NT, NX])
        before_a, mx_a = sb("before_a", [P, NT, NX]), sb("mx_a", [P, NT])
        hid_a = prob_a[:, 0:XC, :]
        y_a, th_a = sb("y_a", [P, T]), oT_a
        W1_s, W2_s = sb("W1_s", [P, 2, HX]), sb("W2_s", [P, 2, XC, E])

        x_b, xn_b, x_f = sb("x_b", [P, NT, E]), sb("xn_b", [P, NT, E]), sb("x_f", [P, NT, E])
        stats_b, mv_b, rs_b = sb("stats_b", [P, NT, 6]), sb("mv_b", [P, NT, 2]), sb("rs_b", [P, 4, NT])
        xnT_b, hT = sb("xnT_b", [P, T]), sb("hT", [P, T])
        pool_b, psum_l = sb("pool_b", [P, 2, NL]), sb("psum_l", [P, 2, NL])
        V_b, V_l = sb("V_b", [P, NT, H0, D0 + 1]), sb("V_l", [P, 4, 32])
        nmax_b, mparts_b = sb("nmax_b", [P, G, NT, 4]), sb("mparts_b", [P, G, NT, 2, 4])
        mhi_b, mT_b = sb("mhi_b", [P, G, NT, 4], BF16), sb("mT_b", [8, 2, T], BF16)
        nmax_l, mhi_l = sb("nmax_l", [P, NT, LH]), sb("mhi_l", [P, NT, LH], BF16)
        mparts_l, mT_l = sb("mparts_l", [P, NT, 2, LH]), sb("mT_l", [2 * LH, T], BF16)
        PR_B = 4
        prob_b = sb("prob_b", [P, PR_B, T])
        res_b = prob_b[:, 0:3, :]
        og_b, rden_b = sb("og_b", [P, T]), sb("rden_b", [P, 32])
        loc_b, rem_b = sb("loc_b", [P, NT, E]), sb("rem_b", [P, NT, NL])
        gate_b = sb("gate_b", [P, NT, 2, H0])
        mix_b, s_b = sb("mix_b", [P, T]), sb("s_b", [P, T])
        kT = sb("kT", [P, FH // 2, 2, T])
        V_f = sb("V_f", [P, NT, FH, FD + 1])
        ss, rn = sb("ss", [P, 2, FH]), sb("rn", [P, 2, 3, 2 * FH])
        nmax_f, mhi_f = sb("nmax_f", [P, NT, FH]), sb("mhi_f", [P, NT, FH], BF16)
        mparts_f, mT_f = sb("mparts_f", [P, NT, 2, FH]), sb("mT_f", [P, T], BF16)
        rden_f = sb("rden_f", [P, 2, 2])
        AREA = RING * 4 * T + LH * (T + NL) // 2 + 3 * T
        area, used = sb("area", [P, AREA]), [0]

        def take_area(words, rows=P):
            used[0] += words
            assert used[0] <= AREA, used
            return area[0:rows, used[0] - words:used[0]]

        Kst_b, Qst_b = (take_area(RING * 4 * T // 2, ROWS).bitcast(BF16).rearrange("p (r h t) -> p r h t", r=RING, t=T)
                        for _ in range(2))
        Qst_l = take_area(LH * T // 2, ROWS).bitcast(BF16).rearrange("p (h t) -> p h t", t=T)
        Kst_l = take_area(LH * NL // 2, ROWS).bitcast(BF16).rearrange("p (h t) -> p h t", t=NL)
        assert 3 * SPLIT * T // 2 <= used[0]
        parts_b = area[:, 0:3 * SPLIT * T // 2].bitcast(BF16).rearrange("p (w c t) -> p w c t", w=3, t=T)
        qkg_b = take_area(3 * T).rearrange("p (w t) -> p w t", t=T)
        used[0] = 0
        qk_raw, sq = (take_area(4 * INNER).rearrange("p (b a n) -> p b a n", b=2, a=2) for _ in range(2))
        cosp = prob_b[:].rearrange("p r t -> p (r t)").rearrange("p (b a n) -> p b a n", b=2, a=2)
        qT = take_area(FH // 2 * T).rearrange("p (c t) -> p c t", t=T)
        used[0] = 0
        oT_f = take_area(INNER // P * T).rearrange("p (c t) -> p c t", t=T)
        gelu_f, u_f = take_area(T), take_area(len(HC) * T).rearrange("p (c t) -> p c t", t=T)
        otok_f = sb("otok_f", [P, 2, NT, P])
        qk_rot = otok_f[:].rearrange("p c t d -> p (c t d)").rearrange("p (a n) -> p a n", a=2)

        def scratch(name, shape):
            return nc.dram_tensor(name, shape, BF16, kind="Internal").ap()

        dq_a, dk_a, dm_a = scratch("dq_a", [SPLIT, P, SPLIT, T]), scratch("dk_a", [P, SPLIT, T]), scratch("dm_a", [G, 8, T])
        dq_b, dk_b, dm_b = scratch("dq_b", [SPLIT, P, SPLIT, T]), scratch("dk_b", [P, SPLIT, T]), scratch("dm_b", [G, 8, T])
        dq_l, dk_l, dm_l = scratch("dq_l", [SPLIT, 64, SPLIT, T]), scratch("dk_l", [64, SPLIT, NL]), scratch("dm_l", [16, T])

        acc_a, acc_b = banks[3], banks[7]

        s_weights, s_setup, s_zeroed = sem("weights"), sem("setup"), sem("zeroed")
        rotary = prob_a[:, 0:2, :].rearrange("p a t -> p (a t)").rearrange("p (a t d) -> p a t d", a=4, d=FD)
        with nc.Block() as block:
            @block.sync
            def _(sp):
                loads = [(ident[:], consts["ident"]), (ident_bf[:], consts["ident_bf"]),
                         (win_q[:], consts["win_q"]), (win_k[:], consts["win_k"]),
                         (band_q[:], consts["band_q"]), (band_k[:], consts["band_k"]),
                         (lat_q[:], consts["lat_q"].rearrange("p (t l) -> p t l", l=NL)), (lat_k[:], consts["lat_k"]),
                         (blocks[:], consts["blocks"]), (pick[:], consts["pick"].rearrange("p (h k) -> p h k", k=P)),
                         (rotary, consts["rotary"].rearrange("p (a t d) -> p a t d", a=4, d=FD)),
                         (att_c[:], att_w.rearrange("h d e -> (h d) e")), (wv0_s[:], wv0T), (wo0_s[:], wo0T),
                         (bv0[:], wv0_b.partition_broadcast(P)), (bo0[:], wo0_b.partition_broadcast(P)),
                         (Wg_s[:], Wg), (bg_s[:], bg.partition_broadcast(P)),
                         (wq_s[:], wq), (wk_s[:], wk), (wv_s[:], wv), (w_out_s[:], w_out),
                         (wgqk_s[:], wgqk), (wgv_s[:], wgv), (r_out_s[:], r_out),
                         (gcol[:, 0:1], gate_l.rearrange("h (d o) -> (h d) o", o=1)),
                         (gcol[:, 1:2], gate_r.rearrange("h (d o) -> (h d) o", o=1)),
                         (wqkv_s[:], wqkv.rearrange("l d n -> d l n")),
                         (wo_s[:], wo.rearrange("l (c p) d -> p l c d", p=P)),
                         (w1_s[:], w1.rearrange("l d n -> d l n")),
                         (Kst_a[STACK:ROWS, :, :, :].rearrange("p r h t -> p (r h t)"), consts["ones_bf"])]
                for l in range(DEPTH):
                    loads += [(dst[:, l:l + 1], src[l, :].rearrange("(d o) -> d o", o=1)) for dst, src in ((lng_s, ln_g), (lnb_s, ln_b))]
                    loads += [(b2_s[:, l, :], b2[l, :].partition_broadcast(P)),
                              (qks[:, l, 0, :], q_sc[l, :].partition_broadcast(P)),
                              (qks[:, l, 1, :], k_sc[l, :].partition_broadcast(P))]
                    for c, (c0, n) in enumerate(HC):
                        loads += [(w2_s[0:n, l, c, :], w2[l, c0:c0 + n, :])]
                        loads += [(b1_s[0:n, l, half, c:c + 1],
                                   b1[l, half * HID + c0:half * HID + c0 + n].rearrange("(p o) -> p o", o=1))
                                  for half in range(2)]
                for dst, src in loads:
                    sp.dma_start(dst, src).then_inc(s_weights, 16)
                sp.wait_ge(s_weights, 16 * len(loads))
                sp.sem_inc(s_setup, 1)

            @block.vector
            def _(dve):
                nc.vector.memset(acc_a[:], 0.0)
                nc.vector.memset(acc_b[:], 0.0)
                for tile in (V_l[:], kT[:], mT_f[:], hT[64:P, 0:1], x1_a[:]):
                    last = nc.vector.memset(tile, 0.0)
                for tile in (V_a[:, :, :, D0:D0 + 1], V_b[:, :, :, D0:D0 + 1], V_f[:, :, :, FD:FD + 1]):
                    last = nc.vector.memset(tile, 1.0)
                last.then_inc(s_zeroed, 1)
                dve.wait_ge(s_zeroed, 1)
                nc.vector.memset(V_l[0:64, :, D0:D0 + 1], 1.0)
                nc.vector.memset(V_l[64:P, :, 16 + D0:16 + D0 + 1], 1.0)
                dve.wait_ge(s_setup, 1)
                blk = blocks[:].unsqueeze(2).to_broadcast([P, H0, D0])
                nc.vector.tensor_tensor(attW[:].rearrange("p (h e) -> p h e", e=D0), blk,
                                        att_c[:].unsqueeze(1).to_broadcast([P, H0, D0]), ALU.mult)
                for g in range(2):
                    nc.vector.tensor_scalar(gateW[:, g, :], blocks[:], gcol[:, g:g + 1], None, ALU.mult)
                for l in range(DEPTH):
                    for a in range(2):
                        s = qks[:, l, a, :].unsqueeze(1)
                        nc.vector.tensor_tensor(rotf[:, l, 2 * a], rotary[:, 2 * a],
                                                s.to_broadcast([P, NT, FD]), ALU.mult)
                        for lo in (0, FD // 2):
                            hi = FD // 2 - lo
                            nc.vector.tensor_tensor(
                                rotf[:, l, 2 * a + 1, :, lo:lo + 32], rotary[:, 2 * a + 1, :, lo:lo + 32],
                                s[:, :, hi:hi + 32].to_broadcast([P, NT, 32]), ALU.mult)

        def engine_sems(p):
            return {e: sem(f"{p}_emptied_by_{e}") for e in ("act", "dve")}

        a_x_in, a_xn, a_split, a_spill = (sem(n) for n in ("a_x_in", "a_xn", "a_split", "a_spill"))
        a_stack = [sem(f"a_stack{g}") for g in range(G)]
        a_mparts, a_mspill, a_mrow = sem("a_mparts"), [sem(f"a_mspill{g}") for g in range(G)], [sem(f"a_mrow{g}") for g in range(G)]
        a_av, a_og, a_tanh, a_x1 = (sem(n) for n in ("a_av", "a_og", "a_tanh", "a_x1"))
        a_w = [sem("a_expert0"), sem("a_expert1")]
        a_filled, a_emptied = sem("a_filled"), engine_sems("a")
        a_dve_step = sem("a_dve_step")
        b_x, b_xn, b_pool, b_split, b_spill = (sem(n) for n in ("b_x", "b_xn", "b_pool", "b_split", "b_spill"))
        b_ones, b_lstack = sem("b_ones"), sem("b_lstack")
        b_stack = [sem(f"b_stack{g}") for g in range(G)]
        b_mparts, b_mspill, b_mrow = sem("b_mparts"), [sem(f"b_mspill{g}") for g in range(G)], [sem(f"b_mrow{g}") for g in range(G)]
        b_lmparts, b_lmspill, b_lmrow = sem("b_lmparts"), sem("b_lmspill"), sem("b_lmrow")
        b_av, b_og, b_gate, b_mix = (sem(n) for n in ("b_av", "b_og", "b_gate", "b_mix"))
        b_filled, b_emptied = sem("b_filled"), engine_sems("b")
        b_dve_step, b_pool_step = sem("b_dve_step"), sem("b_pool_step")
        f_sq, f_cos, f_turned, f_rot, f_mparts = (sem(n) for n in ("f_sq", "f_cos", "f_turned", "f_rot", "f_mparts"))
        f_x, f_norm, f_gelu = (sem(n) for n in ("f_x", "f_norm", "f_gelu"))
        b_tanh, b_out, b_stored = sem("b_tanh"), sem("b_out"), sem("b_stored")

        first = [[("first", g, j, t) for j in range(4) for t in range(NT)] for g in range(G)]
        second = [[("second", g, k, j) for k in range(NT) for j in range(4)] for g in range(G)]
        plan_a = [("xnT", ["act"]), ("xw", ["act"]), ("v", ["dve"]), ("logits", ["dve"])]
        plan_a += [(f, ["dve"]) for f in first[0]] + [(("mT", 0), ["act"])]

        def plan_experts(e0, e1):
            return sum(([(("hid", e, c), ["act"]) for c in range(XC)] + [(("y", e), ["dve"])] for e in range(e0, e1)), [])

        for g in range(G):
            if g == 2:
                plan_a += plan_experts(0, NX // 2)
            for n in range(16):
                if g + 1 < G:
                    plan_a.append((first[g + 1][n], ["dve"]))
                plan_a.append((second[g][n], ["act"]))
            if g + 1 < G:
                plan_a.append((("mT", g + 1), ["act"]))
            plan_a.append((("oT", g), ["dve"]))
        plan_a += [("otokT", ["act"]), ("proj", ["dve"])] + plan_experts(NX // 2, NX)
        bfirst = [[("first", g, t, h) for t in range(NT) for h in range(2)] for g in range(G)]
        bsecond = [[("second", g, k, h) for k in range(NT) for h in range(2)] for g in range(G)]
        plan_b = [("xnT", ["act"]), ("q", ["act"]), ("k", ["act"]), ("gqk", ["act", "dve"]),
                  ("v", ["act"]), ("gv", ["act"]), ("gates", ["act"])]
        plan_b += [(f, ["dve"]) for f in bfirst[0]] + [(("mT", 0), ["act"])]
        plan_b += [(("lfirst", t), ["dve"]) for t in range(NT)] + [("lmT", ["act"])]
        for g in range(G):
            for n in range(8):
                if g + 1 < G:
                    plan_b.append((bfirst[g + 1][n], ["dve"]))
                plan_b.append((bsecond[g][n], ["act"]))
            if g + 1 < G:
                plan_b.append((("mT", g + 1), ["act"]))
            plan_b.append((("oT", g), ["dve"]))
        plan_b += [(("lsecond", u), ["act"]) for u in range(4)] + [("loT", ["dve"]), ("remT", ["act"])]
        plan_b += [("rproj", ["dve"]), ("mixT", ["act"]), ("wout", ["act"])]
        for l in range(DEPTH):
            for t in range(NT):
                plan_b += [(("fq", l, t), ["act"]), (("fk", l, t), ["act"]), (("fv", l, t), ["act"])]
                if t:
                    plan_b += [(("qkT", l, t - 1, a), ["act"]) for a in range(2)]
            plan_b += [(("qkT", l, NT - 1, a), ["act"]) for a in range(2)]
            plan_b += [(("ffirst", l, t, c), ["dve"]) for t in range(NT) for c in range(FH // 2)]
            plan_b += [(("fmT", l), ["act"])]
            for n in range(UNITS + 2):
                if n < UNITS:
                    plan_b.append((("fsecond", l, n), ["act"]))
                if n % NT == 1 and n > NT:
                    plan_b.append((("foT", l, n // NT - 1), ["act"]))
                if 0 < n <= UNITS:
                    plan_b.append((("fav", l, n - 1), ["dve"]))
            plan_b += [(("fwo", l), ["dve"])]
            plan_b += [(("fx", l), ["act"]), (("fback", l), ["dve"]), (("fnT", l), ["dve"])]
            for c in range(len(HC)):
                plan_b += [(("fg", l, c), ["act"]), (("fa", l, c), ["dve"])]
            plan_b += [(("fw2", l), ["dve"])]
            if l + 1 < DEPTH:
                plan_b += [(("fnext", l), ["act"])]
        BA = Banks(banks[0:3], a_filled, a_emptied, plan_a)
        BB = Banks(banks[4:7], b_filled, b_emptied, plan_b)

        def transposes(dst, src, n=E, inc=None):
            for t in range(NT):
                last = nc.tensor.transpose(dst[0:n, t * P:(t + 1) * P], src[:, t, :], ident[:])
            last.then_inc(inc, 1)

        def chain(eng, s):
            count = [0]

            def link(ins):
                count[0] += 1
                ins.then_inc(s, 1)
                eng.wait_ge(s, count[0])
            return link

        def rsqrt(link, v, y, t):
            link(nc.vector.tensor_scalar(y.bitcast(I32), v.bitcast(I32), 1, None, ALU.logical_shift_right))
            link(nc.vector.tensor_scalar(y.bitcast(I32), y.bitcast(I32), -1.0, RSQRT_MAGIC, ALU.mult, ALU.add))
            for _ in range(3):
                link(nc.vector.scalar_tensor_tensor(out=t, in0=v, scalar=-0.5, in1=y, op0=ALU.mult, op1=ALU.mult))
                link(nc.vector.tensor_tensor(t, t, y, ALU.mult))
                link(nc.vector.scalar_tensor_tensor(out=y, in0=t, scalar=1.5, in1=y, op0=ALU.add, op1=ALU.mult))

        def layernorm(link, src, dst, stats, mv, rs, inc):
            for t in range(NT):
                last = nc.vector.bn_stats(stats[:, t, :], src[:, t, :])
            link(last)
            for t in range(NT):
                last = nc.vector.bn_aggr(mv[:, t, :], stats[:, t, :])
            link(last)
            link(nc.vector.tensor_scalar(rs[:, 0, :], mv[:, :, 1], EPS, None, ALU.add))
            rsqrt(link, rs[:, 0, :], rs[:, 1, :], rs[:, 2, :])
            for t in range(NT):
                last = nc.vector.tensor_scalar(dst[:, t, :], src[:, t, :], mv[:, t, 0:1], rs[:, 1, t:t + 1],
                                               ALU.subtract, ALU.mult)
            last.then_inc(inc, 1)

        def split(link, src, res, parts, inc):
            link(nc.vector.tensor_copy(parts[0], src))
            link(nc.vector.tensor_tensor(res, src, parts[0], ALU.subtract))
            link(nc.vector.tensor_copy(parts[1], res))
            link(nc.vector.tensor_tensor(res, res, parts[1], ALU.subtract))
            nc.vector.tensor_copy(parts[2], res).then_inc(inc, 1)

        def split_max(link, nmax, mhi, parts, inc):
            link(nc.vector.tensor_copy(mhi, nmax))
            nc.vector.tensor_copy(parts[0], mhi)
            nc.vector.tensor_tensor(parts[1], nmax, mhi, ALU.subtract).then_inc(inc, 1)

        def spill(sp, parts_q, parts_k, dq, dk, s):
            for i in range(SPLIT):
                sp.dma_start(dq[i, :, 0:SPLIT - i, :], parts_q[:, i:SPLIT, :]).then_inc(s, 16)
                if i:
                    sp.dma_start(dq[i, :, SPLIT - i:SPLIT, :], parts_q[:, 0:i, :]).then_inc(s, 16)
            sp.dma_start(dk, parts_k).then_inc(s, 16)

        SPILLED, STACKED = 6 * 16, 6 * 16

        def load_stack(sp, dq, dk, h, n, Qst, Kst, s):
            for i in range(SPLIT):
                r = slice(i * SPLIT * D0, (i + 1) * SPLIT * D0)
                rows = slice(h * D0, (h + n) * D0)
                sp.dma_start(Qst[r, :, :], dq[i, rows].rearrange("(h d) c t -> (d c) h t", d=D0)).then_inc(s, 16)
                sp.dma_start(Kst[r, :, :], dk[rows].rearrange("(h d) c t -> (d c) h t", d=D0)).then_inc(s, 16)

        def max_to_stack(sp, mT, dm, Qst, spilled, landed):
            sp.dma_start(dm, mT).then_inc(spilled, 16)
            sp.wait_ge(spilled, 16)
            sp.dma_start(Qst[STACK:ROWS, :, :], dm.rearrange("(a h) t -> a h t", a=2)).then_inc(landed, 16)

        def a_sync(sp, b):
            yield 0
            sp.dma_start(x_a[:], x_in[b, :, :].rearrange("o (n p) f -> p (o n) f", p=P)).then_inc(a_x_in, 16)
            yield 4
            sp.wait_ge(a_split, 1)
            spill(sp, parts_a[:, 1], parts_a[:, 0], dq_a, dk_a, a_spill)
            sp.wait_ge(a_spill, SPILLED)

            def stack(g):
                load_stack(sp, dq_a, dk_a, 4 * g, 4, Qst_a[:, g % RING], Kst_a[:, g % RING], a_stack[g])

            for g in range(RING):
                stack(g)

            def experts(e0, e1):
                for e in range(e0, e1):
                    yield A_EXPERT[e] - 9
                    if e >= 2:
                        sp.wait_ge(*BA.made(("y", e - 2)))
                    sp.dma_start(W1_s[:, e % 2, :], W1[e]).then_inc(a_w[e % 2], 16)
                    sp.dma_start(W2_s[:, e % 2], W2[e].rearrange("(c p) d -> p c d", p=P)).then_inc(a_w[e % 2], 16)

            for g in range(G):
                if g == 2:
                    yield from experts(0, NX // 2)
                yield A_GROUP[g] - 1
                sp.wait_ge(*BA.brought(("mT", g), "act"))
                max_to_stack(sp, mT_a[:, g % 2, :], dm_a[g], Qst_a[:, g % RING], a_mspill[g], a_mrow[g])
                if g + RING < G:
                    yield A_GROUP[g] + 19
                    sp.wait_ge(*BA.made(second[g][-1]))
                    stack(g + RING)
            yield from experts(NX // 2, NX)

        def a_tensor(pe):
            yield 1
            pe.wait_ge(a_xn, 1)
            transposes(BA.take(pe, "xnT"), xn_a, inc=a_filled)
            yield 2
            pe.wait_ge(*BA.brought("xnT", "act"))
            nc.tensor.matmul(BA.take(pe, "xw")[:], attW[:], kq_a[:, 0, :], start=True, stop=True).then_inc(a_filled, 1)
            ps = BA.take(pe, "v")
            for t in range(NT):
                last = nc.tensor.matmul(ps[:, t * E:(t + 1) * E], kq_a[:, 0, t * P:(t + 1) * P], wv0_s[:], start=True, stop=True)
            last.then_inc(a_filled, 1)
            ps = BA.take(pe, "logits")
            for t in range(NT):
                last = nc.tensor.matmul(ps[:, t * NX:(t + 1) * NX], kq_a[:, 0, t * P:(t + 1) * P], Wg_s[:], start=True, stop=True)
            last.then_inc(a_filled, 1)

            def first_pass(g, n):
                _, _, j, t = f = first[g][n]
                if n == 0:
                    pe.wait_ge(a_stack[g], STACKED)
                nc.tensor.matmul(BA.take(pe, f)[:], Qst_a[0:STACK, g % RING, j, t * P:(t + 1) * P],
                                 Kst_a[0:STACK, g % RING, j, :], start=True, stop=True).then_inc(a_filled, 1)

            def max_rows(g):
                pe.wait_ge(a_mparts, g + 1)
                transposes(BA.take(pe, ("mT", g)), mparts_a[:, g].rearrange("p t a j -> p t (a j)"), 8, a_filled)

            def values(g, k):
                pe.wait_ge(*BA.brought(("second", g, k, 3), "act"))
                if k == 0:
                    if g == 0:
                        pe.wait_ge(*BA.brought("v", "dve"))
                    else:
                        pe.wait_ge(a_og, g)
                for j in range(4):
                    last = nc.tensor.matmul(acc_a[32 * j:32 * j + D0 + 1, :], V_a[:, k, 4 * g + j, :],
                                            prob_a[:, (4 * k + j) % PR_A, :], start=(k == 0), stop=(k == NT - 1))
                last.then_inc(a_av, 1)

            def experts(e0, e1):
                for e in range(e0, e1):
                    for c in range(XC):
                        yield A_EXPERT[e] + c
                        if c == 0:
                            pe.wait_ge(a_w[e % 2], 32 * (e // 2 + 1))
                        nc.tensor.matmul(BA.take(pe, ("hid", e, c))[:], W1_s[:, e % 2, c * P:(c + 1) * P], kq_a[:, 0, :],
                                         start=True, stop=True).then_inc(a_filled, 1)
                    yield A_EXPERT[e] + 5.5
                    pe.wait_ge(*BA.brought(("hid", e, XC - 1), "act"))
                    ps = BA.take(pe, ("y", e))
                    for t in range(NT):
                        for c in range(XC):
                            last = nc.tensor.matmul(ps[:, t * E:(t + 1) * E], hid_a[:, c, t * P:(t + 1) * P],
                                                    W2_s[:, e % 2, c, :], start=(c == 0), stop=(c == XC - 1))
                    last.then_inc(a_filled, 1)

            for n in range(16):
                yield A_FIRST + 0.7 * n
                first_pass(0, n)
            yield A_MAX
            max_rows(0)
            for g in range(G):
                if g == 2:
                    yield from experts(0, NX // 2)
                for n in range(16):
                    yield A_GROUP[g] + 1.2 * n
                    if g + 1 < G:
                        first_pass(g + 1, n)
                    if n == 0:
                        pe.wait_ge(a_mrow[g], 16)
                    _, _, k, j = s = second[g][n]
                    nc.tensor.matmul(BA.take(pe, s)[:], Kst_a[:, g % RING, j, k * P:(k + 1) * P], Qst_a[:, g % RING, j, :],
                                     start=True, stop=True).then_inc(a_filled, 1)
                    if n % 4 == 1 and n > 4:
                        values(g, n // 4 - 1)
                yield A_GROUP[g] + 20
                values(g, 3)
                if g + 1 < G:
                    max_rows(g + 1)
                yield A_GROUP[g] + 21
                pe.wait_ge(a_og, g + 1)
                transposes(BA.take(pe, ("oT", g)), og_a[:].rearrange("p (t q) -> p t q", q=P), inc=a_filled)
            yield A_PROJ
            pe.wait_ge(*BA.brought(("oT", G - 1), "dve"))
            transposes(BA.take(pe, "otokT"), otok_a, inc=a_filled)
            yield A_PROJ + 2
            pe.wait_ge(*BA.brought("otokT", "act"))
            ps = BA.take(pe, "proj")
            for t in range(NT):
                last = nc.tensor.matmul(ps[:, t * E:(t + 1) * E], oT_a[:, t * P:(t + 1) * P], wo0_s[:], start=True, stop=True)
            last.then_inc(a_filled, 1)
            yield from experts(NX // 2, NX)

        def a_scalar(act):
            def bring(product, dst, func=ACT.Copy, rows=P, **kw):
                nc.scalar.activation(dst, BA.full(act, product)[0:rows, :], func, **kw).then_inc(a_emptied["act"], 1)

            yield 1
            bring("xnT", kq_a[:, 0, :])
            yield 2
            bring("xw", kq_a[:, 1, :])
            def experts(e0, e1):
                for e in range(e0, e1):
                    for c in range(XC):
                        yield A_EXPERT[e] + c
                        if c == 0:
                            if e > e0:
                                act.wait_ge(*BA.made(("y", e - 1)))
                            else:
                                act.wait_ge(a_av, 4 * G * (e0 + 4) // NX)
                        bring(("hid", e, c), hid_a[:, c, :], ACT.Gelu_apprx_tanh)

            yield A_MAX + 1
            bring(("mT", 0), mT_a[:, 0, :], rows=8)
            for g in range(G):
                if g == 2:
                    yield from experts(0, NX // 2)
                    act.wait_ge(*BA.made(("y", NX // 2 - 1)))
                for n in range(16):
                    yield A_GROUP[g] + 1.2 * n
                    if n % 4 == 0 and 4 * g + n // 4 >= 2:
                        act.wait_ge(a_av, 4 * g + n // 4 - 1)
                    bring(second[g][n], prob_a[:, n % PR_A, :], ACT.Exp, scale=HEAD_SCALE)
                yield A_GROUP[g] + 20
                if g + 1 < G:
                    if g >= 1:
                        act.wait_ge(a_mspill[g - 1], 16)
                    bring(("mT", g + 1), mT_a[:, (g + 1) % 2, :], rows=8)
                act.wait_ge(a_av, 4 * g + 4)
                if g:
                    act.wait_ge(*BA.made(("oT", g - 1)))
                nc.scalar.activation(og_a[:], acc_a[:], ACT.Copy).then_inc(a_og, 1)
            yield A_PROJ
            bring("otokT", oT_a[:])
            yield from experts(NX // 2, NX)
            yield A_END
            act.wait_ge(*BA.made("proj"))
            act.wait_ge(*BA.brought(("y", NX - 1), "dve"))
            nc.scalar.activation(th_a[:], y_a[:], ACT.Tanh, scale=0.5).then_inc(a_tanh, 1)

        def a_vector(dve, beside_b):
            link = chain(dve, a_dve_step)
            emptied = a_emptied["dve"]
            yield 0
            dve.wait_ge(a_x_in, 16)
            layernorm(link, x_a, xn_a, stats_a, mv_a, rs_a, a_xn)
            yield 2
            ps = BA.full(dve, "v")
            nc.vector.tensor_tensor(V_a[:, :, :, 0:D0], ps[:].rearrange("p (t h d) -> p t h d", t=NT, d=D0),
                                    bv0[:].rearrange("p (h d) -> p h d", d=D0).unsqueeze(1)
                                    .to_broadcast([P, NT, H0, D0]), ALU.add).then_inc(emptied, 1)
            yield 3
            ps = BA.full(dve, "logits")
            nc.vector.tensor_tensor(lg_a[:], ps[:, 0:NT * NX].rearrange("p (t e) -> p t e", e=NX),
                                    bg_s[:].unsqueeze(1).to_broadcast([P, NT, NX]), ALU.add).then_inc(emptied, 1)
            dve.wait_ge(*BA.brought("logits", "dve"))
            link(nc.vector.tensor_reduce(out=mx_a[:], in_=lg_a[:], op=ALU.max, axis=AX.X))
            link(nc.vector.tensor_tensor(sc_a[:], lg_a[:], mx_a[:].unsqueeze(2).to_broadcast([P, NT, NX]), ALU.is_equal))
            link(nc.vector.memset(before_a[:, :, 0:1], 0.0))
            for e in range(1, NX):
                link(nc.vector.tensor_tensor(before_a[:, :, e:e + 1], before_a[:, :, e - 1:e], sc_a[:, :, e - 1:e], ALU.max))
            link(nc.vector.tensor_scalar(before_a[:], before_a[:], -1.0, 1.0, ALU.mult, ALU.add))
            link(nc.vector.tensor_tensor(hot_a[:], before_a[:], sc_a[:], ALU.mult))
            dve.wait_ge(*BA.brought("xw", "act"))
            split(link, kq_a[:], res_a, [parts_a[:, :, c, :] for c in range(SPLIT)], a_split)

            def first_pass(g, n):
                _, _, j, t = f = first[g][n]
                nc.vector.tensor_reduce(out=nmax_a[:, g, t, j:j + 1], in_=BA.full(dve, f)[:], op=ALU.max, axis=AX.X,
                                        negate=True).then_inc(emptied, 1)

            def max_parts(g):
                dve.wait_ge(*BA.brought(first[g][-1], "dve"))
                split_max(link, nmax_a[:, g], mhi_a[:, g], [mparts_a[:, g, :, p, :] for p in range(2)], a_mparts)

            def experts(e0, e1):
                for e in range(e0, e1):
                    yield A_EXPERT[e] + 6.5
                    ps = BA.full(dve, ("y", e))
                    if e:
                        dve.wait_ge(*BA.brought(("y", e - 1), "dve"))
                    for t in range(NT):
                        y, src, hot = y_a[:, t * E:(t + 1) * E], ps[:, t * E:(t + 1) * E], hot_a[:, t, e:e + 1]
                        if e == 0:
                            last = nc.vector.tensor_scalar(y, src, hot, None, ALU.mult)
                        else:
                            last = nc.vector.scalar_tensor_tensor(out=y, in0=src, scalar=hot, in1=y, op0=ALU.mult, op1=ALU.add)
                    last.then_inc(emptied, 1)

            for n in range(16):
                yield A_FIRST + 0.7 * n
                first_pass(0, n)
            yield A_MAX - 1
            max_parts(0)
            for g in range(G):
                if g == 2:
                    yield from experts(0, NX // 2)
                for n in range(16):
                    yield A_GROUP[g] + 1.2 * n
                    if g + 1 < G:
                        first_pass(g + 1, n)
                yield A_GROUP[g] + 19.5
                if g + 1 < G:
                    max_parts(g + 1)
                yield A_GROUP[g] + 21
                ps = BA.full(dve, ("oT", g))[:].rearrange("p (t j c) -> p t j c", t=NT, c=32)
                link(nc.vector.reciprocal(rden_a[:], ps[:, :, :, D0]))
                nc.vector.tensor_tensor(otok_a[:, :, 32 * g:32 * g + 32].rearrange("p t (j d) -> p t j d", d=D0),
                                        ps[:, :, :, 0:D0], rden_a[:].unsqueeze(3).to_broadcast([P, NT, 4, D0]),
                                        ALU.mult).then_inc(emptied, 1)
            yield A_PROJ + 3
            tiles = "p (t e) -> p t e"
            ps = BA.full(dve, "proj")
            nc.vector.tensor_tensor(s_a[:].rearrange(tiles, e=E), ps[:].rearrange(tiles, e=E),
                                    bo0[:].unsqueeze(1).to_broadcast([P, NT, E]), ALU.add).then_inc(emptied, 1)
            yield from experts(NX // 2, NX)
            yield A_END + 1
            dve.wait_ge(a_tanh, 1)
            link(nc.vector.scalar_tensor_tensor(out=th_a[:], in0=th_a[:], scalar=1.0, in1=y_a[:], op0=ALU.add, op1=ALU.mult))
            link(nc.vector.tensor_tensor(th_a[:], th_a[:], s_a[:], ALU.mult))
            if beside_b:
                dve.wait_ge(b_x, 1)
            nc.vector.scalar_tensor_tensor(out=x1_a[:].rearrange("p t e -> p (t e)"), in0=th_a[:], scalar=0.5,
                                           in1=x_a[:].rearrange("p t e -> p (t e)"), op0=ALU.mult, op1=ALU.add).then_inc(a_x1, 1)

        def b_sync(sp, b):
            yield 4
            sp.wait_ge(b_split, 1)
            spill(sp, parts_b[:, 0], parts_b[:, 1], dq_b, dk_b, b_spill)
            spill(sp, parts_b[0:64, 2], parts_b[64:P, 2, :, 0:NL], dq_l, dk_l, b_spill)
            sp.wait_ge(b_spill, 2 * SPILLED)
            sp.dma_start(Kst_b[STACK:ROWS].rearrange("p r h t -> p (r h t)"), consts["ones_bf"]).then_inc(b_ones, 16)
            sp.dma_start(Kst_l[STACK:ROWS].rearrange("p h t -> p (h t)"), consts["ones_bf"][:, 0:LH * NL]).then_inc(b_ones, 16)

            def stack(g):
                load_stack(sp, dq_b, dk_b, 4 * g, 4, Qst_b[:, g % RING], Kst_b[:, g % RING], b_stack[g])

            stack(0)
            load_stack(sp, dq_l, dk_l, 0, LH, Qst_l, Kst_l, b_lstack)
            stack(1)
            yield 20
            sp.wait_ge(*BB.brought(("mT", 0), "act"))
            max_to_stack(sp, mT_b[:, 0, :], dm_b[0], Qst_b[:, 0], b_mspill[0], b_mrow[0])
            sp.wait_ge(*BB.brought("lmT", "act"))
            max_to_stack(sp, mT_l[:], dm_l, Qst_l, b_lmspill, b_lmrow)
            for g in range(G):
                if g + 1 < G:
                    yield 32 + 12 * g
                    sp.wait_ge(*BB.made(bsecond[g][-1]))
                    if g + RING < G:
                        stack(g + RING)
                    sp.wait_ge(*BB.brought(("mT", g + 1), "act"))
                    max_to_stack(sp, mT_b[:, (g + 1) % 2, :], dm_b[g + 1], Qst_b[:, (g + 1) % RING], b_mspill[g + 1], b_mrow[g + 1])
            yield LAYER_AT + LAYER * DEPTH + 4
            sp.wait_ge(b_out, 1)
            sp.dma_start(out[b, :, :].rearrange("o (n p) f -> p (o n) f", p=P), x_f[:]).then_inc(b_stored, 16)
            sp.wait_ge(b_stored, 16)

        def b_gpsimd(pool):
            yield 0
            nc.gpsimd.tensor_copy(x_b[:], x1_a[:]).then_inc(b_x, 1)
            for l in range(DEPTH):
                for t in range(NT):
                    yield LAYER_AT + LAYER * l + 7 * t + 2
                    n = NT * l + t
                    pool.wait_ge(*BB.brought(("fk", l, t), "act"))
                    pool.wait_ge(f_sq, n + 1)
                    raw = qk_raw[:, t % 2].rearrange("p a (h d) -> p a h d", d=FD)
                    sin = sq[:, t % 2].rearrange("p a (h d) -> p a h d", d=FD)
                    for a in range(2):
                        for lo in (0, FD // 2):
                            hi = FD // 2 - lo
                            last = nc.gpsimd.tensor_tensor(
                                sin[:, a, :, lo:lo + 32], raw[:, a, :, hi:hi + 32],
                                rotf[:, l, 2 * a + 1, t, lo:lo + 32].unsqueeze(1).to_broadcast([P, FH, 32]), ALU.mult)
                    last.then_inc(b_pool_step, 1)
                    pool.wait_ge(b_pool_step, n + 1)
                    pool.wait_ge(f_cos, n + 1)
                    nc.gpsimd.tensor_tensor(cosp[:, t % 2], cosp[:, t % 2], sq[:, t % 2], ALU.add).then_inc(f_turned, 1)

        def b_tensor(pe):
            yield 1
            pe.wait_ge(b_xn, 1)
            transposes(BB.take(pe, "xnT"), xn_b, inc=b_filled)
            yield 2
            pe.wait_ge(*BB.brought("xnT", "act"))
            for product, w in (("q", wq_s), ("k", wk_s), ("gqk", wgqk_s)):
                nc.tensor.matmul(BB.take(pe, product)[:], w[:], xnT_b[:], start=True, stop=True).then_inc(b_filled, 1)
            yield 3
            ps = BB.take(pe, "v")
            for t in range(NT):
                last = nc.tensor.matmul(ps[:, t * E:(t + 1) * E], xnT_b[:, t * P:(t + 1) * P], wv_s[:], start=True, stop=True)
            last.then_inc(b_filled, 1)
            pe.wait_ge(b_pool, 1)
            nc.tensor.matmul(BB.take(pe, "gv")[:, 0:NL], pool_b[:].rearrange("p a l -> p (a l)"), wgv_s[:],
                             start=True, stop=True).then_inc(b_filled, 1)
            pe.wait_ge(*BB.brought("q", "act"))
            ps = BB.take(pe, "gates")
            for t in range(NT):
                last = nc.tensor.matmul(ps[:, t * 32:(t + 1) * 32], qkg_b[:, 0, t * P:(t + 1) * P],
                                        gateW[:].rearrange("p g h -> p (g h)"), start=True, stop=True)
            last.then_inc(b_filled, 1)

            def first_pass(g, n):
                _, _, t, hp = f = bfirst[g][n]
                if n == 0:
                    pe.wait_ge(b_stack[g], STACKED)
                skip = WIN if t == 0 else 0
                nk = LKEYS - skip
                k0 = t * P - WIN + skip
                ps = BB.take(pe, f)
                nc.tensor.matmul(ps[:, 0:2 * nk], ident_bf[:], win_q[:, skip:].unsqueeze(1).to_broadcast([P, 2, nk]),
                                 start=True, stop=False)
                for a in range(2):
                    last = nc.tensor.matmul(ps[:, a * nk:(a + 1) * nk], Qst_b[0:STACK, g % RING, 2 * hp + a, t * P:(t + 1) * P],
                                            Kst_b[0:STACK, g % RING, 2 * hp + a, k0:k0 + nk], start=False, stop=(a == 1))
                last.then_inc(b_filled, 1)

            def max_rows(g):
                pe.wait_ge(b_mparts, g + 1)
                transposes(BB.take(pe, ("mT", g)), mparts_b[:, g].rearrange("p t a j -> p t (a j)"), 8, b_filled)

            def values(g, k):
                pe.wait_ge(*BB.brought(("second", g, k, 1), "act"))
                if k == 0:
                    if g == 0:
                        pe.wait_ge(*BB.brought("v", "act"))
                    else:
                        pe.wait_ge(b_og, g)
                nq = min(LKEYS, T - k * P)
                for j in range(4):
                    last = nc.tensor.matmul(acc_b[32 * j:32 * j + D0 + 1, k * P:k * P + nq], V_b[:, k, 4 * g + j, :],
                                            prob_b[:, (2 * k + j // 2) % PR_B, (j % 2) * nq:(j % 2 + 1) * nq],
                                            start=(k == 0), stop=(k == NT - 1), skip_group_check=True)
                last.then_inc(b_av, 1)

            for n in range(8):
                yield 9 + n
                first_pass(0, n)
            yield 17
            max_rows(0)
            for t in range(NT):
                yield 18 + t / 4
                if t == 0:
                    pe.wait_ge(b_lstack, STACKED)
                ps = BB.take(pe, ("lfirst", t))
                nc.tensor.matmul(ps[:], ident_bf[:], lat_q[:, t, :].unsqueeze(1).to_broadcast([P, LH, NL]), start=True, stop=False)
                for h in range(LH):
                    last = nc.tensor.matmul(ps[:, h * NL:(h + 1) * NL], Qst_l[0:STACK, h, t * P:(t + 1) * P],
                                            Kst_l[0:STACK, h, :], start=False, stop=(h == LH - 1))
                last.then_inc(b_filled, 1)
            yield 19
            pe.wait_ge(b_lmparts, 1)
            transposes(BB.take(pe, "lmT"), mparts_l[:].rearrange("p t a h -> p t (a h)"), 2 * LH, b_filled)
            for g in range(G):
                for n in range(8):
                    yield 22 + 12 * g + n
                    if g + 1 < G:
                        first_pass(g + 1, n)
                    if n == 0:
                        pe.wait_ge(b_mrow[g], 16)
                        pe.wait_ge(b_ones, 32)
                    _, _, k, hp = s = bsecond[g][n]
                    nq = min(LKEYS, T - k * P)
                    ps = BB.take(pe, s)
                    nc.tensor.matmul(ps[:, 0:2 * nq], ident_bf[:], win_k[:, 0:nq].unsqueeze(1).to_broadcast([P, 2, nq]),
                                     start=True, stop=False)
                    for a in range(2):
                        last = nc.tensor.matmul(ps[:, a * nq:(a + 1) * nq], Kst_b[:, g % RING, 2 * hp + a, k * P:(k + 1) * P],
                                                Qst_b[:, g % RING, 2 * hp + a, k * P:k * P + nq], start=False, stop=(a == 1))
                    last.then_inc(b_filled, 1)
                    if n % 2 == 0 and n:
                        values(g, n // 2 - 1)
                yield 30 + 12 * g
                values(g, 3)
                if g + 1 < G:
                    max_rows(g + 1)
                yield 31 + 12 * g
                pe.wait_ge(b_og, g + 1)
                transposes(BB.take(pe, ("oT", g)), og_b[:].rearrange("p (t q) -> p t q", q=P), inc=b_filled)
            for u in range(4):
                yield 72 + u
                if u == 0:
                    pe.wait_ge(b_lmrow, 16)
                ps = BB.take(pe, ("lsecond", u))
                nc.tensor.matmul(ps[:], ident_bf[:], lat_k[:], start=True, stop=False, skip_group_check=True)
                for a in range(2):
                    last = nc.tensor.matmul(ps[64 * a:64 * a + 64, :], Kst_l[:, 2 * u + a, :], Qst_l[:, 2 * u + a, :],
                                            start=False, stop=(a == 1), skip_group_check=True)
                last.then_inc(b_filled, 1)
            yield 76
            pe.wait_ge(*BB.brought(("lsecond", 3), "act"))
            pe.wait_ge(*BB.brought("gv", "act"))
            pe.wait_ge(b_og, G)
            for u in range(4):
                last = nc.tensor.matmul(acc_b[32 * u:32 * u + 32, :], V_l[:, u, :], prob_b[:, u, :], start=True, stop=True)
            last.then_inc(b_av, 1)
            yield 77
            pe.wait_ge(b_og, G + 1)
            transposes(BB.take(pe, "loT"), og_b[:].rearrange("p (t q) -> p t q", q=P), inc=b_filled)
            yield 78
            pe.wait_ge(*BB.brought("loT", "dve"))
            transposes(BB.take(pe, "remT"), rem_b, NL, b_filled)
            yield 79
            pe.wait_ge(*BB.brought("remT", "act"))
            ps = BB.take(pe, "rproj")
            for t in range(NT):
                last = nc.tensor.matmul(ps[:, t * E:(t + 1) * E], og_b[0:NL, t * P:(t + 1) * P], r_out_s[:], start=True, stop=True)
            last.then_inc(b_filled, 1)
            yield 80
            pe.wait_ge(b_mix, 1)
            transposes(BB.take(pe, "mixT"), mix_b[:].rearrange("p (t e) -> p t e", e=E), inc=b_filled)
            yield 81
            pe.wait_ge(*BB.brought("mixT", "act"))
            ps = BB.take(pe, "wout")
            for t in range(NT):
                last = nc.tensor.matmul(ps[:, t * E:(t + 1) * E], og_b[:, t * P:(t + 1) * P], w_out_s[:], start=True, stop=True)
            last.then_inc(b_filled, 1)

            for l in range(DEPTH):
                s0 = LAYER_AT + LAYER * l

                def queries_keys_T(t):
                    pe.wait_ge(f_rot, NT * l + t + 1)
                    for a in range(2):
                        ps = BB.take(pe, ("qkT", l, t, a))
                        for c in range(FH // 2):
                            last = nc.tensor.transpose(ps[:, c * P:(c + 1) * P], qk_rot[:, a, c * P:(c + 1) * P], ident[:])
                        last.then_inc(b_filled, 1)

                for t in range(NT):
                    yield s0 + 7 * t
                    if l and t == 0:
                        pe.wait_ge(*BB.brought(("fnext", l - 1), "act"))
                    for n, product in enumerate(("fq", "fk", "fv")):
                        nc.tensor.matmul(BB.take(pe, (product, l, t))[:], hT[:, t * P:(t + 1) * P],
                                         wqkv_s[:, l, n * INNER:(n + 1) * INNER], start=True, stop=True).then_inc(b_filled, 1)
                    if t:
                        yield s0 + 7 * t + 3
                        queries_keys_T(t - 1)
                yield s0 + 7 * NT + 3
                queries_keys_T(NT - 1)
                for t in range(NT):
                    for c in range(FH // 2):
                        yield s0 + 34 + 4 * t + c
                        if t == 0 and c == 0:
                            pe.wait_ge(*BB.brought(("qkT", l, NT - 1, 1), "act"))
                        skip = FW if t == 0 else 0
                        nk = FKEYS - skip
                        k0 = t * P - FW + skip
                        ps = BB.take(pe, ("ffirst", l, t, c))
                        nc.tensor.matmul(ps[:, 0:2 * nk], ident_bf[:], band_q[:, skip:].unsqueeze(1).to_broadcast([P, 2, nk]),
                                         start=True, stop=False)
                        for a in range(2):
                            last = nc.tensor.matmul(ps[:, a * nk:(a + 1) * nk], qT[:, c, t * P:(t + 1) * P],
                                                    kT[:, c, a, k0:k0 + nk], start=False, stop=(a == 1))
                        last.then_inc(b_filled, 1)
                yield s0 + 52
                pe.wait_ge(f_mparts, l + 1)
                transposes(BB.take(pe, ("fmT", l)), mparts_f[:].rearrange("p t a h -> p t (a h)"), 2 * FH, b_filled)

                def keys_first(n):
                    c, k = n // NT, n % NT
                    if n == 0:
                        pe.wait_ge(*BB.brought(("fmT", l), "act"))
                    nq = min(FKEYS, T - k * P)
                    q = slice(k * P, k * P + nq)
                    ps = BB.take(pe, ("fsecond", l, n))
                    nc.tensor.matmul(ps[:, 0:2 * nq], ident_bf[:], band_k[:, 0:nq].unsqueeze(1).to_broadcast([P, 2, nq]),
                                     start=True, stop=False)
                    for a in range(2):
                        nc.tensor.matmul(ps[:, a * nq:(a + 1) * nq], pick[:, 2 * c + a, :], mT_f[:, q], start=False, stop=False)
                        last = nc.tensor.matmul(ps[:, a * nq:(a + 1) * nq], kT[:, c, a, k * P:(k + 1) * P], qT[:, c, q],
                                                start=False, stop=(a == 1))
                    last.then_inc(b_filled, 1)

                def values_f(n):
                    c, k = n // NT, n % NT
                    pe.wait_ge(*BB.brought(("fsecond", l, n), "act"))
                    ps = BB.take(pe, ("fav", l, n))
                    nq = min(FKEYS, T - k * P)
                    for a in range(2):
                        o = ps[:, a * (FD + 1):(a + 1) * (FD + 1)]
                        last = nc.tensor.matmul(o, prob_b[:, k % PR_B, a * nq:a * nq + P], V_f[:, k, 2 * c + a, :],
                                                start=True, stop=True)
                        if k:
                            last = nc.tensor.matmul(o[0:FW, :], prob_b[:, (k - 1) % PR_B, a * FKEYS + P:(a + 1) * FKEYS],
                                                    V_f[:, k - 1, 2 * c + a, :], start=False, stop=True, skip_group_check=True)
                    last.then_inc(b_filled, 1)

                for n in range(UNITS + 2):
                    yield s0 + 54 + UNIT * n
                    if n < UNITS:
                        keys_first(n)
                    if n % NT == 1 and n > NT:
                        c = n // NT - 1
                        pe.wait_ge(*BB.brought(("fav", l, NT * c + NT - 1), "dve"))
                        transposes(BB.take(pe, ("foT", l, c)), otok_f[:, c % 2], inc=b_filled)
                    if 0 < n <= UNITS:
                        values_f(n - 1)
                yield s0 + 86
                pe.wait_ge(*BB.brought(("foT", l, FH // 2 - 1), "act"))
                ps = BB.take(pe, ("fwo", l))
                for t in range(NT):
                    for c in range(INNER // P):
                        last = nc.tensor.matmul(ps[:, t * E:(t + 1) * E], oT_f[:, c, t * P:(t + 1) * P], wo_s[:, l, c, :],
                                                start=(c == 0), stop=(c == INNER // P - 1))
                last.then_inc(b_filled, 1)
                yield s0 + 88
                pe.wait_ge(*BB.brought(("fwo", l), "dve"))
                transposes(BB.take(pe, ("fx", l)), x_f, inc=b_filled)
                yield s0 + 90
                pe.wait_ge(*BB.brought(("fx", l), "act"))
                transposes(BB.take(pe, ("fback", l)), hT[:].rearrange("p (t q) -> p t q", q=P), inc=b_filled)
                yield s0 + 92
                pe.wait_ge(*BB.brought(("fback", l), "dve"))
                transposes(BB.take(pe, ("fnT", l)), xn_b, inc=b_filled)
                for c, (c0, n) in enumerate(HC):
                    yield s0 + 94 + 2 * c
                    if c == 0:
                        pe.wait_ge(*BB.brought(("fnT", l), "dve"))
                    for product, col in (("fg", HID + c0), ("fa", c0)):
                        nc.tensor.matmul(BB.take(pe, (product, l, c))[0:n, :], w1_s[:, l, col:col + n], xnT_b[:],
                                         start=True, stop=True).then_inc(b_filled, 1)
                yield s0 + 102
                pe.wait_ge(*BB.brought(("fa", l, len(HC) - 1), "dve"))
                ps = BB.take(pe, ("fw2", l))
                for t in range(NT):
                    for c, (c0, n) in enumerate(HC):
                        last = nc.tensor.matmul(ps[:, t * E:(t + 1) * E], u_f[0:n, c, t * P:(t + 1) * P], w2_s[0:n, l, c, :],
                                                start=(c == 0), stop=(c == len(HC) - 1))
                last.then_inc(b_filled, 1)
                if l + 1 < DEPTH:
                    yield s0 + 106
                    pe.wait_ge(f_x, 2 * l + 2)
                    transposes(BB.take(pe, ("fnext", l)), x_f, inc=b_filled)

        def b_scalar(act):
            def bring(product, dst, func=ACT.Copy, rows=slice(0, P), cols=slice(0, T), last=True, **kw):
                ins = nc.scalar.activation(dst, BB.full(act, product)[rows, cols], func, **kw)
                if last:
                    ins.then_inc(b_emptied["act"], 1)

            def shifted(product):
                bring(product, hT[0:64, :], rows=slice(0, 64), last=False)
                bring(product, hT[64:P, 1:T], rows=slice(64, P), cols=slice(0, T - 1))

            yield 1
            bring("xnT", xnT_b[:], last=False)
            shifted("xnT")
            yield 2
            bring("q", qkg_b[:, 0, :])
            bring("k", qkg_b[:, 1, :])
            bring("gqk", qkg_b[0:64, 2, :], rows=slice(0, 64))
            yield 3
            ps = BB.full(act, "v")
            nc.scalar.activation(V_b[:].rearrange("p t h c -> p (t h) c")[:, :, 0:D0],
                                 ps[:].rearrange("p (n d) -> p n d", d=D0), ACT.Copy).then_inc(b_emptied["act"], 1)
            ps = BB.full(act, "gv")
            for a in range(2):
                half = slice(64 * a, 64 * a + 64)
                last = nc.scalar.activation(V_l[half, :, 16 * a:16 * a + D0],
                                            ps[half, 0:NL].rearrange("p (u a d) -> p u a d", a=2, d=D0)[:, :, a, :], ACT.Copy)
            last.then_inc(b_emptied["act"], 1)
            ps = BB.full(act, "gates")
            nc.scalar.activation(gate_b[:].rearrange("p t g h -> p (t g h)"), ps[:, 0:P], ACT.Tanh,
                                 scale=0.5).then_inc(b_emptied["act"], 1)
            yield 18
            bring(("mT", 0), mT_b[:, 0, :], rows=slice(0, 8))
            yield 20
            bring("lmT", mT_l[:], rows=slice(0, 2 * LH))
            for g in range(G):
                for n in range(8):
                    yield 22 + 12 * g + n
                    if n % 2 == 0 and 4 * g + n // 2 >= 2:
                        act.wait_ge(b_av, 4 * g + n // 2 - 1)
                    nq = min(LKEYS, T - n // 2 * P)
                    if g == 0 and n == 0:
                        act.wait_ge(b_split, 1)
                    bring(bsecond[g][n], prob_b[:, n % PR_B, 0:2 * nq], ACT.Exp, cols=slice(0, 2 * nq), scale=HEAD_SCALE)
                yield 30 + 12 * g
                if g + 1 < G:
                    if g >= 1:
                        act.wait_ge(b_mspill[g - 1], 16)
                    bring(("mT", g + 1), mT_b[:, (g + 1) % 2, :], rows=slice(0, 8))
                act.wait_ge(b_av, 4 * g + 4)
                if g:
                    act.wait_ge(*BB.made(("oT", g - 1)))
                nc.scalar.activation(og_b[:], acc_b[:], ACT.Copy).then_inc(b_og, 1)
            for u in range(4):
                yield 72 + u
                bring(("lsecond", u), prob_b[:, u, :], ACT.Exp, scale=HEAD_SCALE)
            yield 76
            act.wait_ge(b_av, 4 * G + 1)
            act.wait_ge(*BB.made(("oT", G - 1)))
            nc.scalar.activation(og_b[:], acc_b[:], ACT.Copy).then_inc(b_og, 1)
            yield 78
            bring("remT", og_b[0:NL, :], rows=slice(0, NL))
            yield 80
            act.wait_ge(*BB.made("rproj"))
            bring("mixT", og_b[:])
            yield 81
            bring("wout", s_b[:])
            for l in range(DEPTH):
                s0 = LAYER_AT + LAYER * l
                def queries_keys_T(t):
                    ps = BB.full(act, ("qkT", l, t, 0))
                    nc.scalar.activation(qT[:, :, t * P:(t + 1) * P], ps[:].rearrange("p (c q) -> p c q", q=P), ACT.Copy)\
                        .then_inc(b_emptied["act"], 1)
                    ps = BB.full(act, ("qkT", l, t, 1))
                    for a in range(2):
                        half = slice(64 * a, 64 * a + 64)
                        last = nc.scalar.activation(kT[half, :, a, t * P:(t + 1) * P],
                                                    ps[half, :].rearrange("p (c q) -> p c q", q=P), ACT.Copy)
                    last.then_inc(b_emptied["act"], 1)

                for t in range(NT):
                    yield s0 + 7 * t
                    n = NT * l + t
                    if n >= 2:
                        act.wait_ge(f_turned, n - 1)
                    for a, product in enumerate(("fq", "fk")):
                        bring((product, l, t), sq[:, t % 2, a, :], ACT.Square, last=False)
                        bring((product, l, t), qk_raw[:, t % 2, a, :])
                    ps = BB.full(act, ("fv", l, t))
                    nc.scalar.activation(V_f[:, t, :, 0:FD], ps[:].rearrange("p (h d) -> p h d", d=FD), ACT.Copy)\
                        .then_inc(b_emptied["act"], 1)
                    if t:
                        yield s0 + 7 * t + 3
                        queries_keys_T(t - 1)
                yield s0 + 7 * NT + 3
                queries_keys_T(NT - 1)
                yield s0 + 52
                bring(("fmT", l), mT_f[0:2 * FH, :], rows=slice(0, 2 * FH))
                for n in range(UNITS + 2):
                    yield s0 + 54 + UNIT * n
                    if n < UNITS:
                        nq = min(FKEYS, T - n % NT * P)
                        if n >= NT:
                            act.wait_ge(*BB.made(("fav", l, n - NT + (n % NT < NT - 1))))
                        bring(("fsecond", l, n), prob_b[:, n % PR_B, 0:2 * nq], ACT.Exp, cols=slice(0, 2 * nq), scale=QK_SCALE)
                    if n % NT == 1 and n > NT:
                        bring(("foT", l, n // NT - 1), oT_f[:, n // NT - 1, :])
                yield s0 + 89
                shifted(("fx", l))
                for c, (c0, n) in enumerate(HC):
                    yield s0 + 94 + 2 * c
                    if c:
                        act.wait_ge(*BB.brought(("fa", l, c - 1), "dve"))
                    nc.scalar.activation(gelu_f[0:n, :], BB.full(act, ("fg", l, c))[0:n, :], ACT.Gelu,
                                         bias=b1_s[0:n, l, 1, c:c + 1]).then_inc(b_emptied["act"], 1)
                if l + 1 < DEPTH:
                    yield s0 + 107
                    shifted(("fnext", l))
            yield LAYER_AT + LAYER * DEPTH + 2
            act.wait_ge(f_x, 2 * DEPTH)
            nc.scalar.activation(mix_b[:], x_f[:].rearrange("p t e -> p (t e)"), ACT.Tanh, scale=0.5).then_inc(b_tanh, 1)

        def b_vector(dve):
            link = chain(dve, b_dve_step)
            emptied = b_emptied["dve"]
            yield 0
            dve.wait_ge(b_x, 1)
            layernorm(link, x_b, xn_b, stats_b, mv_b, rs_b, b_xn)
            yield 1
            dve.wait_ge(*BB.brought("xnT", "act"))
            link(nc.vector.tensor_reduce(out=psum_l[:, 0, :], in_=xnT_b[:].rearrange("p (l t) -> p l t", t=POOL), op=ALU.add,
                                         axis=AX.X))
            for a in range(2):
                last = nc.vector.tensor_scalar(pool_b[:, a, :], psum_l[:, 0, :], 1.0 / POOL, None, ALU.mult)
            last.then_inc(b_pool, 1)
            yield 2
            ps = BB.full(dve, "gqk")
            nc.vector.tensor_reduce(out=psum_l[64:P, 1, :], in_=ps[64:P, :].rearrange("p (l t) -> p l t", t=POOL), op=ALU.add,
                                    axis=AX.X).then_inc(emptied, 1)
            dve.wait_ge(*BB.brought("gqk", "dve"))
            nc.vector.memset(qkg_b[64:P, 2, NL:T], 0.0)
            link(nc.vector.tensor_scalar(qkg_b[64:P, 2, 0:NL], psum_l[64:P, 1, :], 1.0 / POOL, None, ALU.mult))
            yield 3
            dve.wait_ge(*BB.brought("gqk", "act"))
            split(link, qkg_b[:], res_b, [parts_b[:, :, c, :] for c in range(SPLIT)], b_split)
            dve.wait_ge(*BB.brought("gates", "act"))
            g2 = gate_b[:].rearrange("p t g h -> p (t g h)")
            nc.vector.tensor_scalar(g2, g2, 0.5, 0.5, ALU.mult, ALU.add).then_inc(b_gate, 1)

            def first_pass(g, n):
                _, _, t, hp = f = bfirst[g][n]
                nk = LKEYS - (WIN if t == 0 else 0)
                nc.vector.tensor_reduce(out=nmax_b[:, g, t, 2 * hp:2 * hp + 2],
                                        in_=BB.full(dve, f)[:, 0:2 * nk].rearrange("p (a k) -> p a k", a=2),
                                        op=ALU.max, axis=AX.X, negate=True).then_inc(emptied, 1)

            def max_parts(g):
                dve.wait_ge(*BB.brought(bfirst[g][-1], "dve"))
                split_max(link, nmax_b[:, g], mhi_b[:, g], [mparts_b[:, g, :, p, :] for p in range(2)], b_mparts)

            for n in range(8):
                yield 9 + n
                first_pass(0, n)
            yield 17
            max_parts(0)
            for t in range(NT):
                yield 18 + t / 4
                nc.vector.tensor_reduce(out=nmax_l[:, t, :], in_=BB.full(dve, ("lfirst", t))[:].rearrange("p (h l) -> p h l", l=NL),
                                        op=ALU.max, axis=AX.X, negate=True).then_inc(emptied, 1)
            yield 19
            dve.wait_ge(*BB.brought(("lfirst", NT - 1), "dve"))
            split_max(link, nmax_l[:], mhi_l[:], [mparts_l[:, :, p, :] for p in range(2)], b_lmparts)
            for g in range(G):
                for n in range(8):
                    yield 22 + 12 * g + n
                    if g + 1 < G:
                        first_pass(g + 1, n)
                yield 30 + 12 * g
                if g + 1 < G:
                    max_parts(g + 1)
                yield 31 + 12 * g
                ps = BB.full(dve, ("oT", g))[:].rearrange("p (t j c) -> p t j c", t=NT, c=32)
                rden = rden_b[:, 0:4 * NT].rearrange("p (t j) -> p t j", j=4)
                link(nc.vector.reciprocal(rden, ps[:, :, :, D0]))
                nc.vector.tensor_tensor(loc_b[:, :, 32 * g:32 * g + 32].rearrange("p t (j d) -> p t j d", d=D0),
                                        ps[:, :, :, 0:D0], rden.unsqueeze(3).to_broadcast([P, NT, 4, D0]),
                                        ALU.mult).then_inc(emptied, 1)
                dve.wait_ge(*BB.brought(("oT", g), "dve"))
            yield 77
            ps = BB.full(dve, "loT")[:].rearrange("p (n s) -> p n s", s=16)
            link(nc.vector.reciprocal(rden_b[:], ps[:, :, D0]))
            nc.vector.tensor_tensor(rem_b[:].rearrange("p t (h d) -> p (t h) d", d=D0), ps[:, :, 0:D0],
                                    rden_b[:].unsqueeze(2).to_broadcast([P, NT * LH, D0]), ALU.mult).then_inc(emptied, 1)
            yield 79
            dve.wait_ge(b_gate, 1)
            heads = "p t (h d) -> p t h d"

            def gate(g):
                return gate_b[:, :, g, :].unsqueeze(3).to_broadcast([P, NT, H0, D0])

            loc = loc_b[:].rearrange(heads, d=D0)
            link(nc.vector.tensor_tensor(loc, loc, gate(0), ALU.mult))
            nc.vector.tensor_tensor(mix_b[:].rearrange("p (t h d) -> p t h d", t=NT, d=D0),
                                    BB.full(dve, "rproj")[:].rearrange("p (t h d) -> p t h d", t=NT, d=D0),
                                    gate(1), ALU.mult).then_inc(emptied, 1)
            dve.wait_ge(*BB.brought("rproj", "dve"))
            nc.vector.tensor_tensor(mix_b[:], mix_b[:], loc_b[:].rearrange("p t e -> p (t e)"), ALU.add).then_inc(b_mix, 1)

            flat = "p t e -> p (t e)"
            for l in range(DEPTH):
                s0 = LAYER_AT + LAYER * l

                def normalised(t):
                    n = NT * l + t
                    if n:
                        dve.wait_ge(*BB.made(("qkT", (n - 1) // NT, (n - 1) % NT, 1)))
                    dve.wait_ge(f_turned, n + 1)
                    nc.vector.tensor_tensor(qk_rot.rearrange("p a (h d) -> p (a h) d", d=FD),
                                            cosp[:, t % 2].rearrange("p a (h d) -> p (a h) d", d=FD),
                                            rn[:, t % 2, 1, :].unsqueeze(2).to_broadcast([P, 2 * FH, FD]), ALU.mult).then_inc(f_rot, 1)
                    dve.wait_ge(f_rot, n + 1)

                for t in range(NT):
                    yield s0 + 7 * t + 1
                    n = NT * l + t
                    dve.wait_ge(*BB.brought(("fk", l, t), "act"))
                    nc.vector.tensor_reduce(out=ss[:], in_=sq[:, t % 2].rearrange("p a (h d) -> p a h d", d=FD), op=ALU.add,
                                            axis=AX.X).then_inc(f_sq, 1)
                    for a in range(2):
                        last = nc.vector.tensor_tensor(cosp[:, t % 2, a, :].rearrange("p (h d) -> p h d", d=FD),
                                                       qk_raw[:, t % 2, a, :].rearrange("p (h d) -> p h d", d=FD),
                                                       rotf[:, l, 2 * a, t, :].unsqueeze(1).to_broadcast([P, FH, FD]), ALU.mult)
                    last.then_inc(f_cos, 1)
                    v = rn[:, t % 2, 0, :]
                    dve.wait_ge(f_sq, n + 1)
                    link(nc.vector.tensor_scalar(v, ss[:].rearrange("p a h -> p (a h)"), 1e-24, None, ALU.max))
                    rsqrt(link, v, rn[:, t % 2, 1, :], rn[:, t % 2, 2, :])
                    if t:
                        yield s0 + 7 * t + 3
                        normalised(t - 1)
                yield s0 + 7 * NT + 2
                normalised(NT - 1)
                for t in range(NT):
                    for c in range(FH // 2):
                        yield s0 + 34 + 4 * t + c
                        nk = FKEYS - (FW if t == 0 else 0)
                        nc.vector.tensor_reduce(out=nmax_f[:, t, 2 * c:2 * c + 2],
                                                in_=BB.full(dve, ("ffirst", l, t, c))[:, 0:2 * nk].rearrange("p (a k) -> p a k", a=2),
                                                op=ALU.max, axis=AX.X, negate=True).then_inc(emptied, 1)
                yield s0 + 50.5
                dve.wait_ge(*BB.brought(("ffirst", l, NT - 1, FH // 2 - 1), "dve"))
                split_max(link, nmax_f[:], mhi_f[:], [mparts_f[:, :, p, :] for p in range(2)], f_mparts)
                for n in range(UNITS):
                    yield s0 + 54 + UNIT * (n + 1)
                    c, k = n // NT, n % NT
                    ps = BB.full(dve, ("fav", l, n))[:, 0:2 * (FD + 1)].rearrange("p (a d) -> p a d", a=2)
                    if c >= 2 and k == 0:
                        dve.wait_ge(*BB.made(("foT", l, c - 2)))
                    link(nc.vector.reciprocal(rden_f[:, n % 2], ps[:, :, FD]))
                    nc.vector.tensor_tensor(otok_f[:, c % 2, k, :].rearrange("p (a d) -> p a d", a=2), ps[:, :, 0:FD],
                                            rden_f[:, n % 2].unsqueeze(2).to_broadcast([P, 2, FD]), ALU.mult).then_inc(emptied, 1)
                    if n:
                        dve.wait_ge(*BB.brought(("fav", l, n - 1), "dve"))
                yield s0 + 87
                x_in_l = xn_b if l == 0 else x_f
                nc.vector.tensor_tensor(x_f[:].rearrange(flat), BB.full(dve, ("fwo", l))[:], x_in_l[:].rearrange(flat),
                                        ALU.add).then_inc(emptied, 1)
                yield s0 + 91
                ps = BB.full(dve, ("fback", l))
                layernorm(link, ps[:].rearrange("p (t e) -> p t e", e=E), xn_b, stats_b, mv_b, rs_b, emptied)
                yield s0 + 93
                nc.vector.tensor_scalar(xnT_b[:], BB.full(dve, ("fnT", l))[:], lng_s[:, l:l + 1], lnb_s[:, l:l + 1],
                                        ALU.mult, ALU.add).then_inc(emptied, 1)
                for c, (c0, n) in enumerate(HC):
                    yield s0 + 95 + 2 * c
                    dve.wait_ge(*BB.brought(("fg", l, c), "act"))
                    nc.vector.scalar_tensor_tensor(out=u_f[0:n, c, :], in0=BB.full(dve, ("fa", l, c))[0:n, :],
                                                   scalar=b1_s[0:n, l, 0, c:c + 1], in1=gelu_f[0:n, :],
                                                   op0=ALU.add, op1=ALU.mult).then_inc(emptied, 1)
                yield s0 + 103
                nc.vector.tensor_tensor(x_f[:].rearrange(flat), BB.full(dve, ("fw2", l))[:], x_f[:].rearrange(flat),
                                        ALU.add).then_inc(emptied, 1)
                dve.wait_ge(*BB.brought(("fw2", l), "dve"))
                nc.vector.tensor_tensor(x_f[:], x_f[:], b2_s[:, l, :].unsqueeze(1).to_broadcast([P, NT, E]), ALU.add)\
                    .then_inc(f_x, 2)
            yield LAYER_AT + LAYER * DEPTH + 3
            dve.wait_ge(b_tanh, 1)
            dve.wait_ge(f_x, 2 * DEPTH)
            link(nc.vector.scalar_tensor_tensor(out=mix_b[:], in0=mix_b[:], scalar=1.0, in1=x_f[:].rearrange(flat),
                                                op0=ALU.add, op1=ALU.mult))
            dve.wait_ge(*BB.brought("wout", "act"))
            link(nc.vector.tensor_tensor(mix_b[:], mix_b[:], s_b[:], ALU.mult))
            nc.vector.scalar_tensor_tensor(out=x_f[:].rearrange(flat), in0=mix_b[:], scalar=0.5, in1=x_b[:].rearrange(flat),
                                           op0=ALU.mult, op1=ALU.add).then_inc(b_out, 1)


        lo, hi = min(s.num for s in sems), max(s.num for s in sems)

        def clear_all():
            nc.multi_engine_barrier(list(nc.engines), sems_to_clear=range(lo, hi + 1))

        def iteration(row_a, row_b):
            with nc.Block() as block:
                @block.sync
                def _(sp):
                    merge(*([a_sync(sp, row_a)] if row_a is not None else []), *([b_sync(sp, row_b)] if row_b is not None else []))

                @block.gpsimd
                def _(pool):
                    merge(*([b_gpsimd(pool)] if row_b is not None else []))

                @block.tensor
                def _(pe):
                    merge(*([a_tensor(pe)] if row_a is not None else []), *([b_tensor(pe)] if row_b is not None else []))

                @block.scalar
                def _(act):
                    merge(*([a_scalar(act)] if row_a is not None else []), *([b_scalar(act)] if row_b is not None else []))

                @block.vector
                def _(dve):
                    merge(*([a_vector(dve, row_b is not None)] if row_a is not None else []), *([b_vector(dve)] if row_b is not None else []))
            clear_all()

        clear_all()
        iteration(bass.ds(0, 1), None)
        with nc.Fori(1, B) as b:
            iteration(bass.ds(b, 1), bass.ds(b - 1, 1))
        iteration(None, bass.ds(B - 1, 1))


_SAME = {"att_w": "L0_attn_w_att_val", "wv0_b": "L0_attn_wv_b", "wo0_b": "L0_attn_out_b", "W1": "L0_ffn_W1",
         "W2": "L0_ffn_W2", "Wg": "L0_ffn_Wg", "bg": "L0_ffn_bg", "wq": "L1_attn_wq", "wk": "L1_attn_wk",
         "wv": "L1_attn_wv", "wgv": "L1_attn_wgv", "r_out": "L1_attn_r_out_w", "gate_l": "L1_attn_gate_local_w",
         "gate_r": "L1_attn_gate_remote_w", "w_out": "L1_attn_w_out", "wqkv": "L1_ffn_wqkv",
         "q_sc": "L1_ffn_q_scale", "k_sc": "L1_ffn_k_scale", "wo": "L1_ffn_wo", "ln_g": "L1_ffn_ln_g",
         "ln_b": "L1_ffn_ln_b", "w1": "L1_ffn_w1", "b1": "L1_ffn_b1", "w2": "L1_ffn_w2", "b2": "L1_ffn_b2"}


def kernel(**inputs):
    import concourse.bacc as bacc
    from concourse.bass_utils import run_bass_kernel_spmd

    a = {n: np.asarray(v) for n, v in inputs.items()}
    laid = {"x_in": a["L0_attn_x"], "wv0T": a["L0_attn_wv_w"].T, "wo0T": a["L0_attn_out_w"].T,
            "wgqk": np.concatenate([a["L1_attn_wgq"], a["L1_attn_wgk"]], axis=1)}
    laid |= {n: a[full] for n, full in _SAME.items()}
    consts = shape_constants()

    nc = bacc.Bacc("TRN2", target_bir_lowering=False, num_devices=1)
    arrays = {}

    def dram(name, array):
        arrays[name] = np.ascontiguousarray(array)
        return nc.dram_tensor(name, array.shape, mybir.dt.from_np(array.dtype), kind="ExternalInput").ap()

    aps = {n: dram(f"in_{n}", v) for n, v in laid.items()}
    const_aps = {n: dram(f"const_{n}", v) for n, v in consts.items()}
    out = nc.dram_tensor("out_0", (B, T, E), F32, kind="ExternalOutput").ap()
    mixer_kernel(nc, **aps, consts=const_aps, out=out)
    r = run_bass_kernel_spmd(nc, [arrays], core_ids=[0])
    return r.results[0]["out_0"]
```

```python
from contextlib import ExitStack

import numpy as np

import concourse.bass as bass
from concourse import mybir

ALU = mybir.AluOpType
ACT = mybir.ActivationFunctionType
AX = mybir.AxisListType
F32 = mybir.dt.float32
BF16 = mybir.dt.bfloat16
I32 = mybir.dt.int32

P = 128
B, T, E = 16, 512, 128
NT = T // P
H0, D0 = 16, 8
NX, HX = 8, 512
XC = HX // P
WIN = 32
LH, NL = 8, 64
POOL = T // NL
FH, FD, FW = 8, 64, 64
INNER = FH * FD
HID = int(E * 4 * 2 / 3)
HC = [(c, min(P, HID - c)) for c in range(0, HID, P)]
DEPTH = 2
UNITS = FH // 2 * NT
SPLIT = 3
STACK = SPLIT * SPLIT * D0
ROWS = STACK + 2
G = H0 // 4
LKEYS = P + WIN
FKEYS = P + FW
EPS = 1e-5
MASKED = -1e30

A_PROJ, A_END, A_NEXT = 139, 173, 176
A_GROUP = (15, 37, 60, 84)
A_EXPERT = (110, 116, 122, 128, 144, 151, 158, 165)
EARLY = 4
A_KNOTS = (15, 26, 37, 48, 60, 72, 84, 96, 108, 117, 124, 132, 140, 148, 156, 164, 172, 178, 186, 196, 206)
PACE = (2.5, 8, 24, 38, 48, 62, 74, 82, 92, 102.1, 114.0, 131.0, 175, 176, 195, 208, 222, 244, 260, 276, 294)
B_AT = 9
LAYER = 110
LAYER_AT = B_AT + 79
UNIT = 1.8
FINISH = 3
QKV = 7
HEAD_SCALE = float(D0) ** -0.5
QK_SCALE = 8.0
RSQRT_MAGIC = float(0x5F3759DF)


def shape_constants():
    bf = mybir.dt.np(BF16)
    c = {"ident": np.eye(P, dtype=np.float32), "ident_bf": np.eye(P, dtype=np.float32).astype(bf)}
    c["ones_bf"] = np.ones((2, 8 * T), np.float32).astype(bf)
    q, k = np.arange(P)[:, None], np.arange(LKEYS)[None, :] - WIN
    c["win_q"] = np.where((k > q - WIN) & (k <= q), 0.0, MASKED)
    k, q = np.arange(P)[:, None], np.arange(LKEYS)[None, :]
    c["win_k"] = np.where((k > q - WIN) & (k <= q), 0.0, MASKED)
    q, k = np.arange(P)[:, None], np.arange(FKEYS)[None, :] - FW
    c["band_q"] = np.where((k >= q - FW) & (k <= q), 0.0, MASKED)
    k, q = np.arange(P)[:, None], np.arange(FKEYS)[None, :]
    c["band_k"] = np.where((k >= q - FW) & (k <= q), 0.0, MASKED)
    t = np.arange(T).reshape(NT, P).T[:, :, None]
    lat = np.arange(NL)
    c["lat_q"] = np.where(lat[None, None, :] <= t // POOL, 0.0, MASKED).reshape(P, NT * NL)
    c["lat_k"] = np.where((np.arange(P) % NL)[:, None] <= np.arange(T)[None, :] // POOL, 0.0, MASKED)
    for n in ("win_q", "win_k", "band_q", "band_k", "lat_q", "lat_k"):
        c[n] = c[n].astype(np.float32).astype(bf)
    c["blocks"] = np.kron(np.eye(H0), np.ones((D0, 1))).astype(np.float32)
    sel = np.zeros((P, FH, P), np.float32)
    for h in range(FH):
        sel[[h, FH + h], h, :] = 1.0
    c["pick"] = sel.reshape(P, FH * P).astype(bf)
    half = np.arange(0, FD, 2, dtype=np.float32)
    freq = np.arange(T, dtype=np.float32)[:, None] * (1.0 / 10000.0 ** (half / FD)).astype(np.float32)
    freq = np.concatenate([freq, freq], axis=1)
    base = (half + 0.4 * FD) / (1.4 * FD)
    scale = base[None, :] ** ((np.arange(T) - T // 2) / float(FW // 2))[:, None]
    scale = np.concatenate([scale, scale], axis=1)
    sign = np.where(np.arange(FD) < FD // 2, -1.0, 1.0)
    rot = np.stack([np.cos(freq) * scale, np.sin(freq) * scale * sign,
                    np.cos(freq) / scale, np.sin(freq) / scale * sign])
    c["rotary"] = rot.reshape(4, NT, P, FD).transpose(2, 0, 1, 3).reshape(P, 4 * T // P * FD).astype(np.float32)
    return {n: np.ascontiguousarray(a) for n, a in c.items()}


class Banks:

    def __init__(self, tiles, filled, emptied, plan):
        self.tiles, self.filled, self.emptied = tiles, filled, emptied
        self.number, self.outs = {}, {}
        count = dict.fromkeys(emptied, 0)
        self.plan = [product for product, _ in plan]
        for n, (product, engines) in enumerate(plan):
            assert product not in self.number, product
            self.number[product] = n
            for e in engines:
                count[e] += 1
            self.outs[product] = {e: (emptied[e], count[e]) for e in engines}

    def bank(self, product):
        return self.tiles[self.number[product] % len(self.tiles)]

    def made(self, product):
        return self.filled, self.number[product] + 1

    def brought(self, product, engine):
        return self.outs[product][engine]

    def take(self, pe, product):
        n = self.number[product] - len(self.tiles)
        for semaphore, value in self.outs[self.plan[n]].values() if n >= 0 else ():
            pe.wait_ge(semaphore, value)
        return self.bank(product)

    def full(self, eng, product):
        eng.wait_ge(*self.made(product))
        return self.bank(product)


def paced(stream):
    for slot in stream:
        yield float(np.interp(slot, A_KNOTS, PACE))


def merge(*streams):
    heads = [next(s, None) for s in streams]
    while any(h is not None for h in heads):
        n = min((h, i) for i, h in enumerate(heads) if h is not None)[1]
        heads[n] = next(streams[n], None)


def mixer_kernel(nc, x_in, att_w, wv0T, wv0_b, wo0T, wo0_b, W1, W2, Wg, bg, wq, wk, wv, wgqk, wgv,
                 r_out, gate_l, gate_r, w_out, wqkv, q_sc, k_sc, wo, ln_g, ln_b, w1, b1, w2, b2,
                 consts, out):
    ctx = ExitStack()
    with ctx:
        def sb(name, shape, dt=F32):
            return ctx.enter_context(nc.sbuf_tensor(name, shape, dt))

        sems = []

        def sem(name):
            sems.append(ctx.enter_context(nc.semaphore(name)))
            return sems[-1]

        banks = [ctx.enter_context(nc.psum_tensor(f"bank{i}", [P, T], F32)) for i in range(8)]

        ident, ident_bf = sb("ident", [P, P]), sb("ident_bf", [P, P], BF16)
        win_q, win_k = sb("win_q", [P, LKEYS], BF16), sb("win_k", [P, LKEYS], BF16)
        band_q, band_k = sb("band_q", [P, FKEYS], BF16), sb("band_k", [P, FKEYS], BF16)
        lat_q, lat_k = sb("lat_q", [P, NT, NL], BF16), sb("lat_k", [P, T], BF16)
        blocks, pick = sb("blocks", [P, H0]), sb("pick", [P, FH, P], BF16)
        att_c, attW = sb("att_c", [P, D0]), sb("attW", [P, E])
        wv0_s, wo0_s = sb("wv0_s", [P, E]), sb("wo0_s", [P, E])
        bv0, bo0 = sb("bv0", [P, E]), sb("bo0", [P, E])
        Wg_s, bg_s = sb("Wg_s", [P, NX]), sb("bg_s", [P, NX])
        wq_s, wk_s, wv_s, w_out_s = (sb(n, [P, E]) for n in ("wq_s", "wk_s", "wv_s", "w_out_s"))
        wgqk_s, wgv_s, r_out_s = sb("wgqk_s", [P, E]), sb("wgv_s", [P, NL]), sb("r_out_s", [NL, E])
        gcol, gateW = sb("gcol", [P, 2]), sb("gateW", [P, 2, H0])
        wqkv_s, wo_s = sb("wqkv_s", [P, DEPTH, 3 * INNER]), sb("wo_s", [P, DEPTH, INNER // P, E])
        w1_s, w2_s = sb("w1_s", [P, DEPTH, 2 * HID]), sb("w2_s", [P, DEPTH, len(HC), E])
        b1_s, b2_s = sb("b1_s", [P, DEPTH, 2, len(HC)]), sb("b2_s", [P, DEPTH, E])
        lng_s, lnb_s = sb("lng_s", [P, DEPTH]), sb("lnb_s", [P, DEPTH])
        qks = sb("qks", [P, DEPTH, 2, FD])
        rotf = sb("rotf", [P, DEPTH, 4, NT, FD])

        x_a, x1_a, xn_a = sb("x_a", [P, NT, E]), sb("x1_a", [P, NT, E]), sb("xn_a", [P, NT, E])
        stats_a, mv_a, rs_a = sb("stats_a", [P, NT, 6]), sb("mv_a", [P, NT, 2]), sb("rs_a", [P, 2, NT])
        kq_a = sb("kq_a", [P, 2, T])
        RING = 2
        Kst_a, Qst_a = sb("Kst_a", [ROWS, RING, 4, T], BF16), sb("Qst_a", [ROWS, RING, 4, T], BF16)
        V_a = sb("V_a", [P, NT, H0, D0 + 1])
        nmax_a, mparts_a = sb("nmax_a", [P, G, NT, 4]), sb("mparts_a", [P, G, NT, 2, 4])
        mhi_a, mT_a = sb("mhi_a", [P, G, NT, 4], BF16), sb("mT_a", [8, 2, T], BF16)
        PR_A = 8
        prob_a = sb("prob_a", [P, PR_A, T])
        res_a = prob_a[:, 0:2, :]
        parts_a = prob_a[:, 2:5, :].rearrange("p a t -> p (a t)").bitcast(BF16).rearrange("p (w c t) -> p w c t", w=2, t=T)
        og_a, rden_a = sb("og_a", [P, T]), sb("rden_a", [P, NT, 4])
        otok_a, oT_a, s_a = xn_a, sb("oT_a", [P, T]), sb("s_a", [P, T])
        lg_a, hot_a, sc_a = sb("lg_a", [P, NT, NX]), sb("hot_a", [P, NT, NX]), sb("sc_a", [P, NT, NX])
        before_a, mx_a = sb("before_a", [P, NT, NX]), sb("mx_a", [P, NT])
        hid_a = prob_a[:, 0:XC, :]
        y_a, th_a = sb("y_a", [P, T]), oT_a
        W1_s, W2_s = sb("W1_s", [P, 2, HX]), sb("W2_s", [P, 2, XC, E])

        minus_half = sb("minus_half", [P, NT])
        x_b, xn_b, x_f = sb("x_b", [P, NT, E]), sb("xn_b", [P, NT, E]), sb("x_f", [P, NT, E])
        stats_b, mv_b, rs_b = sb("stats_b", [P, NT, 6]), sb("mv_b", [P, NT, 2]), sb("rs_b", [P, 2, NT])
        xnT_b, hT = sb("xnT_b", [P, T]), sb("hT", [P, T])
        pool_b, psum_l = sb("pool_b", [P, 2, NL]), sb("psum_l", [P, 2, NL])
        V_b, V_l = sb("V_b", [P, NT, H0, D0 + 1]), sb("V_l", [P, 4, 32])
        nmax_b, mparts_b = sb("nmax_b", [P, G, NT, 4]), sb("mparts_b", [P, G, NT, 2, 4])
        mhi_b, mT_b = sb("mhi_b", [P, G, NT, 4], BF16), sb("mT_b", [8, 2, T], BF16)
        nmax_l, mhi_l = sb("nmax_l", [P, NT, LH]), sb("mhi_l", [P, NT, LH], BF16)
        mparts_l, mT_l = sb("mparts_l", [P, NT, 2, LH]), sb("mT_l", [2 * LH, T], BF16)
        PR_B = 4
        prob_b = sb("prob_b", [P, PR_B, T])
        res_b = prob_b[:, 0:3, :]
        og_b, rden_b = sb("og_b", [P, T]), sb("rden_b", [P, 32])
        loc_b, rem_b = sb("loc_b", [P, NT, E]), sb("rem_b", [P, NT, NL])
        gate_b = sb("gate_b", [P, NT, 2, H0])
        mix_b, s_b = sb("mix_b", [P, T]), sb("s_b", [P, T])
        kT = sb("kT", [P, FH // 2, 2, T])
        V_f = sb("V_f", [P, NT, FH, FD + 1])
        ss, rn = sb("ss", [P, 2, FH]), sb("rn", [P, 2, 3, 2 * FH])
        nmax_f, mhi_f = sb("nmax_f", [P, NT, FH]), sb("mhi_f", [P, NT, FH], BF16)
        mparts_f, mT_f = sb("mparts_f", [P, NT, 2, FH]), sb("mT_f", [P, T], BF16)
        rden_f = sb("rden_f", [P, 2, 2])
        AREA = RING * 4 * T + LH * (T + NL) // 2 + 3 * T
        area, used = sb("area", [P, AREA]), [0]

        def take_area(words, rows=P):
            used[0] += words
            assert used[0] <= AREA, used
            return area[0:rows, used[0] - words:used[0]]

        Kst_b, Qst_b = (take_area(RING * 4 * T // 2, ROWS).bitcast(BF16).rearrange("p (r h t) -> p r h t", r=RING, t=T)
                        for _ in range(2))
        Qst_l = take_area(LH * T // 2, ROWS).bitcast(BF16).rearrange("p (h t) -> p h t", t=T)
        Kst_l = take_area(LH * NL // 2, ROWS).bitcast(BF16).rearrange("p (h t) -> p h t", t=NL)
        assert 2 * SPLIT * T // 2 <= used[0]
        parts_b = area[:, 0:2 * SPLIT * T // 2].bitcast(BF16).rearrange("p (w c t) -> p w c t", w=2, t=T)
        qkg_b = take_area(3 * T).rearrange("p (w t) -> p w t", t=T)
        used[0] = 0
        qk_raw, sq = (take_area(4 * INNER).rearrange("p (b a n) -> p b a n", b=2, a=2) for _ in range(2))
        cosp = prob_b[:].rearrange("p r t -> p (r t)").rearrange("p (b a n) -> p b a n", b=2, a=2)
        qT = take_area(FH // 2 * T).rearrange("p (c t) -> p c t", t=T)
        used[0] = 0
        oT_f = take_area(INNER // P * T).rearrange("p (c t) -> p c t", t=T)
        gelu_f, u_f = take_area(T), take_area(len(HC) * T).rearrange("p (c t) -> p c t", t=T)
        otok_f = sb("otok_f", [P, 2, NT, P])
        parts_l = otok_f[:].rearrange("p c t d -> p (c t d)")[:, 0:SPLIT * T // 2].bitcast(BF16).rearrange("p (c t) -> p c t", t=T)
        qk_rot = otok_f[:].rearrange("p c t d -> p (c t d)").rearrange("p (a n) -> p a n", a=2)

        def scratch(name, shape):
            return nc.dram_tensor(name, shape, BF16, kind="Internal").ap()

        dq_a, dk_a = scratch("dq_a", [H0, SPLIT, D0, SPLIT, T]), scratch("dk_a", [H0, SPLIT, D0, SPLIT, T])
        dq_b, dk_b = scratch("dq_b", [H0, SPLIT, D0, SPLIT, T]), scratch("dk_b", [H0, SPLIT, D0, SPLIT, T])
        dq_l, dk_l = scratch("dq_l", [LH, SPLIT, D0, SPLIT, T]), scratch("dk_l", [LH, SPLIT, D0, SPLIT, NL])

        acc_a, acc_b = banks[3], banks[7]

        s_weights, s_setup, s_zeroed = sem("weights"), sem("setup"), sem("zeroed")
        rotary = prob_a[:, 0:2, :].rearrange("p a t -> p (a t)").rearrange("p (a t d) -> p a t d", a=4, d=FD)
        with nc.Block() as block:
            @block.sync
            def _(sp):
                loads = [(ident[:], consts["ident"]), (ident_bf[:], consts["ident_bf"]),
                         (win_q[:], consts["win_q"]), (win_k[:], consts["win_k"]),
                         (band_q[:], consts["band_q"]), (band_k[:], consts["band_k"]),
                         (lat_q[:], consts["lat_q"].rearrange("p (t l) -> p t l", l=NL)), (lat_k[:], consts["lat_k"]),
                         (blocks[:], consts["blocks"]), (pick[:], consts["pick"].rearrange("p (h k) -> p h k", k=P)),
                         (rotary, consts["rotary"].rearrange("p (a t d) -> p a t d", a=4, d=FD)),
                         (att_c[:], att_w.rearrange("h d e -> (h d) e")), (wv0_s[:], wv0T), (wo0_s[:], wo0T),
                         (bv0[:], wv0_b.partition_broadcast(P)), (bo0[:], wo0_b.partition_broadcast(P)),
                         (Wg_s[:], Wg), (bg_s[:], bg.partition_broadcast(P)),
                         (wq_s[:], wq), (wk_s[:], wk), (wv_s[:], wv), (w_out_s[:], w_out),
                         (wgqk_s[:], wgqk), (wgv_s[:], wgv), (r_out_s[:], r_out),
                         (gcol[:, 0:1], gate_l.rearrange("h (d o) -> (h d) o", o=1)),
                         (gcol[:, 1:2], gate_r.rearrange("h (d o) -> (h d) o", o=1)),
                         (wqkv_s[:], wqkv.rearrange("l d n -> d l n")),
                         (wo_s[:], wo.rearrange("l (c p) d -> p l c d", p=P)),
                         (w1_s[:], w1.rearrange("l d n -> d l n")),
                         (Kst_a[STACK:ROWS, :, :, :].rearrange("p r h t -> p (r h t)"), consts["ones_bf"])]
                for l in range(DEPTH):
                    loads += [(dst[:, l:l + 1], src[l, :].rearrange("(d o) -> d o", o=1)) for dst, src in ((lng_s, ln_g), (lnb_s, ln_b))]
                    loads += [(b2_s[:, l, :], b2[l, :].partition_broadcast(P)),
                              (qks[:, l, 0, :], q_sc[l, :].partition_broadcast(P)),
                              (qks[:, l, 1, :], k_sc[l, :].partition_broadcast(P))]
                    for c, (c0, n) in enumerate(HC):
                        loads += [(w2_s[0:n, l, c, :], w2[l, c0:c0 + n, :])]
                        loads += [(b1_s[0:n, l, half, c:c + 1],
                                   b1[l, half * HID + c0:half * HID + c0 + n].rearrange("(p o) -> p o", o=1))
                                  for half in range(2)]
                for dst, src in loads:
                    sp.dma_start(dst, src).then_inc(s_weights, 16)
                sp.wait_ge(s_weights, 16 * len(loads))
                sp.sem_inc(s_setup, 1)

            @block.vector
            def _(dve):
                nc.vector.memset(acc_a[:], 0.0)
                nc.vector.memset(acc_b[:], 0.0)
                for tile in (V_l[:], kT[:], mT_f[:], hT[64:P, 0:1], x1_a[:]):
                    last = nc.vector.memset(tile, 0.0)
                for tile in (V_a[:, :, :, D0:D0 + 1], V_b[:, :, :, D0:D0 + 1], V_f[:, :, :, FD:FD + 1]):
                    last = nc.vector.memset(tile, 1.0)
                nc.vector.memset(minus_half[:], -0.5)
                last.then_inc(s_zeroed, 1)
                dve.wait_ge(s_zeroed, 1)
                nc.vector.memset(V_l[0:64, :, D0:D0 + 1], 1.0)
                nc.vector.memset(V_l[64:P, :, 16 + D0:16 + D0 + 1], 1.0)
                dve.wait_ge(s_setup, 1)
                blk = blocks[:].unsqueeze(2).to_broadcast([P, H0, D0])
                nc.vector.tensor_tensor(attW[:].rearrange("p (h e) -> p h e", e=D0), blk,
                                        att_c[:].unsqueeze(1).to_broadcast([P, H0, D0]), ALU.mult)
                for g in range(2):
                    nc.vector.tensor_scalar(gateW[:, g, :], blocks[:], gcol[:, g:g + 1], None, ALU.mult)
                for l in range(DEPTH):
                    for a in range(2):
                        s = qks[:, l, a, :].unsqueeze(1)
                        nc.vector.tensor_tensor(rotf[:, l, 2 * a], rotary[:, 2 * a],
                                                s.to_broadcast([P, NT, FD]), ALU.mult)
                        for lo in (0, FD // 2):
                            hi = FD // 2 - lo
                            nc.vector.tensor_tensor(
                                rotf[:, l, 2 * a + 1, :, lo:lo + 32], rotary[:, 2 * a + 1, :, lo:lo + 32],
                                s[:, :, hi:hi + 32].to_broadcast([P, NT, 32]), ALU.mult)

        def engine_sems(p):
            return {e: sem(f"{p}_emptied_by_{e}") for e in ("act", "dve")}

        a_x_in, a_xn, a_split, a_spill = (sem(n) for n in ("a_x_in", "a_xn", "a_split", "a_spill"))
        a_stack = [sem(f"a_stack{g}") for g in range(G)]
        a_mparts, a_mrow = sem("a_mparts"), [sem(f"a_mrow{g}") for g in range(G)]
        a_av, a_og, a_tanh, a_x1 = (sem(n) for n in ("a_av", "a_og", "a_tanh", "a_x1"))
        a_w = [sem("a_expert0"), sem("a_expert1")]
        a_filled, a_emptied = sem("a_filled"), engine_sems("a")
        h_filled, h_emptied, h_mparts = sem("h_filled"), engine_sems("h"), sem("h_mparts")
        a_dve_step = sem("a_dve_step")
        b_x, b_xn, b_pool, b_split, b_spill, b_lspill = (sem(n) for n in ("b_x", "b_xn", "b_pool", "b_split", "b_spill", "b_lspill"))
        b_ones, b_lstack = sem("b_ones"), sem("b_lstack")
        b_stack = [sem(f"b_stack{g}") for g in range(G)]
        b_mparts, b_mrow = sem("b_mparts"), [sem(f"b_mrow{g}") for g in range(G)]
        b_lmparts, b_lmrow = sem("b_lmparts"), sem("b_lmrow")
        b_av, b_og, b_gate, b_mix = (sem(n) for n in ("b_av", "b_og", "b_gate", "b_mix"))
        b_filled, b_emptied = sem("b_filled"), engine_sems("b")
        b_dve_step, b_pool_step = sem("b_dve_step"), sem("b_pool_step")
        a_var, a_rstd, b_var, b_rstd = sem("a_var"), sem("a_rstd"), sem("b_var"), sem("b_rstd")
        f_sq, f_cos, f_turned, f_rot, f_mparts = (sem(n) for n in ("f_sq", "f_cos", "f_turned", "f_rot", "f_mparts"))
        f_x, f_wo, f_mid, f_w2 = (sem(n) for n in ("f_x", "f_wo", "f_mid", "f_w2"))
        b_tanh, b_out, b_stored = sem("b_tanh"), sem("b_out"), sem("b_stored")

        first = [[("first", g, j, t) for j in range(4) for t in range(NT)] for g in range(G)]
        second = [[("second", g, k, j) for k in range(NT) for j in range(4)] for g in range(G)]
        plan_head = [("xnT", ["act"]), ("xw", ["act"]), ("v", ["dve"]), ("logits", ["dve"])]
        plan_head += [(f, ["dve"]) for f in first[0]] + [(("mT", 0), ["act"])]
        plan_a = []

        def plan_experts(e0, e1):
            return sum(([(("hid", e, c), ["act"]) for c in range(XC)] + [(("y", e), ["dve"])] for e in range(e0, e1)), [])

        for g in range(G):
            for n in range(16):
                if g + 1 < G:
                    plan_a.append((first[g + 1][n], ["dve"]))
                plan_a.append((second[g][n], ["act"]))
            if g + 1 < G:
                plan_a.append((("mT", g + 1), ["act"]))
            plan_a.append((("oT", g), ["dve"]))
        plan_a += plan_experts(0, EARLY) + [("otokT", ["act"]), ("proj", ["dve"])] + plan_experts(EARLY, NX)
        bfirst = [[("first", g, t, h) for t in range(NT) for h in range(2)] for g in range(G)]
        bsecond = [[("second", g, k, h) for k in range(NT) for h in range(2)] for g in range(G)]
        plan_b = [("xnT", ["act"]), ("q", ["act"]), ("k", ["act"]), ("gqk", ["act", "dve"]),
                  ("v", ["act"]), ("gv", ["act"]), ("gates", ["act"])]
        plan_b += [(f, ["dve"]) for f in bfirst[0]] + [(("mT", 0), ["act"])]
        plan_b += [(("lfirst", t), ["dve"]) for t in range(NT)] + [("lmT", ["act"])]
        for g in range(G):
            for n in range(8):
                if g + 1 < G:
                    plan_b.append((bfirst[g + 1][n], ["dve"]))
                plan_b.append((bsecond[g][n], ["act"]))
            if g + 1 < G:
                plan_b.append((("mT", g + 1), ["act"]))
            plan_b.append((("oT", g), ["dve"]))
        plan_b += [(("lsecond", u), ["act"]) for u in range(4)] + [("loT", ["dve"]), ("remT", ["act"])]
        plan_b += [("rproj", ["dve"]), ("mixT", ["act"]), ("wout", ["act"])]
        for l in range(DEPTH):
            for t in range(NT):
                plan_b += [(("fq", l, t), ["act"]), (("fk", l, t), ["act"]), (("fv", l, t), ["act"])]
                if t >= 2:
                    plan_b += [(("qkT", l, t - 2, a), ["act"]) for a in range(2)]
            plan_b += [(("qkT", l, t, a), ["act"]) for t in range(NT - 2, NT) for a in range(2)]
            plan_b += [(("ffirst", l, t, c), ["dve"]) for t in range(NT) for c in range(FH // 2)]
            plan_b += [(("fmT", l), ["act"])]
            for n in range(UNITS + 2):
                if n < UNITS:
                    plan_b.append((("fsecond", l, n), ["act"]))
                if n % NT == 1 and n > NT:
                    plan_b.append((("foT", l, n // NT - 1), ["act"]))
                if 0 < n <= UNITS:
                    plan_b.append((("fav", l, n - 1), ["dve"]))
            plan_b += [(("fx", l), ["act"]), (("fback", l), ["dve"]), (("fnT", l), ["dve"])]
            for c in range(len(HC)):
                plan_b += [(("fg", l, c), ["act"]), (("fa", l, c), ["dve"])]
            if l + 1 < DEPTH:
                plan_b += [(("fnext", l), ["act"])]
        BA = Banks(banks[0:3], a_filled, a_emptied, plan_a)
        BH = Banks(banks[0:3], h_filled, h_emptied, plan_head)
        BB = Banks(banks[4:7], b_filled, b_emptied, plan_b)

        def transposes(dst, src, n=E, inc=None):
            for t in range(NT):
                last = nc.tensor.transpose(dst[0:n, t * P:(t + 1) * P], src[:, t, :], ident[:])
            last.then_inc(inc, 1)

        def chain(eng, s):
            count = [0]

            def link(ins):
                count[0] += 1
                ins.then_inc(s, 1)
                eng.wait_ge(s, count[0])
            return link

        def rsqrt(link, v, y, t):
            link(nc.vector.tensor_scalar(y.bitcast(I32), v.bitcast(I32), 1, None, ALU.logical_shift_right))
            link(nc.vector.tensor_scalar(y.bitcast(I32), y.bitcast(I32), -1.0, RSQRT_MAGIC, ALU.mult, ALU.add))
            for _ in range(3):
                link(nc.vector.scalar_tensor_tensor(out=t, in0=v, scalar=-0.5, in1=y, op0=ALU.mult, op1=ALU.mult))
                link(nc.vector.tensor_tensor(t, t, y, ALU.mult))
                link(nc.vector.scalar_tensor_tensor(out=y, in0=t, scalar=1.5, in1=y, op0=ALU.add, op1=ALU.mult))

        def layernorm(link, src, dst, stats, mv, rs, inc, var, rstd, count):
            for t in range(NT):
                last = nc.vector.bn_stats(stats[:, t, :], src[:, t, :])
            link(last)
            for t in range(NT):
                last = nc.vector.bn_aggr(mv[:, t, :], stats[:, t, :])
            link(last)
            nc.vector.tensor_scalar(rs[:, 0, :], mv[:, :, 1], EPS, None, ALU.add).then_inc(var, 1)
            nc.vector.wait_ge(rstd, count)
            for t in range(NT):
                last = nc.vector.tensor_scalar(dst[:, t, :], src[:, t, :], mv[:, t, 0:1], rs[:, 1, t:t + 1],
                                               ALU.subtract, ALU.mult)
            last.then_inc(inc, 1)

        def split(link, src, res, parts, inc):
            link(nc.vector.tensor_copy(parts[0], src))
            link(nc.vector.tensor_tensor(res, src, parts[0], ALU.subtract))
            link(nc.vector.tensor_copy(parts[1], res))
            link(nc.vector.tensor_tensor(res, res, parts[1], ALU.subtract))
            nc.vector.tensor_copy(parts[2], res).then_inc(inc, 1)

        def split_max(link, nmax, mhi, parts, inc):
            link(nc.vector.tensor_copy(mhi, nmax))
            nc.vector.tensor_copy(parts[0], mhi)
            nc.vector.tensor_tensor(parts[1], nmax, mhi, ALU.subtract).then_inc(inc, 1)

        def spill(sp, parts_q, parts_k, dq, dk, s):
            for i in range(SPLIT):
                sp.dma_start(dq[:, i, :, 0:SPLIT - i, :], parts_q[:, i:SPLIT, :]).then_inc(s, 16)
                if i:
                    sp.dma_start(dq[:, i, :, SPLIT - i:SPLIT, :], parts_q[:, 0:i, :]).then_inc(s, 16)
                sp.dma_start(dk[:, i], parts_k).then_inc(s, 16)

        SPILLED, STACKED = 8 * 16, 2 * 16

        def load_stack(sp, dq, dk, h, n, Qst, Kst, s):
            for stack, d in ((Qst, dq), (Kst, dk)):
                sp.dma_start(stack[0:STACK], d[h:h + n].rearrange("h i d c t -> (i d c) h t")).then_inc(s, 16)

        def max_to_stack(sp, mT, Qst, landed):
            sp.dma_start(Qst[STACK:ROWS, :, :], mT).then_inc(landed, 16)

        def a_stack_load(sp, g):
            load_stack(sp, dq_a, dk_a, 4 * g, 4, Qst_a[:, g % RING], Kst_a[:, g % RING], a_stack[g])

        def head_sync(sp, b, after_body):
            yield A_NEXT
            if after_body:
                sp.wait_ge(a_x1, 1)
            sp.dma_start(x_a[:], x_in[b, :, :].rearrange("o (n p) f -> p (o n) f", p=P)).then_inc(a_x_in, 16)
            yield A_NEXT + 12
            sp.wait_ge(a_split, 1)
            spill(sp, parts_a[:, 1], parts_a[:, 0], dq_a, dk_a, a_spill)
            sp.wait_ge(a_spill, SPILLED)
            for g in range(RING):
                a_stack_load(sp, g)
            yield A_NEXT + 30
            sp.wait_ge(*BH.brought(("mT", 0), "act"))
            max_to_stack(sp, mT_a[:, 0, :], Qst_a[:, 0], a_mrow[0])
            for landed, count in ((a_stack[0], STACKED), (a_stack[1], STACKED), (a_mrow[0], 16)):
                sp.wait_ge(landed, count)

        def a_sync(sp):
            def experts(e0, e1):
                for e in range(e0, e1):
                    yield A_EXPERT[e] - 9
                    if e >= 2:
                        sp.wait_ge(*BA.made(("y", e - 2)))
                    sp.dma_start(W1_s[:, e % 2, :], W1[e]).then_inc(a_w[e % 2], 16)
                    sp.dma_start(W2_s[:, e % 2], W2[e].rearrange("(c p) d -> p c d", p=P)).then_inc(a_w[e % 2], 16)

            for g in range(G):
                yield A_GROUP[g] - 1
                if g:
                    sp.wait_ge(*BA.brought(("mT", g), "act"))
                    max_to_stack(sp, mT_a[:, g % 2, :], Qst_a[:, g % RING], a_mrow[g])
                if g + RING < G:
                    yield A_GROUP[g] + 19
                    sp.wait_ge(*BA.made(second[g][-1]))
                    a_stack_load(sp, g + RING)
            yield from experts(0, NX)

        def head_tensor(pe, after_body):
            yield A_NEXT + 2
            pe.wait_ge(a_xn, 1)
            if after_body:
                pe.wait_ge(*BA.brought(("y", NX - 1), "dve"))
            transposes(BH.take(pe, "xnT"), xn_a, inc=h_filled)
            yield A_NEXT + 4
            pe.wait_ge(*BH.brought("xnT", "act"))
            nc.tensor.matmul(BH.take(pe, "xw")[:], attW[:], kq_a[:, 0, :], start=True, stop=True).then_inc(h_filled, 1)
            ps = BH.take(pe, "v")
            for t in range(NT):
                last = nc.tensor.matmul(ps[:, t * E:(t + 1) * E], kq_a[:, 0, t * P:(t + 1) * P], wv0_s[:], start=True, stop=True)
            last.then_inc(h_filled, 1)
            ps = BH.take(pe, "logits")
            for t in range(NT):
                last = nc.tensor.matmul(ps[:, t * NX:(t + 1) * NX], kq_a[:, 0, t * P:(t + 1) * P], Wg_s[:], start=True, stop=True)
            last.then_inc(h_filled, 1)
            for n, f in enumerate(first[0]):
                _, _, j, t = f
                yield A_NEXT + 16 + 0.7 * n
                if n == 0:
                    pe.wait_ge(a_stack[0], STACKED)
                nc.tensor.matmul(BH.take(pe, f)[:], Qst_a[0:STACK, 0, j, t * P:(t + 1) * P],
                                 Kst_a[0:STACK, 0, j, :], start=True, stop=True).then_inc(h_filled, 1)
            yield A_NEXT + 29
            pe.wait_ge(h_mparts, 1)
            transposes(BH.take(pe, ("mT", 0)), mparts_a[:, 0].rearrange("p t a j -> p t (a j)"), 8, h_filled)

        def a_tensor(pe):

            def first_pass(g, n):
                _, _, j, t = f = first[g][n]
                if n == 0 and g >= RING:
                    pe.wait_ge(a_stack[g], STACKED)
                nc.tensor.matmul(BA.take(pe, f)[:], Qst_a[0:STACK, g % RING, j, t * P:(t + 1) * P],
                                 Kst_a[0:STACK, g % RING, j, :], start=True, stop=True).then_inc(a_filled, 1)

            def max_rows(g):
                pe.wait_ge(a_mparts, g)
                transposes(BA.take(pe, ("mT", g)), mparts_a[:, g].rearrange("p t a j -> p t (a j)"), 8, a_filled)

            def values(g, k):
                pe.wait_ge(*BA.brought(("second", g, k, 3), "act"))
                if k == 0:
                    if g:
                        pe.wait_ge(a_og, g)
                for j in range(4):
                    last = nc.tensor.matmul(acc_a[32 * j:32 * j + D0 + 1, :], V_a[:, k, 4 * g + j, :],
                                            prob_a[:, (4 * k + j) % PR_A, :], start=(k == 0), stop=(k == NT - 1))
                last.then_inc(a_av, 1)

            def experts(e0, e1):
                for e in range(e0, e1):
                    for c in range(XC):
                        yield A_EXPERT[e] + c
                        if c == 0:
                            pe.wait_ge(a_w[e % 2], 32 * (e // 2 + 1))
                        nc.tensor.matmul(BA.take(pe, ("hid", e, c))[:], W1_s[:, e % 2, c * P:(c + 1) * P], kq_a[:, 0, :],
                                         start=True, stop=True).then_inc(a_filled, 1)
                    yield A_EXPERT[e] + 5.5
                    pe.wait_ge(*BA.brought(("hid", e, XC - 1), "act"))
                    ps = BA.take(pe, ("y", e))
                    for t in range(NT):
                        for c in range(XC):
                            last = nc.tensor.matmul(ps[:, t * E:(t + 1) * E], hid_a[:, c, t * P:(t + 1) * P],
                                                    W2_s[:, e % 2, c, :], start=(c == 0), stop=(c == XC - 1))
                    last.then_inc(a_filled, 1)

            for g in range(G):
                for n in range(16):
                    yield A_GROUP[g] + 1.2 * n
                    if g + 1 < G:
                        first_pass(g + 1, n)
                    if n == 0 and g:
                        pe.wait_ge(a_mrow[g], 16)
                    _, _, k, j = s = second[g][n]
                    nc.tensor.matmul(BA.take(pe, s)[:], Kst_a[:, g % RING, j, k * P:(k + 1) * P], Qst_a[:, g % RING, j, :],
                                     start=True, stop=True).then_inc(a_filled, 1)
                    if n % 4 == 1 and n > 4:
                        values(g, n // 4 - 1)
                yield A_GROUP[g] + 20
                values(g, 3)
                if g + 1 < G:
                    max_rows(g + 1)
                yield A_GROUP[g] + 21
                pe.wait_ge(a_og, g + 1)
                transposes(BA.take(pe, ("oT", g)), og_a[:].rearrange("p (t q) -> p t q", q=P), inc=a_filled)
            yield from experts(0, EARLY)
            yield A_PROJ
            pe.wait_ge(*BA.brought(("oT", G - 1), "dve"))
            transposes(BA.take(pe, "otokT"), otok_a, inc=a_filled)
            yield A_PROJ + 2
            pe.wait_ge(*BA.brought("otokT", "act"))
            ps = BA.take(pe, "proj")
            for t in range(NT):
                last = nc.tensor.matmul(ps[:, t * E:(t + 1) * E], oT_a[:, t * P:(t + 1) * P], wo0_s[:], start=True, stop=True)
            last.then_inc(a_filled, 1)
            yield from experts(EARLY, NX)

        def head_gpsimd(pool):
            yield A_NEXT + 1
            pool.wait_ge(a_var, 1)
            nc.gpsimd.tensor_tensor(rs_a[:, 1, :], rs_a[:, 0, :], minus_half[:], ALU.pow).then_inc(a_rstd, 1)

        def head_scalar(act):
            yield A_NEXT + 3
            for n, product in enumerate(("xnT", "xw")):
                nc.scalar.activation(kq_a[:, n, :], BH.full(act, product)[:], ACT.Copy).then_inc(h_emptied["act"], 1)
                if n == 0:
                    yield A_NEXT + 5
            yield A_NEXT + 29.5
            nc.scalar.activation(mT_a[:, 0, :], BH.full(act, ("mT", 0))[0:8, :], ACT.Copy).then_inc(h_emptied["act"], 1)

        def a_scalar(act):
            def bring(product, dst, func=ACT.Copy, rows=P, **kw):
                nc.scalar.activation(dst, BA.full(act, product)[0:rows, :], func, **kw).then_inc(a_emptied["act"], 1)

            def experts(e0, e1):
                for e in range(e0, e1):
                    for c in range(XC):
                        yield A_EXPERT[e] + c
                        if c == 0:
                            if e:
                                act.wait_ge(*BA.made(("y", e - 1)))
                            else:
                                act.wait_ge(a_av, 4 * G)
                        bring(("hid", e, c), hid_a[:, c, :], ACT.Gelu_apprx_tanh)

            for g in range(G):
                for n in range(16):
                    yield A_GROUP[g] + 1.2 * n
                    if n % 4 == 0 and 4 * g + n // 4 >= 2:
                        act.wait_ge(a_av, 4 * g + n // 4 - 1)
                    bring(second[g][n], prob_a[:, n % PR_A, :], ACT.Exp, scale=HEAD_SCALE)
                yield A_GROUP[g] + 20
                if g + 1 < G:
                    if g >= 2:
                        act.wait_ge(a_mrow[g - 1], 16)
                    bring(("mT", g + 1), mT_a[:, (g + 1) % 2, :], rows=8)
                act.wait_ge(a_av, 4 * g + 4)
                if g:
                    act.wait_ge(*BA.made(("oT", g - 1)))
                nc.scalar.activation(og_a[:], acc_a[:], ACT.Copy).then_inc(a_og, 1)
            yield from experts(0, EARLY)
            yield A_PROJ
            bring("otokT", oT_a[:])
            yield from experts(EARLY, NX)
            yield A_END
            act.wait_ge(*BA.made("proj"))
            act.wait_ge(*BA.brought(("y", NX - 1), "dve"))
            nc.scalar.activation(th_a[:], y_a[:], ACT.Tanh, scale=0.5).then_inc(a_tanh, 1)

        def head_vector(dve, link):
            emptied = h_emptied["dve"]
            yield A_NEXT + 1
            dve.wait_ge(a_x_in, 16)
            layernorm(link, x_a, xn_a, stats_a, mv_a, rs_a, a_xn, a_var, a_rstd, 1)
            yield A_NEXT + 6
            ps = BH.full(dve, "v")
            nc.vector.tensor_tensor(V_a[:, :, :, 0:D0], ps[:].rearrange("p (t h d) -> p t h d", t=NT, d=D0),
                                    bv0[:].rearrange("p (h d) -> p h d", d=D0).unsqueeze(1)
                                    .to_broadcast([P, NT, H0, D0]), ALU.add).then_inc(emptied, 1)
            ps = BH.full(dve, "logits")
            nc.vector.tensor_tensor(lg_a[:], ps[:, 0:NT * NX].rearrange("p (t e) -> p t e", e=NX),
                                    bg_s[:].unsqueeze(1).to_broadcast([P, NT, NX]), ALU.add).then_inc(emptied, 1)
            dve.wait_ge(*BH.brought("logits", "dve"))
            link(nc.vector.tensor_reduce(out=mx_a[:], in_=lg_a[:], op=ALU.max, axis=AX.X))
            link(nc.vector.tensor_tensor(sc_a[:], lg_a[:], mx_a[:].unsqueeze(2).to_broadcast([P, NT, NX]), ALU.is_equal))
            link(nc.vector.memset(before_a[:, :, 0:1], 0.0))
            for e in range(1, NX):
                link(nc.vector.tensor_tensor(before_a[:, :, e:e + 1], before_a[:, :, e - 1:e], sc_a[:, :, e - 1:e], ALU.max))
            link(nc.vector.tensor_scalar(before_a[:], before_a[:], -1.0, 1.0, ALU.mult, ALU.add))
            link(nc.vector.tensor_tensor(hot_a[:], before_a[:], sc_a[:], ALU.mult))
            yield A_NEXT + 7
            dve.wait_ge(*BH.brought("xw", "act"))
            split(link, kq_a[:], res_a, [parts_a[:, :, c, :] for c in range(SPLIT)], a_split)
            for n, f in enumerate(first[0]):
                _, _, j, t = f
                yield A_NEXT + 16 + 0.7 * n
                nc.vector.tensor_reduce(out=nmax_a[:, 0, t, j:j + 1], in_=BH.full(dve, f)[:], op=ALU.max, axis=AX.X,
                                        negate=True).then_inc(emptied, 1)
            yield A_NEXT + 28
            dve.wait_ge(*BH.brought(first[0][-1], "dve"))
            split_max(link, nmax_a[:, 0], mhi_a[:, 0], [mparts_a[:, 0, :, p, :] for p in range(2)], h_mparts)

        def a_vector(dve, link, beside_b):
            emptied = a_emptied["dve"]

            def first_pass(g, n):
                _, _, j, t = f = first[g][n]
                nc.vector.tensor_reduce(out=nmax_a[:, g, t, j:j + 1], in_=BA.full(dve, f)[:], op=ALU.max, axis=AX.X,
                                        negate=True).then_inc(emptied, 1)

            def max_parts(g):
                dve.wait_ge(*BA.brought(first[g][-1], "dve"))
                split_max(link, nmax_a[:, g], mhi_a[:, g], [mparts_a[:, g, :, p, :] for p in range(2)], a_mparts)

            def experts(e0, e1):
                for e in range(e0, e1):
                    yield A_EXPERT[e] + 6.5
                    ps = BA.full(dve, ("y", e))
                    if e:
                        dve.wait_ge(*BA.brought(("y", e - 1), "dve"))
                    for t in range(NT):
                        y, src, hot = y_a[:, t * E:(t + 1) * E], ps[:, t * E:(t + 1) * E], hot_a[:, t, e:e + 1]
                        if e == 0:
                            last = nc.vector.tensor_scalar(y, src, hot, None, ALU.mult)
                        else:
                            last = nc.vector.scalar_tensor_tensor(out=y, in0=src, scalar=hot, in1=y, op0=ALU.mult, op1=ALU.add)
                    last.then_inc(emptied, 1)

            for g in range(G):
                for n in range(16):
                    yield A_GROUP[g] + 1.2 * n
                    if g + 1 < G:
                        first_pass(g + 1, n)
                yield A_GROUP[g] + 19.5
                if g + 1 < G:
                    max_parts(g + 1)
                yield A_GROUP[g] + 21
                ps = BA.full(dve, ("oT", g))[:].rearrange("p (t j c) -> p t j c", t=NT, c=32)
                link(nc.vector.reciprocal(rden_a[:], ps[:, :, :, D0]))
                nc.vector.tensor_tensor(otok_a[:, :, 32 * g:32 * g + 32].rearrange("p t (j d) -> p t j d", d=D0),
                                        ps[:, :, :, 0:D0], rden_a[:].unsqueeze(3).to_broadcast([P, NT, 4, D0]),
                                        ALU.mult).then_inc(emptied, 1)
            yield from experts(0, EARLY)
            yield A_PROJ + 3
            tiles = "p (t e) -> p t e"
            ps = BA.full(dve, "proj")
            nc.vector.tensor_tensor(s_a[:].rearrange(tiles, e=E), ps[:].rearrange(tiles, e=E),
                                    bo0[:].unsqueeze(1).to_broadcast([P, NT, E]), ALU.add).then_inc(emptied, 1)
            yield from experts(EARLY, NX)
            yield A_END + 1
            dve.wait_ge(a_tanh, 1)
            link(nc.vector.scalar_tensor_tensor(out=th_a[:], in0=th_a[:], scalar=1.0, in1=y_a[:], op0=ALU.add, op1=ALU.mult))
            link(nc.vector.tensor_tensor(th_a[:], th_a[:], s_a[:], ALU.mult))
            if beside_b:
                dve.wait_ge(b_x, 1)
            nc.vector.scalar_tensor_tensor(out=x1_a[:].rearrange("p t e -> p (t e)"), in0=th_a[:], scalar=0.5,
                                           in1=x_a[:].rearrange("p t e -> p (t e)"), op0=ALU.mult, op1=ALU.add).then_inc(a_x1, 1)

        def b_sync(sp):
            yield 4
            sp.wait_ge(b_split, 1)
            spill(sp, parts_b[:, 0], parts_b[:, 1], dq_b, dk_b, b_spill)
            sp.wait_ge(b_spill, SPILLED)
            def stack(g):
                load_stack(sp, dq_b, dk_b, 4 * g, 4, Qst_b[:, g % RING], Kst_b[:, g % RING], b_stack[g])

            stack(0)
            yield 5
            sp.wait_ge(b_split, 2)
            spill(sp, parts_l[0:64], parts_l[64:P, :, 0:NL], dq_l, dk_l, b_lspill)
            sp.wait_ge(b_lspill, SPILLED)
            sp.dma_start(Kst_b[STACK:ROWS].rearrange("p r h t -> p (r h t)"), consts["ones_bf"]).then_inc(b_ones, 16)
            sp.dma_start(Kst_l[STACK:ROWS].rearrange("p h t -> p (h t)"), consts["ones_bf"][:, 0:LH * NL]).then_inc(b_ones, 16)
            load_stack(sp, dq_l, dk_l, 0, LH, Qst_l, Kst_l, b_lstack)
            stack(1)
            yield B_AT + 11
            sp.wait_ge(*BB.brought(("mT", 0), "act"))
            max_to_stack(sp, mT_b[:, 0, :], Qst_b[:, 0], b_mrow[0])
            sp.wait_ge(*BB.brought("lmT", "act"))
            max_to_stack(sp, mT_l[:], Qst_l, b_lmrow)
            for g in range(G):
                if g + 1 < G:
                    yield B_AT + 23 + 12 * g
                    sp.wait_ge(*BB.made(bsecond[g][-1]))
                    if g + RING < G:
                        stack(g + RING)
                    sp.wait_ge(*BB.brought(("mT", g + 1), "act"))
                    max_to_stack(sp, mT_b[:, (g + 1) % 2, :], Qst_b[:, (g + 1) % RING], b_mrow[g + 1])

        def finish_sync(sp, row):
            yield FINISH + 3
            sp.wait_ge(b_out, 1)
            sp.dma_start(out[row, :, :].rearrange("o (n p) f -> p (o n) f", p=P), x_f[:]).then_inc(b_stored, 16)
            yield LAYER_AT
            sp.wait_ge(b_stored, 16)

        def b_gpsimd(pool, after_finish):
            def inverse_root(n):
                pool.wait_ge(b_var, n)
                nc.gpsimd.tensor_tensor(rs_b[:, 1, :], rs_b[:, 0, :], minus_half[:], ALU.pow).then_inc(b_rstd, 1)

            yield 0
            inverse_root(1)
            yield FINISH + 4
            if after_finish:
                pool.wait_ge(b_out, 1)
            nc.gpsimd.tensor_copy(x_b[:], x1_a[:]).then_inc(b_x, 1)
            for l in range(DEPTH):
                for t in range(NT):
                    yield LAYER_AT + LAYER * l + QKV * max(t - 1, 0) + t % 2 + 0.5
                    n = NT * l + t
                    pool.wait_ge(*BB.brought(("fk", l, t), "act"))
                    pool.wait_ge(f_sq, n + 1)
                    raw = qk_raw[:, t % 2].rearrange("p a (h d) -> p a h d", d=FD)
                    sin = sq[:, t % 2].rearrange("p a (h d) -> p a h d", d=FD)
                    for a in range(2):
                        for lo in (0, FD // 2):
                            hi = FD // 2 - lo
                            last = nc.gpsimd.tensor_tensor(
                                sin[:, a, :, lo:lo + 32], raw[:, a, :, hi:hi + 32],
                                rotf[:, l, 2 * a + 1, t, lo:lo + 32].unsqueeze(1).to_broadcast([P, FH, 32]), ALU.mult)
                    last.then_inc(b_pool_step, 1)
                    pool.wait_ge(b_pool_step, n + 1)
                    pool.wait_ge(f_cos, n + 1)
                    nc.gpsimd.tensor_tensor(cosp[:, t % 2], cosp[:, t % 2], sq[:, t % 2], ALU.add).then_inc(f_turned, 1)
                yield LAYER_AT + LAYER * l + 91
                inverse_root(l + 2)

        def b_tensor(pe):
            yield 1
            pe.wait_ge(b_xn, 1)
            transposes(BB.take(pe, "xnT"), xn_b, inc=b_filled)
            yield 2
            pe.wait_ge(*BB.brought("xnT", "act"))
            for product, w in (("q", wq_s), ("k", wk_s), ("gqk", wgqk_s)):
                nc.tensor.matmul(BB.take(pe, product)[:], w[:], xnT_b[:], start=True, stop=True).then_inc(b_filled, 1)
            yield 3
            ps = BB.take(pe, "v")
            for t in range(NT):
                last = nc.tensor.matmul(ps[:, t * E:(t + 1) * E], xnT_b[:, t * P:(t + 1) * P], wv_s[:], start=True, stop=True)
            last.then_inc(b_filled, 1)
            pe.wait_ge(b_pool, 1)
            nc.tensor.matmul(BB.take(pe, "gv")[:, 0:NL], pool_b[:].rearrange("p a l -> p (a l)"), wgv_s[:],
                             start=True, stop=True).then_inc(b_filled, 1)
            pe.wait_ge(*BB.brought("q", "act"))
            ps = BB.take(pe, "gates")
            for t in range(NT):
                last = nc.tensor.matmul(ps[:, t * 32:(t + 1) * 32], qkg_b[:, 0, t * P:(t + 1) * P],
                                        gateW[:].rearrange("p g h -> p (g h)"), start=True, stop=True)
            last.then_inc(b_filled, 1)

            def first_pass(g, n):
                _, _, t, hp = f = bfirst[g][n]
                if n == 0:
                    pe.wait_ge(b_stack[g], STACKED)
                skip = WIN if t == 0 else 0
                nk = LKEYS - skip
                k0 = t * P - WIN + skip
                ps = BB.take(pe, f)
                nc.tensor.matmul(ps[:, 0:2 * nk], ident_bf[:], win_q[:, skip:].unsqueeze(1).to_broadcast([P, 2, nk]),
                                 start=True, stop=False)
                for a in range(2):
                    last = nc.tensor.matmul(ps[:, a * nk:(a + 1) * nk], Qst_b[0:STACK, g % RING, 2 * hp + a, t * P:(t + 1) * P],
                                            Kst_b[0:STACK, g % RING, 2 * hp + a, k0:k0 + nk], start=False, stop=(a == 1))
                last.then_inc(b_filled, 1)

            def max_rows(g):
                pe.wait_ge(b_mparts, g + 1)
                transposes(BB.take(pe, ("mT", g)), mparts_b[:, g].rearrange("p t a j -> p t (a j)"), 8, b_filled)

            def values(g, k):
                pe.wait_ge(*BB.brought(("second", g, k, 1), "act"))
                if k == 0:
                    if g == 0:
                        pe.wait_ge(*BB.brought("v", "act"))
                    else:
                        pe.wait_ge(b_og, g)
                nq = min(LKEYS, T - k * P)
                for j in range(4):
                    last = nc.tensor.matmul(acc_b[32 * j:32 * j + D0 + 1, k * P:k * P + nq], V_b[:, k, 4 * g + j, :],
                                            prob_b[:, (2 * k + j // 2) % PR_B, (j % 2) * nq:(j % 2 + 1) * nq],
                                            start=(k == 0), stop=(k == NT - 1), skip_group_check=True)
                last.then_inc(b_av, 1)

            for n in range(8):
                yield B_AT + n
                first_pass(0, n)
            yield B_AT + 8
            max_rows(0)
            for t in range(NT):
                yield B_AT + 9 + t / 4
                if t == 0:
                    pe.wait_ge(b_lstack, STACKED)
                ps = BB.take(pe, ("lfirst", t))
                nc.tensor.matmul(ps[:], ident_bf[:], lat_q[:, t, :].unsqueeze(1).to_broadcast([P, LH, NL]), start=True, stop=False)
                for h in range(LH):
                    last = nc.tensor.matmul(ps[:, h * NL:(h + 1) * NL], Qst_l[0:STACK, h, t * P:(t + 1) * P],
                                            Kst_l[0:STACK, h, :], start=False, stop=(h == LH - 1))
                last.then_inc(b_filled, 1)
            yield B_AT + 10
            pe.wait_ge(b_lmparts, 1)
            transposes(BB.take(pe, "lmT"), mparts_l[:].rearrange("p t a h -> p t (a h)"), 2 * LH, b_filled)
            for g in range(G):
                for n in range(8):
                    yield B_AT + 13 + 12 * g + n
                    if g + 1 < G:
                        first_pass(g + 1, n)
                    if n == 0:
                        pe.wait_ge(b_mrow[g], 16)
                        pe.wait_ge(b_ones, 32)
                    _, _, k, hp = s = bsecond[g][n]
                    nq = min(LKEYS, T - k * P)
                    ps = BB.take(pe, s)
                    nc.tensor.matmul(ps[:, 0:2 * nq], ident_bf[:], win_k[:, 0:nq].unsqueeze(1).to_broadcast([P, 2, nq]),
                                     start=True, stop=False)
                    for a in range(2):
                        last = nc.tensor.matmul(ps[:, a * nq:(a + 1) * nq], Kst_b[:, g % RING, 2 * hp + a, k * P:(k + 1) * P],
                                                Qst_b[:, g % RING, 2 * hp + a, k * P:k * P + nq], start=False, stop=(a == 1))
                    last.then_inc(b_filled, 1)
                    if n % 2 == 0 and n:
                        values(g, n // 2 - 1)
                yield B_AT + 21 + 12 * g
                values(g, 3)
                if g + 1 < G:
                    max_rows(g + 1)
                yield B_AT + 22 + 12 * g
                pe.wait_ge(b_og, g + 1)
                transposes(BB.take(pe, ("oT", g)), og_b[:].rearrange("p (t q) -> p t q", q=P), inc=b_filled)
            for u in range(4):
                yield B_AT + 63 + u
                if u == 0:
                    pe.wait_ge(b_lmrow, 16)
                ps = BB.take(pe, ("lsecond", u))
                nc.tensor.matmul(ps[:], ident_bf[:], lat_k[:], start=True, stop=False, skip_group_check=True)
                for a in range(2):
                    last = nc.tensor.matmul(ps[64 * a:64 * a + 64, :], Kst_l[:, 2 * u + a, :], Qst_l[:, 2 * u + a, :],
                                            start=False, stop=(a == 1), skip_group_check=True)
                last.then_inc(b_filled, 1)
            yield B_AT + 67
            pe.wait_ge(*BB.brought(("lsecond", 3), "act"))
            pe.wait_ge(*BB.brought("gv", "act"))
            pe.wait_ge(b_og, G)
            for u in range(4):
                last = nc.tensor.matmul(acc_b[32 * u:32 * u + 32, :], V_l[:, u, :], prob_b[:, u, :], start=True, stop=True)
            last.then_inc(b_av, 1)
            yield B_AT + 68
            pe.wait_ge(b_og, G + 1)
            transposes(BB.take(pe, "loT"), og_b[:].rearrange("p (t q) -> p t q", q=P), inc=b_filled)
            yield B_AT + 69
            pe.wait_ge(*BB.brought("loT", "dve"))
            transposes(BB.take(pe, "remT"), rem_b, NL, b_filled)
            yield B_AT + 70
            pe.wait_ge(*BB.brought("remT", "act"))
            ps = BB.take(pe, "rproj")
            for t in range(NT):
                last = nc.tensor.matmul(ps[:, t * E:(t + 1) * E], og_b[0:NL, t * P:(t + 1) * P], r_out_s[:], start=True, stop=True)
            last.then_inc(b_filled, 1)
            yield B_AT + 71
            pe.wait_ge(b_mix, 1)
            transposes(BB.take(pe, "mixT"), mix_b[:].rearrange("p (t e) -> p t e", e=E), inc=b_filled)
            yield B_AT + 72
            pe.wait_ge(*BB.brought("mixT", "act"))
            ps = BB.take(pe, "wout")
            for t in range(NT):
                last = nc.tensor.matmul(ps[:, t * E:(t + 1) * E], og_b[:, t * P:(t + 1) * P], w_out_s[:], start=True, stop=True)
            last.then_inc(b_filled, 1)

            for l in range(DEPTH):
                s0 = LAYER_AT + LAYER * l

                def queries_keys_T(t):
                    pe.wait_ge(f_rot, NT * l + t + 1)
                    for a in range(2):
                        ps = BB.take(pe, ("qkT", l, t, a))
                        for c in range(FH // 2):
                            last = nc.tensor.transpose(ps[:, c * P:(c + 1) * P], qk_rot[:, a, c * P:(c + 1) * P], ident[:])
                        last.then_inc(b_filled, 1)

                for t in range(NT):
                    yield s0 + QKV * max(t - 1, 0) + t % 2
                    if l and t == 0:
                        pe.wait_ge(*BB.brought(("fnext", l - 1), "act"))
                    for n, product in enumerate(("fq", "fk", "fv")):
                        nc.tensor.matmul(BB.take(pe, (product, l, t))[:], hT[:, t * P:(t + 1) * P],
                                         wqkv_s[:, l, n * INNER:(n + 1) * INNER], start=True, stop=True).then_inc(b_filled, 1)
                    if t >= 2:
                        yield s0 + QKV * (t - 1) + 3
                        queries_keys_T(t - 2)
                for t in range(NT - 2, NT):
                    yield s0 + QKV * (t + 1) + 3
                    queries_keys_T(t)
                for t in range(NT):
                    for c in range(FH // 2):
                        yield s0 + 34 + 4 * t + c
                        if t == 0 and c == 0:
                            pe.wait_ge(*BB.brought(("qkT", l, NT - 1, 1), "act"))
                        skip = FW if t == 0 else 0
                        nk = FKEYS - skip
                        k0 = t * P - FW + skip
                        ps = BB.take(pe, ("ffirst", l, t, c))
                        nc.tensor.matmul(ps[:, 0:2 * nk], ident_bf[:], band_q[:, skip:].unsqueeze(1).to_broadcast([P, 2, nk]),
                                         start=True, stop=False)
                        for a in range(2):
                            last = nc.tensor.matmul(ps[:, a * nk:(a + 1) * nk], qT[:, c, t * P:(t + 1) * P],
                                                    kT[:, c, a, k0:k0 + nk], start=False, stop=(a == 1))
                        last.then_inc(b_filled, 1)
                yield s0 + 52
                pe.wait_ge(f_mparts, l + 1)
                transposes(BB.take(pe, ("fmT", l)), mparts_f[:].rearrange("p t a h -> p t (a h)"), 2 * FH, b_filled)

                def keys_first(n):
                    c, k = n // NT, n % NT
                    if n == 0:
                        pe.wait_ge(*BB.brought(("fmT", l), "act"))
                    nq = min(FKEYS, T - k * P)
                    q = slice(k * P, k * P + nq)
                    ps = BB.take(pe, ("fsecond", l, n))
                    nc.tensor.matmul(ps[:, 0:2 * nq], ident_bf[:], band_k[:, 0:nq].unsqueeze(1).to_broadcast([P, 2, nq]),
                                     start=True, stop=False)
                    for a in range(2):
                        nc.tensor.matmul(ps[:, a * nq:(a + 1) * nq], pick[:, 2 * c + a, :], mT_f[:, q], start=False, stop=False)
                        last = nc.tensor.matmul(ps[:, a * nq:(a + 1) * nq], kT[:, c, a, k * P:(k + 1) * P], qT[:, c, q],
                                                start=False, stop=(a == 1))
                    last.then_inc(b_filled, 1)

                def values_f(n):
                    c, k = n // NT, n % NT
                    pe.wait_ge(*BB.brought(("fsecond", l, n), "act"))
                    ps = BB.take(pe, ("fav", l, n))
                    nq = min(FKEYS, T - k * P)
                    for a in range(2):
                        o = ps[:, a * (FD + 1):(a + 1) * (FD + 1)]
                        last = nc.tensor.matmul(o, prob_b[:, k % PR_B, a * nq:a * nq + P], V_f[:, k, 2 * c + a, :],
                                                start=True, stop=True)
                        if k:
                            last = nc.tensor.matmul(o[0:FW, :], prob_b[:, (k - 1) % PR_B, a * FKEYS + P:(a + 1) * FKEYS],
                                                    V_f[:, k - 1, 2 * c + a, :], start=False, stop=True, skip_group_check=True)
                    last.then_inc(b_filled, 1)

                def projected(c):
                    pe.wait_ge(*BB.brought(("foT", l, c), "act"))
                    for t in range(NT):
                        last = nc.tensor.matmul(acc_b[:, t * E:(t + 1) * E], oT_f[:, c, t * P:(t + 1) * P], wo_s[:, l, c, :],
                                                start=(c == 0 and t == 0), stop=(c == INNER // P - 1), skip_group_check=True)
                    last.then_inc(f_wo, 1)

                for n in range(UNITS + 2):
                    yield s0 + 54 + UNIT * n
                    if n < UNITS:
                        keys_first(n)
                    if n % NT == 1 and n > NT:
                        c = n // NT - 1
                        pe.wait_ge(*BB.brought(("fav", l, NT * c + NT - 1), "dve"))
                        transposes(BB.take(pe, ("foT", l, c)), otok_f[:, c % 2], inc=b_filled)
                    if 0 < n <= UNITS:
                        values_f(n - 1)
                    if n % NT == 3 and n > NT:
                        projected(n // NT - 1)
                yield s0 + 86
                projected(FH // 2 - 1)
                yield s0 + 88
                pe.wait_ge(f_mid, l + 1)
                transposes(BB.take(pe, ("fx", l)), x_f, inc=b_filled)
                yield s0 + 90
                pe.wait_ge(*BB.brought(("fx", l), "act"))
                transposes(BB.take(pe, ("fback", l)), hT[:].rearrange("p (t q) -> p t q", q=P), inc=b_filled)
                yield s0 + 92
                pe.wait_ge(*BB.brought(("fback", l), "dve"))
                transposes(BB.take(pe, ("fnT", l)), xn_b, inc=b_filled)
                for c, (c0, n) in enumerate(HC):
                    yield s0 + 94 + 2 * c
                    if c == 0:
                        pe.wait_ge(*BB.brought(("fnT", l), "dve"))
                    for product, col in (("fg", HID + c0), ("fa", c0)):
                        nc.tensor.matmul(BB.take(pe, (product, l, c))[0:n, :], w1_s[:, l, col:col + n], xnT_b[:],
                                         start=True, stop=True).then_inc(b_filled, 1)
                for c, (c0, n) in enumerate(HC):
                    yield s0 + (97.5 if c == 0 else 98 + 2 * c)
                    pe.wait_ge(*BB.brought(("fa", l, c), "dve"))
                    for t in range(NT):
                        last = nc.tensor.matmul(acc_b[:, t * E:(t + 1) * E], u_f[0:n, c, t * P:(t + 1) * P], w2_s[0:n, l, c, :],
                                                start=(c == 0 and t == 0), stop=(c == len(HC) - 1), skip_group_check=True)
                    last.then_inc(f_w2, 1)
                if l + 1 < DEPTH:
                    yield s0 + 106
                    pe.wait_ge(f_x, 2 * l + 2)
                    transposes(BB.take(pe, ("fnext", l)), x_f, inc=b_filled)

        def finish_scalar(act):
            yield FINISH
            nc.scalar.activation(mix_b[:], x_f[:].rearrange("p t e -> p (t e)"), ACT.Tanh, scale=0.5).then_inc(b_tanh, 1)

        def b_scalar(act, after_finish):
            def bring(product, dst, func=ACT.Copy, rows=slice(0, P), cols=slice(0, T), last=True, **kw):
                ins = nc.scalar.activation(dst, BB.full(act, product)[rows, cols], func, **kw)
                if last:
                    ins.then_inc(b_emptied["act"], 1)

            def shifted(product):
                bring(product, hT[0:64, :], rows=slice(0, 64), last=False)
                bring(product, hT[64:P, 1:T], rows=slice(64, P), cols=slice(0, T - 1))

            yield 1
            bring("xnT", xnT_b[:], last=False)
            shifted("xnT")
            yield 2
            bring("q", qkg_b[:, 0, :])
            bring("k", qkg_b[:, 1, :])
            bring("gqk", qkg_b[0:64, 2, :], rows=slice(0, 64))
            yield 3
            ps = BB.full(act, "v")
            nc.scalar.activation(V_b[:].rearrange("p t h c -> p (t h) c")[:, :, 0:D0],
                                 ps[:].rearrange("p (n d) -> p n d", d=D0), ACT.Copy).then_inc(b_emptied["act"], 1)
            ps = BB.full(act, "gv")
            for a in range(2):
                half = slice(64 * a, 64 * a + 64)
                last = nc.scalar.activation(V_l[half, :, 16 * a:16 * a + D0],
                                            ps[half, 0:NL].rearrange("p (u a d) -> p u a d", a=2, d=D0)[:, :, a, :], ACT.Copy)
            last.then_inc(b_emptied["act"], 1)
            ps = BB.full(act, "gates")
            nc.scalar.activation(gate_b[:].rearrange("p t g h -> p (t g h)"), ps[:, 0:P], ACT.Tanh,
                                 scale=0.5).then_inc(b_emptied["act"], 1)
            yield B_AT + 9
            bring(("mT", 0), mT_b[:, 0, :], rows=slice(0, 8))
            yield B_AT + 11
            bring("lmT", mT_l[:], rows=slice(0, 2 * LH))
            for g in range(G):
                for n in range(8):
                    yield B_AT + 13 + 12 * g + n
                    if n % 2 == 0 and 4 * g + n // 2 >= 2:
                        act.wait_ge(b_av, 4 * g + n // 2 - 1)
                    nq = min(LKEYS, T - n // 2 * P)
                    if g == 0 and n == 0:
                        act.wait_ge(b_split, 2)
                    bring(bsecond[g][n], prob_b[:, n % PR_B, 0:2 * nq], ACT.Exp, cols=slice(0, 2 * nq), scale=HEAD_SCALE)
                yield B_AT + 21 + 12 * g
                if g + 1 < G:
                    if g >= 1:
                        act.wait_ge(b_mrow[g - 1], 16)
                    bring(("mT", g + 1), mT_b[:, (g + 1) % 2, :], rows=slice(0, 8))
                act.wait_ge(b_av, 4 * g + 4)
                if g:
                    act.wait_ge(*BB.made(("oT", g - 1)))
                nc.scalar.activation(og_b[:], acc_b[:], ACT.Copy).then_inc(b_og, 1)
            for u in range(4):
                yield B_AT + 63 + u
                bring(("lsecond", u), prob_b[:, u, :], ACT.Exp, scale=HEAD_SCALE)
            yield B_AT + 67
            act.wait_ge(b_av, 4 * G + 1)
            act.wait_ge(*BB.made(("oT", G - 1)))
            nc.scalar.activation(og_b[:], acc_b[:], ACT.Copy).then_inc(b_og, 1)
            yield B_AT + 69
            bring("remT", og_b[0:NL, :], rows=slice(0, NL))
            yield B_AT + 71
            act.wait_ge(*BB.made("rproj"))
            bring("mixT", og_b[:])
            yield B_AT + 72
            if after_finish:
                act.wait_ge(b_out, 1)
            bring("wout", s_b[:])
            for l in range(DEPTH):
                s0 = LAYER_AT + LAYER * l
                def queries_keys_T(t):
                    ps = BB.full(act, ("qkT", l, t, 0))
                    nc.scalar.activation(qT[:, :, t * P:(t + 1) * P], ps[:].rearrange("p (c q) -> p c q", q=P), ACT.Copy)\
                        .then_inc(b_emptied["act"], 1)
                    ps = BB.full(act, ("qkT", l, t, 1))
                    for a in range(2):
                        half = slice(64 * a, 64 * a + 64)
                        last = nc.scalar.activation(kT[half, :, a, t * P:(t + 1) * P],
                                                    ps[half, :].rearrange("p (c q) -> p c q", q=P), ACT.Copy)
                    last.then_inc(b_emptied["act"], 1)

                for t in range(NT):
                    yield s0 + QKV * max(t - 1, 0) + t % 2
                    n = NT * l + t
                    if n >= 2:
                        act.wait_ge(f_turned, n - 1)
                    for a, product in enumerate(("fq", "fk")):
                        bring((product, l, t), sq[:, t % 2, a, :], ACT.Square, last=False)
                        bring((product, l, t), qk_raw[:, t % 2, a, :])
                    ps = BB.full(act, ("fv", l, t))
                    nc.scalar.activation(V_f[:, t, :, 0:FD], ps[:].rearrange("p (h d) -> p h d", d=FD), ACT.Copy)\
                        .then_inc(b_emptied["act"], 1)
                    if t >= 2:
                        yield s0 + QKV * (t - 1) + 3
                        queries_keys_T(t - 2)
                for t in range(NT - 2, NT):
                    yield s0 + QKV * (t + 1) + 3
                    queries_keys_T(t)
                yield s0 + 52
                bring(("fmT", l), mT_f[0:2 * FH, :], rows=slice(0, 2 * FH))
                for n in range(UNITS + 2):
                    yield s0 + 54 + UNIT * n
                    if n < UNITS:
                        nq = min(FKEYS, T - n % NT * P)
                        if n >= NT:
                            act.wait_ge(*BB.made(("fav", l, n - NT + (n % NT < NT - 1))))
                        bring(("fsecond", l, n), prob_b[:, n % PR_B, 0:2 * nq], ACT.Exp, cols=slice(0, 2 * nq), scale=QK_SCALE)
                    if n % NT == 1 and n > NT:
                        bring(("foT", l, n // NT - 1), oT_f[:, n // NT - 1, :])
                yield s0 + 89
                shifted(("fx", l))
                for c, (c0, n) in enumerate(HC):
                    yield s0 + 94 + 2 * c
                    if c:
                        act.wait_ge(*BB.brought(("fa", l, c - 1), "dve"))
                    nc.scalar.activation(gelu_f[0:n, :], BB.full(act, ("fg", l, c))[0:n, :], ACT.Gelu,
                                         bias=b1_s[0:n, l, 1, c:c + 1]).then_inc(b_emptied["act"], 1)
                if l + 1 < DEPTH:
                    yield s0 + 107
                    shifted(("fnext", l))

        def finish_vector(dve, link):
            flat = "p t e -> p (t e)"
            yield FINISH + 2
            dve.wait_ge(b_tanh, 1)
            link(nc.vector.scalar_tensor_tensor(out=mix_b[:], in0=mix_b[:], scalar=1.0, in1=x_f[:].rearrange(flat),
                                                op0=ALU.add, op1=ALU.mult))
            link(nc.vector.tensor_tensor(mix_b[:], mix_b[:], s_b[:], ALU.mult))
            nc.vector.scalar_tensor_tensor(out=x_f[:].rearrange(flat), in0=mix_b[:], scalar=0.5, in1=x_b[:].rearrange(flat),
                                           op0=ALU.mult, op1=ALU.add).then_inc(b_out, 1)

        def b_vector(dve, link, after_finish):
            emptied = b_emptied["dve"]
            yield 0
            layernorm(link, x1_a, xn_b, stats_b, mv_b, rs_b, b_xn, b_var, b_rstd, 1)
            yield 1
            dve.wait_ge(*BB.brought("xnT", "act"))
            link(nc.vector.tensor_reduce(out=psum_l[:, 0, :], in_=xnT_b[:].rearrange("p (l t) -> p l t", t=POOL), op=ALU.add,
                                         axis=AX.X))
            for a in range(2):
                last = nc.vector.tensor_scalar(pool_b[:, a, :], psum_l[:, 0, :], 1.0 / POOL, None, ALU.mult)
            last.then_inc(b_pool, 1)
            yield 2
            ps = BB.full(dve, "gqk")
            nc.vector.tensor_reduce(out=psum_l[64:P, 1, :], in_=ps[64:P, :].rearrange("p (l t) -> p l t", t=POOL), op=ALU.add,
                                    axis=AX.X).then_inc(emptied, 1)
            yield 3
            dve.wait_ge(*BB.brought("k", "act"))
            split(link, qkg_b[:, 0:2], res_b[:, 0:2], [parts_b[:, :, c, :] for c in range(SPLIT)], b_split)
            yield 3.5
            dve.wait_ge(*BB.brought("gqk", "dve"))
            nc.vector.memset(qkg_b[64:P, 2, NL:T], 0.0)
            link(nc.vector.tensor_scalar(qkg_b[64:P, 2, 0:NL], psum_l[64:P, 1, :], 1.0 / POOL, None, ALU.mult))
            dve.wait_ge(*BB.brought("gqk", "act"))
            split(link, qkg_b[:, 2], res_b[:, 2], [parts_l[:, c, :] for c in range(SPLIT)], b_split)
            dve.wait_ge(*BB.brought("gates", "act"))
            g2 = gate_b[:].rearrange("p t g h -> p (t g h)")
            nc.vector.tensor_scalar(g2, g2, 0.5, 0.5, ALU.mult, ALU.add).then_inc(b_gate, 1)

            def first_pass(g, n):
                _, _, t, hp = f = bfirst[g][n]
                nk = LKEYS - (WIN if t == 0 else 0)
                nc.vector.tensor_reduce(out=nmax_b[:, g, t, 2 * hp:2 * hp + 2],
                                        in_=BB.full(dve, f)[:, 0:2 * nk].rearrange("p (a k) -> p a k", a=2),
                                        op=ALU.max, axis=AX.X, negate=True).then_inc(emptied, 1)

            def max_parts(g):
                dve.wait_ge(*BB.brought(bfirst[g][-1], "dve"))
                split_max(link, nmax_b[:, g], mhi_b[:, g], [mparts_b[:, g, :, p, :] for p in range(2)], b_mparts)

            for n in range(8):
                yield B_AT + n
                first_pass(0, n)
            yield B_AT + 8
            max_parts(0)
            for t in range(NT):
                yield B_AT + 9 + t / 4
                nc.vector.tensor_reduce(out=nmax_l[:, t, :], in_=BB.full(dve, ("lfirst", t))[:].rearrange("p (h l) -> p h l", l=NL),
                                        op=ALU.max, axis=AX.X, negate=True).then_inc(emptied, 1)
            yield B_AT + 10
            dve.wait_ge(*BB.brought(("lfirst", NT - 1), "dve"))
            split_max(link, nmax_l[:], mhi_l[:], [mparts_l[:, :, p, :] for p in range(2)], b_lmparts)
            for g in range(G):
                for n in range(8):
                    yield B_AT + 13 + 12 * g + n
                    if g + 1 < G:
                        first_pass(g + 1, n)
                yield B_AT + 21 + 12 * g
                if g + 1 < G:
                    max_parts(g + 1)
                yield B_AT + 22 + 12 * g
                ps = BB.full(dve, ("oT", g))[:].rearrange("p (t j c) -> p t j c", t=NT, c=32)
                rden = rden_b[:, 0:4 * NT].rearrange("p (t j) -> p t j", j=4)
                link(nc.vector.reciprocal(rden, ps[:, :, :, D0]))
                nc.vector.tensor_tensor(loc_b[:, :, 32 * g:32 * g + 32].rearrange("p t (j d) -> p t j d", d=D0),
                                        ps[:, :, :, 0:D0], rden.unsqueeze(3).to_broadcast([P, NT, 4, D0]),
                                        ALU.mult).then_inc(emptied, 1)
                dve.wait_ge(*BB.brought(("oT", g), "dve"))
            yield B_AT + 68
            ps = BB.full(dve, "loT")[:].rearrange("p (n s) -> p n s", s=16)
            link(nc.vector.reciprocal(rden_b[:], ps[:, :, D0]))
            nc.vector.tensor_tensor(rem_b[:].rearrange("p t (h d) -> p (t h) d", d=D0), ps[:, :, 0:D0],
                                    rden_b[:].unsqueeze(2).to_broadcast([P, NT * LH, D0]), ALU.mult).then_inc(emptied, 1)
            yield B_AT + 70
            dve.wait_ge(b_gate, 1)
            heads = "p t (h d) -> p t h d"

            def gate(g):
                return gate_b[:, :, g, :].unsqueeze(3).to_broadcast([P, NT, H0, D0])

            loc = loc_b[:].rearrange(heads, d=D0)
            link(nc.vector.tensor_tensor(loc, loc, gate(0), ALU.mult))
            if after_finish:
                dve.wait_ge(b_out, 1)
            nc.vector.tensor_tensor(mix_b[:].rearrange("p (t h d) -> p t h d", t=NT, d=D0),
                                    BB.full(dve, "rproj")[:].rearrange("p (t h d) -> p t h d", t=NT, d=D0),
                                    gate(1), ALU.mult).then_inc(emptied, 1)
            dve.wait_ge(*BB.brought("rproj", "dve"))
            nc.vector.tensor_tensor(mix_b[:], mix_b[:], loc_b[:].rearrange("p t e -> p (t e)"), ALU.add).then_inc(b_mix, 1)

            flat = "p t e -> p (t e)"
            for l in range(DEPTH):
                s0 = LAYER_AT + LAYER * l

                def normalised(t):
                    n = NT * l + t
                    if n:
                        dve.wait_ge(*BB.made(("qkT", (n - 1) // NT, (n - 1) % NT, 1)))
                    dve.wait_ge(f_turned, n + 1)
                    nc.vector.tensor_tensor(qk_rot.rearrange("p a (h d) -> p (a h) d", d=FD),
                                            cosp[:, t % 2].rearrange("p a (h d) -> p (a h) d", d=FD),
                                            rn[:, t % 2, 1, :].unsqueeze(2).to_broadcast([P, 2 * FH, FD]), ALU.mult).then_inc(f_rot, 1)
                    dve.wait_ge(f_rot, n + 1)

                for t in range(NT):
                    yield s0 + QKV * max(t - 1, 0) + t % 2 + 0.5
                    n = NT * l + t
                    dve.wait_ge(*BB.brought(("fk", l, t), "act"))
                    nc.vector.tensor_reduce(out=ss[:], in_=sq[:, t % 2].rearrange("p a (h d) -> p a h d", d=FD), op=ALU.add,
                                            axis=AX.X).then_inc(f_sq, 1)
                    for a in range(2):
                        last = nc.vector.tensor_tensor(cosp[:, t % 2, a, :].rearrange("p (h d) -> p h d", d=FD),
                                                       qk_raw[:, t % 2, a, :].rearrange("p (h d) -> p h d", d=FD),
                                                       rotf[:, l, 2 * a, t, :].unsqueeze(1).to_broadcast([P, FH, FD]), ALU.mult)
                    last.then_inc(f_cos, 1)
                    v = rn[:, t % 2, 0, :]
                    dve.wait_ge(f_sq, n + 1)
                    link(nc.vector.tensor_scalar(v, ss[:].rearrange("p a h -> p (a h)"), 1e-24, None, ALU.max))
                    rsqrt(link, v, rn[:, t % 2, 1, :], rn[:, t % 2, 2, :])
                    if t:
                        yield s0 + QKV * t + 2
                        normalised(t - 1)
                yield s0 + QKV * NT + 2
                normalised(NT - 1)
                for t in range(NT):
                    for c in range(FH // 2):
                        yield s0 + 34 + 4 * t + c
                        nk = FKEYS - (FW if t == 0 else 0)
                        nc.vector.tensor_reduce(out=nmax_f[:, t, 2 * c:2 * c + 2],
                                                in_=BB.full(dve, ("ffirst", l, t, c))[:, 0:2 * nk].rearrange("p (a k) -> p a k", a=2),
                                                op=ALU.max, axis=AX.X, negate=True).then_inc(emptied, 1)
                yield s0 + 50.5
                dve.wait_ge(*BB.brought(("ffirst", l, NT - 1, FH // 2 - 1), "dve"))
                split_max(link, nmax_f[:], mhi_f[:], [mparts_f[:, :, p, :] for p in range(2)], f_mparts)
                for n in range(UNITS):
                    yield s0 + 54 + UNIT * (n + 1)
                    c, k = n // NT, n % NT
                    ps = BB.full(dve, ("fav", l, n))[:, 0:2 * (FD + 1)].rearrange("p (a d) -> p a d", a=2)
                    if c >= 2 and k == 0:
                        dve.wait_ge(*BB.made(("foT", l, c - 2)))
                    link(nc.vector.reciprocal(rden_f[:, n % 2], ps[:, :, FD]))
                    nc.vector.tensor_tensor(otok_f[:, c % 2, k, :].rearrange("p (a d) -> p a d", a=2), ps[:, :, 0:FD],
                                            rden_f[:, n % 2].unsqueeze(2).to_broadcast([P, 2, FD]), ALU.mult).then_inc(emptied, 1)
                    if n:
                        dve.wait_ge(*BB.brought(("fav", l, n - 1), "dve"))
                yield s0 + 87
                x_in_l = xn_b if l == 0 else x_f
                dve.wait_ge(f_wo, INNER // P * (l + 1))
                if after_finish and l == 0:
                    dve.wait_ge(b_stored, 16)
                nc.vector.tensor_tensor(x_f[:].rearrange(flat), acc_b[:], x_in_l[:].rearrange(flat), ALU.add).then_inc(f_mid, 1)
                yield s0 + 91
                ps = BB.full(dve, ("fback", l))
                layernorm(link, ps[:].rearrange("p (t e) -> p t e", e=E), xn_b, stats_b, mv_b, rs_b, emptied, b_var, b_rstd, l + 2)
                yield s0 + 93
                nc.vector.tensor_scalar(xnT_b[:], BB.full(dve, ("fnT", l))[:], lng_s[:, l:l + 1], lnb_s[:, l:l + 1],
                                        ALU.mult, ALU.add).then_inc(emptied, 1)
                for c, (c0, n) in enumerate(HC):
                    yield s0 + 95 + 2 * c
                    dve.wait_ge(*BB.brought(("fg", l, c), "act"))
                    nc.vector.scalar_tensor_tensor(out=u_f[0:n, c, :], in0=BB.full(dve, ("fa", l, c))[0:n, :],
                                                   scalar=b1_s[0:n, l, 0, c:c + 1], in1=gelu_f[0:n, :],
                                                   op0=ALU.add, op1=ALU.mult).then_inc(emptied, 1)
                yield s0 + 103
                dve.wait_ge(f_w2, len(HC) * (l + 1))
                link(nc.vector.tensor_tensor(x_f[:].rearrange(flat), acc_b[:], x_f[:].rearrange(flat), ALU.add))
                nc.vector.tensor_tensor(x_f[:], x_f[:], b2_s[:, l, :].unsqueeze(1).to_broadcast([P, NT, E]), ALU.add)\
                    .then_inc(f_x, 2)

        lo, hi = min(s.num for s in sems), max(s.num for s in sems)

        def clear_all():
            nc.multi_engine_barrier(list(nc.engines), sems_to_clear=range(lo, hi + 1))

        def iteration(body, row_next, row_b, row_done):
            head, second, finish = row_next is not None, row_b is not None, row_done is not None

            def streams(*pairs):
                merge(*(stream for given, stream in pairs if given))

            with nc.Block() as block:
                @block.sync
                def _(sp):
                    streams((body, paced(a_sync(sp))), (head, paced(head_sync(sp, row_next, body))),
                            (finish, finish_sync(sp, row_done)), (second, b_sync(sp)))

                @block.gpsimd
                def _(pool):
                    streams((head, paced(head_gpsimd(pool))), (second, b_gpsimd(pool, finish)))

                @block.tensor
                def _(pe):
                    streams((body, paced(a_tensor(pe))), (head, paced(head_tensor(pe, body))), (second, b_tensor(pe)))

                @block.scalar
                def _(act):
                    streams((body, paced(a_scalar(act))), (head, paced(head_scalar(act))),
                            (finish, finish_scalar(act)), (second, b_scalar(act, finish)))

                @block.vector
                def _(dve):
                    link_a, link_b = chain(dve, a_dve_step), chain(dve, b_dve_step)
                    streams((body, paced(a_vector(dve, link_a, second))), (head, paced(head_vector(dve, link_a))),
                            (finish, finish_vector(dve, link_b)), (second, b_vector(dve, link_b, finish)))
            clear_all()

        clear_all()
        iteration(False, bass.ds(0, 1), None, None)
        iteration(True, bass.ds(1, 1), None, None)
        iteration(True, bass.ds(2, 1), bass.ds(0, 1), None)
        with nc.Fori(2, B - 1) as b:
            iteration(True, bass.ds(b + 1, 1), bass.ds(b - 1, 1), bass.ds(b - 2, 1))
        iteration(True, None, bass.ds(B - 2, 1), bass.ds(B - 3, 1))
        iteration(False, None, bass.ds(B - 1, 1), bass.ds(B - 2, 1))
        iteration(False, None, None, bass.ds(B - 1, 1))


_SAME = {"att_w": "L0_attn_w_att_val", "wv0_b": "L0_attn_wv_b", "wo0_b": "L0_attn_out_b", "W1": "L0_ffn_W1",
         "W2": "L0_ffn_W2", "Wg": "L0_ffn_Wg", "bg": "L0_ffn_bg", "wq": "L1_attn_wq", "wk": "L1_attn_wk",
         "wv": "L1_attn_wv", "wgv": "L1_attn_wgv", "r_out": "L1_attn_r_out_w", "gate_l": "L1_attn_gate_local_w",
         "gate_r": "L1_attn_gate_remote_w", "w_out": "L1_attn_w_out", "wqkv": "L1_ffn_wqkv",
         "q_sc": "L1_ffn_q_scale", "k_sc": "L1_ffn_k_scale", "wo": "L1_ffn_wo", "ln_g": "L1_ffn_ln_g",
         "ln_b": "L1_ffn_ln_b", "w1": "L1_ffn_w1", "b1": "L1_ffn_b1", "w2": "L1_ffn_w2", "b2": "L1_ffn_b2"}


def kernel(**inputs):
    import concourse.bacc as bacc
    from concourse.bass_utils import run_bass_kernel_spmd

    a = {n: np.asarray(v) for n, v in inputs.items()}
    laid = {"x_in": a["L0_attn_x"], "wv0T": a["L0_attn_wv_w"].T, "wo0T": a["L0_attn_out_w"].T,
            "wgqk": np.concatenate([a["L1_attn_wgq"], a["L1_attn_wgk"]], axis=1)}
    laid |= {n: a[full] for n, full in _SAME.items()}
    consts = shape_constants()

    nc = bacc.Bacc("TRN2", target_bir_lowering=False, num_devices=1)
    arrays = {}

    def dram(name, array):
        arrays[name] = np.ascontiguousarray(array)
        return nc.dram_tensor(name, array.shape, mybir.dt.from_np(array.dtype), kind="ExternalInput").ap()

    aps = {n: dram(f"in_{n}", v) for n, v in laid.items()}
    const_aps = {n: dram(f"const_{n}", v) for n, v in consts.items()}
    out = nc.dram_tensor("out_0", (B, T, E), F32, kind="ExternalOutput").ap()
    mixer_kernel(nc, **aps, consts=const_aps, out=out)
    r = run_bass_kernel_spmd(nc, [arrays], core_ids=[0])
    return r.results[0]["out_0"]
```
